# Optimizing a Trainium2 kernel written in Bass

```python
import numpy as np
import jax
import jax.numpy as jnp

def _softmax(x, axis=-1):
    return jax.nn.softmax(x, axis=axis)

def _gelu(x):
    return jax.nn.gelu(x, approximate=True)

def _silu(x):
    return jax.nn.silu(x)

def _sigmoid(x):
    return jax.nn.sigmoid(x)

def _layernorm(x, axis=-1, eps=1e-05):
    m = jnp.mean(x, axis=axis, keepdims=True)
    v = jnp.var(x, axis=axis, keepdims=True)
    return (x - m) / jnp.sqrt(v + eps)

def _scatter_add(tgt, idx, src, axis=0):
    return tgt.at[idx].add(src)

def _segment_sum(src, seg, n):
    return jax.ops.segment_sum(src, seg, n)
kernel_name = 'mk_gnn_ffn_d2_gnn_r8_3c0a08'

def setup_inputs(seed: int=0):
    np.random.seed(seed)
    _w = jnp.asarray

    def _rec_inputs():
        import jax
        import jax.numpy as jnp
        _gk = jax.random.key(seed)
        x = -0.0002117 + 1 * jax.random.normal(jax.random.fold_in(_gk, 1), (6250, 256), jnp.float32)
        _s = jax.random.randint(jax.random.fold_in(_gk, 2), (50000,), 0, 6250, jnp.int32)
        _d = jax.random.randint(jax.random.fold_in(_gk, 3), (50000,), 0, 6250, jnp.int32)
        _loop = jnp.arange(6250, dtype=jnp.int32)
        src = jnp.concatenate([_s, _d, _loop])
        dst = jnp.concatenate([_d, _s, _loop])
        _o = jnp.argsort(dst, stable=True)
        src = src[_o]
        dst = dst[_o]
        return (x, src, dst)
    x, src, dst = _rec_inputs()

    def _L0_gnn_setup():
        import jax, jax.numpy as jnp
        import numpy as np
        N = 12500
        E = 200000
        D = 256
        BN_EPS = 1e-05
        key = jax.random.key(seed)
        ks = jax.random.split(key, 6)
        node_feats = jax.random.normal(ks[0], (N, D), dtype=jnp.float32)
        src = jax.random.randint(ks[1], (E,), 0, N, dtype=jnp.int64)
        dst = jax.random.randint(ks[2], (E,), 0, N, dtype=jnp.int64)
        eps = jnp.zeros((1,), dtype=jnp.float32)
        W1 = jax.random.normal(ks[3], (D, 2 * D), dtype=jnp.float32) * (1.0 / np.sqrt(D))
        b1 = jnp.zeros((2 * D,), dtype=jnp.float32)
        W2 = jax.random.normal(ks[4], (2 * D, D), dtype=jnp.float32) * (1.0 / np.sqrt(2 * D))
        b2 = jnp.zeros((D,), dtype=jnp.float32)
        gamma = jnp.ones((D,), dtype=jnp.float32)
        beta = jnp.zeros((D,), dtype=jnp.float32)
        return {'node_feats': node_feats, 'src': src, 'dst': dst, 'eps': eps, 'W1': W1, 'b1': b1, 'W2': W2, 'b2': b2, 'gamma': gamma, 'beta': beta}
    _L0_gnn_all = _L0_gnn_setup()
    _L0_gnn_in = {k: v for k, v in _L0_gnn_all.items() if k in ('eps', 'W1', 'b1', 'W2', 'b2', 'gamma', 'beta')}
    del _L0_gnn_all

    def _L0_ffn_setup():
        import jax, jax.numpy as jnp
        import numpy as np
        N_EXPERTS = 8
        TOP_K = 2
        key = jax.random.key(seed)
        ks = jax.random.split(key, 5)
        B, T, C, E, H = (8, 256, 256, 8, 682)
        scale = 1.0 / np.sqrt(C)
        return {'x': jax.random.normal(ks[0], (B, T, C), dtype=jnp.float32), 'router_w': jax.random.normal(ks[1], (E, C), dtype=jnp.float32) * scale, 'w1': jax.random.normal(ks[2], (E, H, C), dtype=jnp.float32) * scale, 'w2': jax.random.normal(ks[3], (E, C, H), dtype=jnp.float32) * (1.0 / np.sqrt(H)), 'w3': jax.random.normal(ks[4], (E, H, C), dtype=jnp.float32) * scale}
    _L0_ffn_all = _L0_ffn_setup()
    _L0_ffn_in = {k: v for k, v in _L0_ffn_all.items() if k in ('router_w', 'w1', 'w2', 'w3')}
    del _L0_ffn_all

    def _L1_gnn_setup():
        import jax, jax.numpy as jnp
        import numpy as np
        N = 6250
        E = 100000
        DIN = 256
        DOUT = 256
        K = 3
        key = jax.random.key(seed)
        k1, k2, k3 = jax.random.split(key, 3)
        x = jax.random.normal(k1, (N, DIN), dtype=jnp.float32)
        edge_index = jax.random.randint(k2, (2, E), 0, N, dtype=jnp.int32)
        limit = float(np.sqrt(6.0 / (DIN + DOUT)))
        weight = jax.random.uniform(k3, (K + 1, DIN, DOUT), dtype=jnp.float32, minval=-limit, maxval=limit)
        bias = jnp.zeros((DOUT,), dtype=jnp.float32)
        return {'x': x, 'edge_index': edge_index, 'weight': weight, 'bias': bias}
    _L1_gnn_all = _L1_gnn_setup()
    _L1_gnn_in = {k: v for k, v in _L1_gnn_all.items() if k in ('weight', 'bias')}
    del _L1_gnn_all

    def _L1_ffn_setup():
        import math
        import jax, jax.numpy as jnp
        import numpy as np
        CAPACITY_FACTOR = 1.25
        key = jax.random.key(seed)
        ks = jax.random.split(key, 5)
        B, L, D, F, E = (8, 1024, 256, 1024, 8)
        h = jax.random.normal(ks[0], (B, L, D), dtype=jnp.float32)
        gate_w = jax.random.normal(ks[1], (D, E), dtype=jnp.float32) * 0.02
        gate_b = jnp.zeros((E,), dtype=jnp.float32)
        w1 = jax.random.normal(ks[2], (E, D, F), dtype=jnp.float32) * (1.0 / math.sqrt(D))
        b1 = jnp.zeros((E, F), dtype=jnp.float32)
        w2 = jax.random.normal(ks[3], (E, F, D), dtype=jnp.float32) * (1.0 / math.sqrt(F))
        b2 = jnp.zeros((E, D), dtype=jnp.float32)
        return {'h': h, 'gate_w': gate_w, 'gate_b': gate_b, 'w1': w1, 'b1': b1, 'w2': w2, 'b2': b2}
    _L1_ffn_all = _L1_ffn_setup()
    _L1_ffn_in = {k: v for k, v in _L1_ffn_all.items() if k in ('gate_w', 'gate_b', 'w1', 'b1', 'w2', 'b2')}
    del _L1_ffn_all
    return {'x': x, 'src': src, 'dst': dst, 'L0_gnn_eps': _L0_gnn_in['eps'], 'L0_gnn_W1': _L0_gnn_in['W1'], 'L0_gnn_b1': _L0_gnn_in['b1'], 'L0_gnn_W2': _L0_gnn_in['W2'], 'L0_gnn_b2': _L0_gnn_in['b2'], 'L0_gnn_gamma': _L0_gnn_in['gamma'], 'L0_gnn_beta': _L0_gnn_in['beta'], 'L0_ffn_router_w': _L0_ffn_in['router_w'], 'L0_ffn_w1': _L0_ffn_in['w1'], 'L0_ffn_w2': _L0_ffn_in['w2'], 'L0_ffn_w3': _L0_ffn_in['w3'], 'L1_gnn_weight': _L1_gnn_in['weight'], 'L1_gnn_bias': _L1_gnn_in['bias'], 'L1_ffn_gate_w': _L1_ffn_in['gate_w'], 'L1_ffn_gate_b': _L1_ffn_in['gate_b'], 'L1_ffn_w1': _L1_ffn_in['w1'], 'L1_ffn_b1': _L1_ffn_in['b1'], 'L1_ffn_w2': _L1_ffn_in['w2'], 'L1_ffn_b2': _L1_ffn_in['b2']}

def reference(x, src, dst, L0_gnn_eps, L0_gnn_W1, L0_gnn_b1, L0_gnn_W2, L0_gnn_b2, L0_gnn_gamma, L0_gnn_beta, L0_ffn_router_w, L0_ffn_w1, L0_ffn_w2, L0_ffn_w3, L1_gnn_weight, L1_gnn_bias, L1_ffn_gate_w, L1_ffn_gate_b, L1_ffn_w1, L1_ffn_b1, L1_ffn_w2, L1_ffn_b2):
    import jax
    import jax.numpy as jnp

    def _L0_gnn_ref(node_feats, src, dst, eps, W1, b1, W2, b2, gamma, beta):
        import jax, jax.numpy as jnp
        import numpy as np
        N = 12500
        E = 200000
        D = 256
        BN_EPS = 1e-05
        n = node_feats.shape[0]
        neigh = jax.ops.segment_sum(node_feats[src], dst, num_segments=n)
        h = (1.0 + eps) * node_feats + neigh
        h = jax.nn.relu(h @ W1 + b1) @ W2 + b2
        mean = jnp.mean(h, axis=0)
        var = jnp.mean(jnp.square(h - mean), axis=0)
        h = (h - mean) * jax.lax.rsqrt(var + BN_EPS) * gamma + beta
        return h

    def _L0_ffn_ref(x, router_w, w1, w2, w3):
        import jax, jax.numpy as jnp
        import numpy as np
        N_EXPERTS = 8
        TOP_K = 2
        B, T, C = x.shape
        flat = x.reshape(-1, C)
        logits = flat @ router_w.T
        probs = jax.nn.softmax(logits, axis=-1)
        topk_probs, topk_idx = jax.lax.top_k(probs, TOP_K)
        topk_probs = topk_probs / (jnp.sum(topk_probs, axis=-1, keepdims=True) + 1e-09)
        onehot = jax.nn.one_hot(topk_idx, N_EXPERTS, dtype=flat.dtype)
        gates = jnp.einsum('nk,nke->ne', topk_probs, onehot)
        h1 = jnp.einsum('nc,ehc->neh', flat, w1)
        h3 = jnp.einsum('nc,ehc->neh', flat, w3)
        h = jax.nn.silu(h1) * h3
        y = jnp.einsum('neh,ech->nec', h, w2)
        out = jnp.einsum('ne,nec->nc', gates, y)
        return out.reshape(B, T, C)

    def _L1_gnn_ref(x, edge_index, weight, bias):
        import jax, jax.numpy as jnp
        import numpy as np
        N = 6250
        E = 100000
        DIN = 256
        DOUT = 256
        K = 3
        num_nodes = x.shape[0]
        loops = jnp.arange(num_nodes, dtype=edge_index.dtype)
        row = jnp.concatenate([edge_index[0], loops])
        col = jnp.concatenate([edge_index[1], loops])
        deg = jax.ops.segment_sum(jnp.ones_like(row, dtype=x.dtype), row, num_segments=num_nodes)
        deg_inv_sqrt = jnp.where(deg > 0, jax.lax.rsqrt(jnp.maximum(deg, 1e-30)), 0.0)
        Lvals = -deg_inv_sqrt[row] * deg_inv_sqrt[col]
        Lvals = jnp.where(row == col, Lvals + 1.0, Lvals)

        def spmm(v):
            return jax.ops.segment_sum(Lvals[:, None] * v[col], row, num_segments=num_nodes)
        out = jnp.matmul(x, weight[0])
        Tx_0 = x
        Tx_1 = spmm(x)
        out = out + jnp.matmul(Tx_1, weight[1])
        for k in range(2, K + 1):
            Tx_2 = 2.0 * spmm(Tx_1) - Tx_0
            out = out + jnp.matmul(Tx_2, weight[k])
            Tx_0, Tx_1 = (Tx_1, Tx_2)
        return out + bias

    def _L1_ffn_ref(h, gate_w, gate_b, w1, b1, w2, b2):
        import math
        import jax, jax.numpy as jnp
        import numpy as np
        CAPACITY_FACTOR = 1.25
        B, L, D = h.shape
        E = gate_w.shape[1]
        T = B * L
        C = max(1, math.ceil(CAPACITY_FACTOR * T / E))
        x = h.reshape(T, D)
        logits = x @ gate_w + gate_b
        probs = jax.nn.softmax(logits, axis=-1)
        idx = jnp.argmax(probs, axis=-1)
        prb = jnp.take_along_axis(probs, idx[:, None], axis=1)[:, 0]
        one_hot = jax.nn.one_hot(idx, E, dtype=jnp.float32)
        pos = (jnp.cumsum(one_hot, axis=0) * one_hot).sum(-1).astype(jnp.int32) - 1
        kept = pos < C
        pos_safe = jnp.where(kept, pos, C)
        buf = jnp.zeros((E, C, D), dtype=h.dtype).at[idx, pos_safe].set(x, mode='drop')
        hmid = jax.nn.relu(jnp.einsum('ecd,edf->ecf', buf, w1) + b1[:, None, :])
        ybuf = jnp.einsum('ecf,efd->ecd', hmid, w2) + b2[:, None, :]
        pos_g = jnp.minimum(pos, C - 1)
        y_tok = ybuf[idx, pos_g] * (prb * kept)[:, None]
        y = y_tok.reshape(B, L, D)
        y = jnp.nan_to_num(y, nan=0.0, posinf=10000.0, neginf=-10000.0)
        return y
    edge_index = jnp.stack([src, dst])
    x = x + _L0_gnn_ref(_layernorm(x, axis=-1), src, dst, L0_gnn_eps, L0_gnn_W1, L0_gnn_b1, L0_gnn_W2, L0_gnn_b2, L0_gnn_gamma, L0_gnn_beta)
    x = x + _L0_ffn_ref(_layernorm(x, axis=-1)[None], L0_ffn_router_w, L0_ffn_w1, L0_ffn_w2, L0_ffn_w3)[0]
    x = x + _L1_gnn_ref(_layernorm(x, axis=-1), edge_index, L1_gnn_weight, L1_gnn_bias)
    x = x + _L1_ffn_ref(_layernorm(x, axis=-1)[None], L1_ffn_gate_w, L1_ffn_gate_b, L1_ffn_w1, L1_ffn_b1, L1_ffn_w2, L1_ffn_b2)[0]
    return x

_drawn_inputs = setup_inputs


def setup_inputs(seed=0):
    import zlib

    import numpy as np

    out = dict(_drawn_inputs(seed))
    spreads = {'L0_gnn_b1': (0.0, 0.1),
     'L0_gnn_b2': (0.0, 2.0),
     'L0_gnn_gamma': (1.0, 0.2),
     'L0_gnn_beta': (0.0, 0.1),
     'L1_gnn_bias': (0.0, 0.8),
     'L1_ffn_gate_b': (0.0, 0.8),
     'L1_ffn_b1': (0.0, 0.8),
     'L1_ffn_b2': (0.0, 2.0)}
    factors = {'L1_ffn_gate_w': 8.0, 'L1_ffn_w1': 8.0, 'L1_ffn_w2': 8.0}
    for name, (base, spread) in spreads.items():
        noise = np.random.default_rng([zlib.crc32(name.encode()), seed]).standard_normal(out[name].shape)
        drawn = base * np.exp(spread * noise) if base else spread * noise
        out[name] = jnp.asarray(drawn.astype(out[name].dtype))
    for name, factor in factors.items():
        out[name] = (out[name] * factor).astype(out[name].dtype)
    return out
```

```python
import numpy as np
from contextlib import ExitStack

import concourse.bass as bass
from concourse import mybir
from concourse.alu_op_type import AluOpType as ALU

F32 = mybir.dt.float32
BF16 = mybir.dt.bfloat16
I32 = mybir.dt.int32
U32 = mybir.dt.uint32
ACT = mybir.ActivationFunctionType
AX = mybir.AxisListType
DVE_ENGINE = mybir.EngineType.DVE
PE_ENGINE = mybir.EngineType.PE

P = 128
N = 6250
D = 256
DH = D // P
NB = -(-N // P)
NP = NB * P
LAST = N - (NB - 1) * P
E_IN = 106250
E_ALL = E_IN + N
G = 8
ET = -(-E_ALL // (P * 2 * G)) * 2 * G
EP = ET * P
NG = ET // G
PAD_KEY = NP - 1
ACC_W = NP + P
HID = 512
NE = 8
H0 = 682
F1 = 1024
CAP = -(-125 * N // (100 * NE))
LN_EPS = 1e-5
CH = 512
CHUNKS = [(c, min(CH, NP - c)) for c in range(0, NP, CH)]


class Scope:

    def __init__(self, nc, tag):
        self.nc, self.tag, self.ctx, self.sems = nc, tag, ExitStack(), []

    def __enter__(self):
        self.ctx.__enter__()
        return self

    def __exit__(self, *a):
        self.nc.clear_and_free_semaphores(self.sems)
        self.nc.all_engine_barrier()
        return self.ctx.__exit__(*a)

    def sb(self, name, shape, dt):
        return self.ctx.enter_context(self.nc.sbuf_tensor(f"{self.tag}_{name}", shape, dt))

    def ps(self, name, shape, dt=F32):
        return self.ctx.enter_context(self.nc.psum_tensor(f"{self.tag}_{name}", shape, dt))

    def sem(self, name):
        self.sems.append(self.nc.alloc_semaphore(name=f"{self.tag}_{name}"))
        return self.sems[-1]


def bc_mid(ap, n):
    return ap.unsqueeze(1).to_broadcast([ap.shape[0], n, ap.shape[1]])


def bc_last(ap, n):
    return ap.unsqueeze(2).to_broadcast([ap.shape[0], ap.shape[1], n])


def constants_stage(nc, K):
    with Scope(nc, "cst") as s:
        made = s.sem("made")
        floats = s.sem("floats")
        iota_i = s.sb("iota_i", [P, P], I32)
        part_i = s.sb("part_i", [P, 1], I32)
        zeroed = s.sem("zeroed")
        with nc.Block() as block:
            @block.gpsimd
            def _(pool):
                nc.gpsimd.iota(iota_i[:, :], pattern=[[1, P]], base=0, channel_multiplier=0).then_inc(made, 1)
                nc.gpsimd.iota(part_i[:, :], pattern=[[0, 1]], base=0, channel_multiplier=1).then_inc(made, 1)

            @block.vector
            def _(dve):
                nc.vector.memset(K["ones"][:, :], 1.0).then_inc(zeroed, 1)
                nc.vector.memset(K["zero"][:, :, :], 0.0).then_inc(zeroed, 1)
                dve.wait_ge(made, 2)
                nc.vector.tensor_copy(K["iota"][:, :], iota_i[:, :]).then_inc(floats, 1)
                nc.vector.tensor_copy(K["iota_b"][:, :], iota_i[:, :]).then_inc(floats, 1)
                nc.vector.tensor_copy(K["part"][:, :], part_i[:, :]).then_inc(floats, 1)
                dve.wait_ge(floats, 3)
                nc.vector.tensor_scalar(K["ident"][:, :], K["iota"][:, :], K["part"][:, 0:1], None,
                                        ALU.is_equal).then_inc(floats, 1)
                nc.vector.tensor_scalar(K["before"][:, :], K["iota"][:, :], K["part"][:, 0:1], None,
                                        ALU.is_lt).then_inc(floats, 1)
                nc.vector.tensor_scalar(K["after"][:, :], K["iota"][:, :], K["part"][:, 0:1], None,
                                        ALU.is_gt).then_inc(floats, 1)


def counts_stage(nc, K, dst_p, src_p, dst_r, src_r, rows):
    with Scope(nc, "cnt") as s:
        loaded = s.sem("loaded")
        ends = s.sb("ends", [P, 2, ET], I32)
        lo_i = s.sb("lo_i", [P, 2, ET], I32)
        hi_i = s.sb("hi_i", [P, 2, ET], I32)
        lo_b = s.sb("lo_b", [P, 2, ET], BF16)
        hi_b = s.sb("hi_b", [P, 2, ET], BF16)
        self_b = s.sb("self_b", [P, ET], BF16)
        row_i = s.sb("row_i", [P, 2, ET], I32)
        row_f = s.sb("row_f", [P, 2, ET], F32)
        rlo_i = s.sb("rlo_i", [P, 2, ET], I32)
        rlo_f = s.sb("rlo_f", [P, 2, ET], F32)
        oh_lo = s.sb("oh_lo", [P, 2, 2, G, P], BF16)
        oh_hi = s.sb("oh_hi", [P, 2, 3, G, NB], BF16)
        total = s.sb("total", [P, 2, NB], F32)
        excl = s.sb("excl", [P, 2, NB + 1], F32)
        rdeg = s.sb("rdeg", [P, NB], F32)
        degc = s.sb("degc", [P, NB], F32)
        p_dst = s.ps("p_dst", [P, NB])
        p_src = s.ps("p_src", [P, 2, NB])
        p_pre = s.ps("p_pre", [P, 2, NB])
        p_tot = s.ps("p_tot", [P, 2, NB])
        bits = s.sem("bits")
        floats = s.sem("floats")
        hots = s.sem("hots")
        counted = s.sem("counted")
        chain = s.sem("chain")
        cnt_done = s.sem("cnt_done")
        pre_done = s.sem("pre_done")
        rooted = s.sem("rooted")
        rows_out = s.sem("rows_out")
        rows_ready = s.sem("rows_ready")
        with nc.Block() as block:
            @block.sync
            def _(sp):
                sp.dma_start(ends[:, 0, :], dst_p).then_inc(loaded, 16)
                sp.dma_start(ends[:, 1, :], src_p).then_inc(loaded, 16)
                sp.dma_start(row_i[:, 0, :], dst_r).then_inc(loaded, 16)
                sp.dma_start(row_i[:, 1, :], src_r).then_inc(loaded, 16)
                sp.wait_ge(rows_ready, 2)
                for k in range(2):
                    sp.dma_start(rows[k, 0].rearrange("(p t) -> p t", p=P), row_f[:, k, :]).then_inc(rows_out, 16)
                    sp.dma_start(rows[k, 1].rearrange("(p t) -> p t", p=P), rlo_f[:, k, :]).then_inc(rows_out, 16)
                sp.wait_ge(rows_out, 64)

            @block.vector
            def _(dve):
                dve.wait_ge(loaded, 64)
                nc.vector.tensor_scalar(lo_i[:, :, :], ends[:, :, :], P - 1, None, ALU.bitwise_and).then_inc(bits, 1)
                nc.vector.tensor_scalar(hi_i[:, :, :], ends[:, :, :], 7, None,
                                        ALU.arith_shift_right).then_inc(bits, 1)
                nc.vector.tensor_scalar(rlo_i[:, :, :], row_i[:, :, :], P - 1, None,
                                        ALU.bitwise_and).then_inc(bits, 1)
                dve.wait_ge(bits, 3)
                nc.vector.tensor_copy(lo_b[:, :, :], lo_i[:, :, :]).then_inc(floats, 1)
                nc.vector.tensor_copy(hi_b[:, :, :], hi_i[:, :, :]).then_inc(floats, 1)
                nc.vector.tensor_tensor(self_b[:, :], ends[:, 0, :], ends[:, 1, :], ALU.is_equal).then_inc(floats, 1)
                nc.vector.tensor_copy(row_f[:, :, :], row_i[:, :, :]).then_inc(rows_ready, 1)
                nc.vector.tensor_copy(rlo_f[:, :, :], rlo_i[:, :, :]).then_inc(rows_ready, 1)
                dve.wait_ge(floats, 3)

                def one_hots(h, col):
                    for k in range(2):
                        nc.vector.tensor_tensor(oh_lo[:, h, k], bc_mid(K["iota_b"][:, :], G),
                                                bc_last(lo_b[:, k, bass.ds(col, G)], P),
                                                ALU.is_equal).then_inc(hots, 1)
                        nc.vector.tensor_tensor(oh_hi[:, h, k], bc_mid(K["iota_b"][:, 0:NB], G),
                                                bc_last(hi_b[:, k, bass.ds(col, G)], NB),
                                                ALU.is_equal).then_inc(hots, 1)

                def loops_hot(h, col):
                    nc.vector.tensor_tensor(oh_hi[:, h, 2], oh_hi[:, h, 1],
                                            bc_last(self_b[:, bass.ds(col, G)], NB),
                                            ALU.mult).then_inc(hots, 1)

                for h in range(2):
                    one_hots(h, h * G)
                    dve.wait_ge(hots, 5 * h + 4)
                    loops_hot(h, h * G)
                with dve.Fori(1, NG // 2) as i:
                    for h in range(2):
                        dve.wait_ge(counted, 2 * i + h - 1)
                        one_hots(h, (2 * i + h) * G)
                        dve.wait_ge(hots, 10 * i + 5 * h + 4)
                        loops_hot(h, (2 * i + h) * G)
                dve.wait_ge(counted, NG)
                nc.vector.tensor_copy(total[:, 0, :], p_dst[:, :]).then_inc(cnt_done, 1)
                nc.vector.tensor_copy(total[:, 1, :], p_src[:, 0, :]).then_inc(cnt_done, 1)
                nc.vector.tensor_copy(K["nloop"][:, :], p_src[:, 1, :]).then_inc(cnt_done, 1)
                nc.vector.memset(excl[:, :, 0:1], 0.0).then_inc(chain, 1)
                dve.wait_ge(cnt_done, 3)
                nc.vector.tensor_scalar(degc[:, :], total[:, 1, :], 1.0, None, ALU.max).then_inc(cnt_done, 1)
                dve.wait_ge(pre_done, 1)
                for b in range(NB):
                    dve.wait_ge(chain, b + 1)
                    nc.vector.tensor_tensor(excl[:, :, b + 1:b + 2], excl[:, :, b:b + 1], p_tot[:, :, b:b + 1],
                                            ALU.add).then_inc(chain, 1)
                dve.wait_ge(chain, NB + 1)
                nc.vector.tensor_tensor(K["first"][:, :, :], excl[:, :, 0:NB], p_pre[:, :, :],
                                        ALU.add).then_inc(chain, 1)
                dve.wait_ge(rooted, 1)
                nc.vector.reciprocal(K["dis"][:, :], rdeg[:, :]).then_inc(chain, 1)
                dve.wait_ge(chain, NB + 3)
                nc.vector.tensor_tensor(rdeg[:, :], K["dis"][:, :], K["dis"][:, :], ALU.mult).then_inc(chain, 1)
                dve.wait_ge(chain, NB + 4)
                nc.vector.tensor_tensor(degc[:, :], rdeg[:, :], degc[:, :], ALU.mult).then_inc(chain, 1)
                dve.wait_ge(chain, NB + 5)
                nc.vector.tensor_scalar(rdeg[:, :], degc[:, :], -0.5, 1.5, ALU.mult, ALU.add).then_inc(chain, 1)
                dve.wait_ge(chain, NB + 6)
                nc.vector.tensor_tensor(K["dis"][:, :], rdeg[:, :], K["dis"][:, :], ALU.mult).then_inc(chain, 1)
                dve.wait_ge(chain, NB + 7)
                nc.vector.tensor_scalar(K["ndis"][:, :], K["dis"][:, :], -1.0, None, ALU.mult).then_inc(chain, 1)

            @block.scalar
            def _(act):
                act.wait_ge(cnt_done, 4)
                nc.scalar.activation(rdeg[:, :], degc[:, :], ACT.Sqrt).then_inc(rooted, 1)

            @block.tensor
            def _(pe):
                def count(h, start, stop):
                    for g in range(G):
                        a, z = start and g == 0, stop and g == G - 1
                        nc.tensor.matmul(p_dst[:, :], oh_lo[:, h, 0, g], oh_hi[:, h, 0, g], start=a, stop=z)
                        last = nc.tensor.matmul(p_src[:, :, :], oh_lo[:, h, 1, g], oh_hi[:, h, 1:3, g],
                                                start=a, stop=z)
                    last.then_inc(counted, 1)

                for h in range(2):
                    pe.wait_ge(hots, 5 * h + 5)
                    count(h, h == 0, False)
                with pe.Fori(1, NG // 2 - 1) as i:
                    for h in range(2):
                        pe.wait_ge(hots, 10 * i + 5 * h + 5)
                        count(h, False, False)
                for h in range(2):
                    pe.wait_ge(hots, 5 * (NG - 2) + 5 * h + 5)
                    count(h, False, h == 1)
                pe.wait_ge(cnt_done, 3)
                nc.tensor.matmul(p_pre[:, :, :], K["after"][:, :], total[:, :, :], start=True, stop=True)
                nc.tensor.matmul(p_tot[:, :, :], K["ones"][:, :], total[:, :, :],
                                 start=True, stop=True).then_inc(pre_done, 1)


def sort_stage(nc, K, tag, which, key_p, other_p, rows, placed):
    with Scope(nc, tag) as s:
        ends = s.sb("ends", [P, 2, ET], I32)
        lo_i = s.sb("lo_i", [P, ET], I32)
        hi_i = s.sb("hi_i", [P, ET], I32)
        lo_b = s.sb("lo_b", [P, ET], BF16)
        hi_b = s.sb("hi_b", [P, ET], BF16)
        key_f = s.sb("key_f", [P, ET], F32)
        row = s.sb("row", [P, 2, 2, G * P], F32)
        oh_lo = s.sb("oh_lo", [P, 2, G, P], BF16)
        oh_hi = s.sb("oh_hi", [P, 2, G, NB], BF16)
        oh_loT = s.sb("oh_loT", [P, 2, G, P], F32)
        base = s.sb("base", [P, 2, G + 1, NB], F32)
        same = s.sb("same", [P, P], F32)
        rank = s.sb("rank", [P, G], F32)
        picked = s.sb("picked", [P, G, NB], F32)
        place_f = s.sb("place_f", [P, G], F32)
        place_g = s.sb("place_g", [P, G], F32)
        place_i = s.sb("place_i", [P, G], I32)
        pl_hi = s.sb("pl_hi", [P, G], I32)
        pl_lo = s.sb("pl_lo", [P, G], I32)
        addr_f = s.sb("addr_f", [P, G], F32)
        addr = s.sb("addr", [P, 2, G], U32)
        pair = s.sb("pair", [P, 2, G, 2], I32)
        p_cnt = s.ps("p_cnt", [P, 2, 512])
        p_pick = s.ps("p_pick", [P, 2, 512])
        loaded, prep = s.sem("loaded"), s.sem("prep")
        row_in = [s.sem(f"row_in{h}") for h in range(2)]
        hots, hotsT, counted = s.sem("hots"), s.sem("hotsT"), s.sem("counted")
        based, base_moved, pick_done = s.sem("based"), s.sem("base_moved"), s.sem("pick_done")
        chain, addr_ready, pair_ready = s.sem("chain"), s.sem("addr_ready"), s.sem("pair_ready")
        rows_used = s.sem("rows_used")
        scattered = [s.sem(f"scattered{h}") for h in range(2)]
        pool_go = s.sem("pool_go")
        STEPS = 6 + G
        with nc.Block() as block:
            @block.sync
            def _(sp):
                sp.dma_start(ends[:, 0, :], key_p).then_inc(loaded, 16)
                sp.dma_start(ends[:, 1, :], other_p).then_inc(loaded, 16)

                def load(h, q):
                    for r in range(2):
                        sp.dma_start(row[:, h, r, :], rows[which, r, bass.ds(q * (G * P), G * P)]
                                     .partition_broadcast(P)).then_inc(row_in[h], 16)
                for h in range(2):
                    load(h, h)
                with sp.Fori(1, NG // 2) as i:
                    for h in range(2):
                        sp.wait_ge(rows_used, 2 * i + h - 1)
                        load(h, 2 * i + h)

            @block.vector
            def _(dve):
                dve.wait_ge(loaded, 32)
                nc.vector.tensor_scalar(lo_i[:, :], ends[:, 0, :], P - 1, None, ALU.bitwise_and).then_inc(prep, 1)
                nc.vector.tensor_scalar(hi_i[:, :], ends[:, 0, :], 7, None, ALU.arith_shift_right).then_inc(prep, 1)
                nc.vector.tensor_copy(key_f[:, :], ends[:, 0, :]).then_inc(prep, 1)
                nc.vector.tensor_copy(base[:, 0, 0, :], K["first"][:, which, :]).then_inc(prep, 1)
                dve.wait_ge(prep, 4)
                nc.vector.tensor_copy(lo_b[:, :], lo_i[:, :]).then_inc(prep, 1)
                nc.vector.tensor_copy(hi_b[:, :], hi_i[:, :]).then_inc(prep, 1)
                dve.wait_ge(prep, 6)

                def one_hots(h, q):
                    nc.vector.tensor_tensor(oh_lo[:, h], bc_mid(K["iota_b"][:, :], G),
                                            bc_last(lo_b[:, bass.ds(q * G, G)], P), ALU.is_equal).then_inc(hots, 1)
                    nc.vector.tensor_tensor(oh_hi[:, h], bc_mid(K["iota_b"][:, 0:NB], G),
                                            bc_last(hi_b[:, bass.ds(q * G, G)], NB), ALU.is_equal).then_inc(hots, 1)

                def group(h, q, n, first, last):
                    if not last:
                        if not first:
                            dve.wait_ge(pick_done, q)
                        one_hots(1 - h, q + 1)
                    dve.wait_ge(row_in[h], 32 * n + 32)
                    nc.vector.tensor_scalar(oh_loT[:, h].rearrange("p g e -> p (g e)"), row[:, h, 1, :],
                                            K["part"][:, 0:1], None, ALU.is_equal).then_inc(hotsT, 1)
                    for g in range(G):
                        if g == 0:
                            if not first:
                                dve.wait_ge(chain, q * STEPS)
                        else:
                            dve.wait_ge(chain, q * STEPS + g)
                        r = nc.vector.scalar_tensor_tensor(same[:, :], row[:, h, 0, g * P:(g + 1) * P],
                                                           key_f[:, bass.ds(q * G + g, 1)],
                                                           K["before"][:, :], ALU.is_equal, ALU.mult,
                                                           accum_out=rank[:, g:g + 1])
                        r.then_inc(chain, 1)
                    dve.wait_ge(chain, q * STEPS + G)
                    nc.vector.memset(place_g[:, :], 0.0).then_inc(rows_used, 1)
                    dve.wait_ge(counted, q + 1)
                    if not first:
                        dve.wait_ge(base_moved, q)
                    nc.vector.tensor_tensor(base[:, h, 1:G + 1, :], bc_mid(base[:, h, 0, :], G),
                                            p_cnt[:, h, 0:G * NB].rearrange("p (g b) -> p g b", g=G),
                                            ALU.add).then_inc(based, 1)
                    dve.wait_ge(based, q + 1)
                    if not first:
                        dve.wait_ge(pick_done, q)
                    nc.vector.tensor_copy(base[:, 1 - h, 0, :], base[:, h, G, :]).then_inc(base_moved, 1)
                    dve.wait_ge(pick_done, q + 1)
                    c = q * STEPS + G
                    nc.vector.tensor_tensor(picked[:, :, :], p_pick[:, h, 0:G * NB].rearrange("p (g b) -> p g b", g=G),
                                            oh_hi[:, h], ALU.mult).then_inc(chain, 1)
                    dve.wait_ge(chain, c + 1)
                    nc.vector.tensor_reduce(place_f[:, :], picked[:, :, :], AX.X, ALU.add).then_inc(chain, 1)
                    dve.wait_ge(chain, c + 2)
                    nc.vector.tensor_tensor(place_i[:, :], place_f[:, :], rank[:, :], ALU.add).then_inc(chain, 1)
                    dve.wait_ge(chain, c + 3)
                    nc.vector.tensor_scalar(pl_hi[:, :], place_i[:, :], 7, None, ALU.arith_shift_right)
                    nc.vector.tensor_scalar(pl_lo[:, :], place_i[:, :], P - 1, None, ALU.bitwise_and).then_inc(chain, 1)
                    dve.wait_ge(chain, c + 4)
                    nc.vector.tensor_scalar(addr_f[:, :], pl_lo[:, :], float(ET), None, ALU.mult).then_inc(chain, 1)
                    dve.wait_ge(chain, c + 5)
                    if not first:
                        dve.wait_ge(scattered[h], 16 * G * n)
                    nc.vector.tensor_tensor(addr[:, h, :], addr_f[:, :], pl_hi[:, :], ALU.add).then_inc(chain, 1)
                    dve.wait_ge(chain, c + 6)
                    dve.sem_inc(addr_ready, 1)

                one_hots(0, 0)
                group(0, 0, 0, True, False)
                group(1, 1, 0, False, False)
                with dve.Fori(1, NG // 2 - 1) as i:
                    group(0, 2 * i, i, False, False)
                    group(1, 2 * i + 1, i, False, False)
                group(0, NG - 2, NG // 2 - 1, False, False)
                group(1, NG - 1, NG // 2 - 1, False, True)

            @block.tensor
            def _(pe):
                def group(h, q):
                    pe.wait_ge(hots, 2 * q + 2)
                    for g in range(G):
                        w = (G - g) * NB
                        last = nc.tensor.matmul(
                            p_cnt[:, h, g * NB:G * NB].rearrange("p (g b) -> p g b", b=NB),
                            oh_lo[:, h, g], bc_mid(oh_hi[:, h, g], G - g), start=(g == 0), stop=(g == G - 1))
                    last.then_inc(counted, 1)
                    pe.wait_ge(hotsT, q + 1)
                    pe.wait_ge(based, q + 1)
                    for g in range(G):
                        last = nc.tensor.matmul(p_pick[:, h, g * NB:(g + 1) * NB], oh_loT[:, h, g],
                                                base[:, h, g], start=True, stop=True)
                    last.then_inc(pick_done, 1)

                for h in range(2):
                    group(h, h)
                with pe.Fori(1, NG // 2) as i:
                    for h in range(2):
                        pe.wait_ge(addr_ready, 2 * i + h - 1)
                        group(h, 2 * i + h)

            @block.scalar
            def _(act):
                act.wait_ge(loaded, 32)

                def pairs(h, q):
                    for k in range(2):
                        nc.scalar.copy(pair[:, h, :, k], ends[:, k, bass.ds(q * G, G)]).then_inc(pair_ready, 1)
                for h in range(2):
                    pairs(h, h)
                with act.Fori(1, NG // 2) as i:
                    for h in range(2):
                        act.wait_ge(scattered[h], 16 * G * i)
                        pairs(h, 2 * i + h)

            @block.gpsimd
            def _(pool):
                with pool.Fori(0, NG // 2) as i:
                    for h in range(2):
                        pool.wait_ge(pair_ready, 4 * i + 2 * h + 2)
                        pool.sem_inc(pool_go, 1)
                        pool.wait_ge(addr_ready, 2 * i + h + 1)
                        pool.sem_inc(pool_go, 1)
                        for g in range(G):
                            nc.gpsimd.indirect_dma_start(
                                out=placed, out_offset=bass.IndirectOffsetOnAxis(ap=addr[:, h, g:g + 1], axis=0),
                                in_=pair[:, h, g, :], in_offset=None).then_inc(scattered[h], 16)
                pool.wait_ge(scattered[0], 16 * G * (NG // 2))
                pool.wait_ge(scattered[1], 16 * G * (NG // 2))


def spread_stage(nc, K, tag, placed, table, acc):
    with Scope(nc, tag) as s:
        pairs = s.sb("pairs", [P, ET, 2], I32)
        key_f = s.sb("key_f", [P, ET], F32)
        col = s.sb("col", [P, ET], F32)
        idx = s.sb("idx", [P, 2, G], U32)
        gath = s.sb("gath", [P, 2, G, D], F32)
        hot = s.sb("hot", [P, 2, G, P], F32)
        p_sum = s.ps("p_sum", [P, G, 512])
        loaded, prep, starts = s.sem("loaded"), s.sem("prep"), s.sem("starts")
        idx_ready, hot_ready = s.sem("idx_ready"), s.sem("hot_ready")
        gathered = [s.sem(f"gathered{h}") for h in range(2)]
        summed, added, pool_go, col_ready = s.sem("summed"), s.sem("added"), s.sem("pool_go"), s.sem("col_ready")
        pieces = [(c, min(512, ET - c)) for c in range(0, ET, 512)]
        with nc.Block() as block:
            @block.sync
            def _(sp):
                sp.dma_start(pairs[:, :, :], placed.rearrange("(p t) k -> p t k", p=P)).then_inc(loaded, 16)

            @block.tensor
            def _(pe):
                pe.wait_ge(prep, 1)
                for n, (c, w) in enumerate(pieces):
                    nc.tensor.matmul(p_sum[:, n, 0:w], K["ones"][0:1, :], key_f[0:1, c:c + w],
                                     start=True, stop=True).then_inc(starts, 1)
                pe.wait_ge(col_ready, len(pieces))

                def sums(h, q, i, first):
                    pe.wait_ge(gathered[h], 16 * G * i + 16 * G)
                    pe.wait_ge(hot_ready, q + 1)
                    for g in range(G):
                        if not first:
                            pe.wait_ge(added, q * G + g - G + 1)
                        for d in range(2):
                            last = nc.tensor.matmul(p_sum[:, g, d * P:(d + 1) * P],
                                                    gath[:, h, g, d * P:(d + 1) * P], hot[:, h, g],
                                                    start=True, stop=True)
                        last.then_inc(summed, 1)

                sums(0, 0, 0, True)
                sums(1, 1, 0, False)
                with pe.Fori(1, NG // 2) as i:
                    for h in range(2):
                        sums(h, 2 * i + h, i, False)

            @block.vector
            def _(dve):
                dve.wait_ge(loaded, 16)
                nc.vector.tensor_copy(key_f[:, :], pairs[:, :, 0]).then_inc(prep, 1)
                dve.wait_ge(prep, 1)
                for n, (c, w) in enumerate(pieces):
                    dve.wait_ge(starts, n + 1)
                    nc.vector.tensor_tensor(col[:, c:c + w], key_f[:, c:c + w], p_sum[:, n, 0:w],
                                            ALU.subtract).then_inc(col_ready, 1)
                dve.wait_ge(col_ready, len(pieces))

                def hots(h, q):
                    nc.vector.tensor_tensor(hot[:, h], bc_mid(K["iota"][:, :], G),
                                            bc_last(col[:, bass.ds(q * G, G)], P), ALU.is_equal).then_inc(hot_ready, 1)

                def adds(h, q, first, last):
                    if not last:
                        if not first:
                            dve.wait_ge(summed, q * G)
                        hots(1 - h, q + 1)
                    offs = nc.values_load_multi_w_load_instructions(
                        pairs[0:1, bass.ds(q * G, G), 0], engines=[DVE_ENGINE], min_val=0, max_val=PAD_KEY,
                        skip_runtime_bounds_check_because="an edge's end is a node or PAD_KEY")[1]
                    for g in range(G):
                        dve.wait_ge(summed, q * G + g + 1)
                        if not (first and g == 0):
                            dve.wait_ge(added, q * G + g)
                        win = acc[:, :, bass.ds(offs[g], P)]
                        nc.vector.tensor_tensor(win, win, p_sum[:, g, 0:2 * P].rearrange("p (d v) -> p d v", d=2),
                                                ALU.add).then_inc(added, 1)

                hots(0, 0)
                adds(0, 0, True, False)
                adds(1, 1, False, False)
                with dve.Fori(1, NG // 2 - 1) as i:
                    for h in range(2):
                        adds(h, 2 * i + h, False, False)
                adds(0, NG - 2, False, False)
                adds(1, NG - 1, False, True)

            @block.scalar
            def _(act):
                act.wait_ge(loaded, 16)
                for h in range(2):
                    nc.scalar.copy(idx[:, h, :], pairs[:, h * G:(h + 1) * G, 1]).then_inc(idx_ready, 1)
                with act.Fori(1, NG // 2) as i:
                    for h in range(2):
                        act.wait_ge(gathered[h], 16 * G * i)
                        nc.scalar.copy(idx[:, h, :], pairs[:, bass.ds((2 * i + h) * G, G), 1]).then_inc(idx_ready, 1)

            @block.gpsimd
            def _(pool):
                def gathers(h):
                    for g in range(G):
                        nc.gpsimd.indirect_dma_start(
                            out=gath[:, h, g, :], out_offset=None, in_=table,
                            in_offset=bass.IndirectOffsetOnAxis(ap=idx[:, h, g:g + 1], axis=0)).then_inc(gathered[h], 16)

                for h in range(2):
                    pool.wait_ge(idx_ready, h + 1)
                    gathers(h)
                with pool.Fori(1, NG // 2) as i:
                    for h in range(2):
                        pool.wait_ge(idx_ready, 2 * i + h + 1)
                        pool.sem_inc(pool_go, 1)
                        pool.wait_ge(summed, (2 * i + h - 1) * G)
                        pool.sem_inc(pool_go, 1)
                        gathers(h)


def clear_stage(nc, tag, arrays, acc):
    with Scope(nc, tag) as s:
        ROWS = 8
        zero = s.sb("zero", [P, ROWS * D], F32)
        made, stored = s.sem("made"), s.sem("stored")
        n = 0
        with nc.Block() as block:
            @block.vector
            def _(dve):
                nc.vector.memset(zero[:, :], 0.0).then_inc(made, 1)
                nc.vector.memset(acc[:, :, :], 0.0).then_inc(made, 1)
                dve.wait_ge(made, 2)

            @block.sync
            def _(sp):
                sp.wait_ge(made, 1)
                n = 0
                for a in arrays:
                    for r in range(0, a.shape[0], P * ROWS):
                        m = min(ROWS, (a.shape[0] - r) // P)
                        sp.dma_start(a[r:r + m * P, :].rearrange("(p r) d -> p (r d)", p=P),
                                     zero[:, 0:m * D]).then_inc(stored, 16)
                        n += 1
                sp.wait_ge(stored, 16 * n)


def norm_stage(nc, K, tag, X, x_in=None, xl_out=None, scaled_out=None, turned=None, proj=None):
    W = proj[0].shape[1] if proj else 0
    with Scope(nc, tag) as s:
        stats = s.sb("stats", [P, NB, 6], F32)
        mean = s.sb("mean", [P, NB], F32)
        var = s.sb("var", [P, NB], F32)
        half = s.sb("half", [P, NB], F32)
        root = s.sb("root", [P, NB], F32)
        rstd = s.sb("rstd", [P, NB], F32)
        xl = s.sb("xl", [P, 2, D], F32)
        xs = s.sb("xs", [P, 2, D], F32)
        xT = s.sb("xT", [P, 2, DH, P], F32)
        factor = s.sb("factor", [P, 1], F32)
        w = s.sb("w", [P, DH, max(W, 1)], F32)
        p_turn = s.ps("p_turn", [P, 2, 512])
        p_proj = s.ps("p_proj", [P, 2, 512])
        x_loaded, w_loaded, padded = s.sem("x_loaded"), s.sem("w_loaded"), s.sem("padded")
        stat, chain, rooted = s.sem("stat"), s.sem("chain"), s.sem("rooted")
        normed, scaled, turned_sem, evac = s.sem("normed"), s.sem("scaled"), s.sem("turned"), s.sem("evac")
        projd, proj_out = s.sem("projd"), s.sem("proj_out")
        xl_stored = [s.sem(f"xl_stored{h}") for h in range(2)]
        xs_stored = [s.sem(f"xs_stored{h}") for h in range(2)]
        PAIRS = NB // 2

        def blocks(eng, body):
            with eng.Fori(1, PAIRS) as i:
                for h in range(2):
                    body(h, 2 * i + h, i)

        with nc.Block() as block:
            @block.sync
            def _(sp):
                if x_in is not None:
                    whole = (NB - 1) * P
                    sp.wait_ge(padded, 1)
                    sp.dma_start(X[0:LAST, NB - 1, :], x_in[whole:N, :]).then_inc(x_loaded, 16)
                    for c in range(0, NB - 1, 12):
                        sp.dma_start(X[:, c:c + 12, :], x_in[c * P:(c + 12) * P, :]
                                     .rearrange("(b p) d -> p b d", p=P)).then_inc(x_loaded, 16)
                if turned:
                    sp.dma_start(factor[:, :], turned[1].partition_broadcast(P)).then_inc(w_loaded, 16)
                if proj:
                    sp.dma_start(w[:, :, :], proj[0].rearrange("(k p) w -> p k w", p=P)).then_inc(w_loaded, 16)

                if xl_out is not None:
                    def store(h, b, i):
                        sp.wait_ge(normed, b + 1)
                        sp.dma_start(xl_out[bass.ds(b * P, P), :], xl[:, h, :]).then_inc(xl_stored[h], 16)
                    store(0, 0, 0)
                    store(1, 1, 0)
                    blocks(sp, store)
                    store(0, NB - 1, PAIRS)
                    sp.wait_ge(xl_stored[0], 16 * (PAIRS + 1))
                    sp.wait_ge(xl_stored[1], 16 * PAIRS)

            @block.vector
            def _(dve):
                if x_in is not None:
                    nc.vector.memset(X[:, NB - 1, :], 0.0).then_inc(padded, 1)
                    dve.wait_ge(x_loaded, 16 * (1 + len(range(0, NB - 1, 12))))
                with dve.Fori(0, NB) as b:
                    nc.vector.bn_stats(stats[:, bass.ds(b, 1), :].rearrange("p a s -> p (a s)"),
                                       X[:, bass.ds(b, 1), :].rearrange("p a d -> p (a d)")).then_inc(stat, 1)
                dve.wait_ge(stat, NB)
                nc.vector.tensor_tensor(mean[:, :], stats[:, :, 1], stats[:, :, 4], ALU.add).then_inc(chain, 1)
                nc.vector.tensor_tensor(half[:, :], stats[:, :, 1], stats[:, :, 4], ALU.subtract).then_inc(chain, 1)
                nc.vector.tensor_tensor(var[:, :], stats[:, :, 2], stats[:, :, 5], ALU.add).then_inc(chain, 1)
                dve.wait_ge(chain, 3)
                nc.vector.tensor_scalar(mean[:, :], mean[:, :], 0.5, None, ALU.mult).then_inc(chain, 1)
                nc.vector.tensor_tensor(half[:, :], half[:, :], half[:, :], ALU.mult).then_inc(chain, 1)
                nc.vector.tensor_scalar(var[:, :], var[:, :], 1.0 / D, LN_EPS, ALU.mult, ALU.add).then_inc(chain, 1)
                dve.wait_ge(chain, 6)
                nc.vector.scalar_tensor_tensor(var[:, :], half[:, :], 0.25, var[:, :], ALU.mult,
                                               ALU.add).then_inc(chain, 1)
                dve.wait_ge(rooted, 1)
                nc.vector.reciprocal(rstd[:, :], root[:, :]).then_inc(chain, 1)
                dve.wait_ge(chain, 8)
                nc.vector.tensor_tensor(half[:, :], rstd[:, :], rstd[:, :], ALU.mult).then_inc(chain, 1)
                dve.wait_ge(chain, 9)
                nc.vector.tensor_tensor(half[:, :], half[:, :], var[:, :], ALU.mult).then_inc(chain, 1)
                dve.wait_ge(chain, 10)
                nc.vector.tensor_scalar(half[:, :], half[:, :], -0.5, 1.5, ALU.mult, ALU.add).then_inc(chain, 1)
                dve.wait_ge(chain, 11)
                nc.vector.tensor_tensor(rstd[:, :], rstd[:, :], half[:, :], ALU.mult).then_inc(chain, 1)
                dve.wait_ge(chain, 12)

                def norm(h, b, i, first=False):
                    if not first:
                        if xl_out is not None:
                            dve.wait_ge(xl_stored[h], 16 * i)
                        if scaled_out is not None:
                            dve.wait_ge(scaled, b - 1)
                        dve.wait_ge(turned_sem, b - 1)
                    nc.vector.tensor_scalar(xl[:, h, :], X[:, bass.ds(b, 1), :].rearrange("p a d -> p (a d)"),
                                            mean[:, bass.ds(b, 1)], rstd[:, bass.ds(b, 1)],
                                            ALU.subtract, ALU.mult).then_inc(normed, 1)

                def take(h, b):
                    dve.wait_ge(projd, b + 1)
                    nc.vector.tensor_copy(proj[1][:, bass.ds(b, 1), :].rearrange("p a w -> p (a w)"),
                                          p_proj[:, h, 0:W]).then_inc(proj_out, 1)

                def step(h, b, i):
                    norm(h, b, i)
                    if proj:
                        take(1 - h, b - 1)

                norm(0, 0, 0, True)
                norm(1, 1, 0, True)
                if proj:
                    take(0, 0)
                blocks(dve, step)
                step(0, NB - 1, PAIRS)
                if proj:
                    take(0, NB - 1)
                    dve.wait_ge(proj_out, NB)

            @block.scalar
            def _(act):
                act.wait_ge(chain, 7)
                nc.scalar.activation(root[:, :], var[:, :], ACT.Sqrt).then_inc(rooted, 1)
                if turned:
                    act.wait_ge(w_loaded, 16)

                def step(h, b, i, first=False):
                    if scaled_out is not None:
                        act.wait_ge(normed, b + 1)
                        if not first:
                            act.wait_ge(xs_stored[h], 16 * i)
                        nc.scalar.activation(xs[:, h, :], xl[:, h, :], ACT.Copy,
                                             scale=K["dis"][:, bass.ds(b, 1)]).then_inc(scaled, 1)
                        act.wait_ge(scaled, b + 1)
                        act.dma_start(scaled_out[bass.ds(b * P, P), :], xs[:, h, :]).then_inc(xs_stored[h], 16)
                    act.wait_ge(turned_sem, b + 1)
                    src = p_turn[:, h, 0:D].rearrange("p (k v) -> p k v", k=DH)
                    if turned:
                        nc.scalar.activation(turned[0][:, :, bass.ds(b * P, P)], src, ACT.Copy,
                                             scale=factor[:, 0:1]).then_inc(evac, 1)
                    else:
                        if not first:
                            act.wait_ge(projd, b - 1)
                        nc.scalar.copy(xT[:, h], src).then_inc(evac, 1)

                step(0, 0, 0, True)
                step(1, 1, 0, True)
                blocks(act, step)
                step(0, NB - 1, PAIRS)
                if scaled_out is not None:
                    act.wait_ge(xs_stored[0], 16 * (PAIRS + 1))
                    act.wait_ge(xs_stored[1], 16 * PAIRS)
                act.wait_ge(evac, NB)

            @block.tensor
            def _(pe):
                if proj:
                    pe.wait_ge(w_loaded, 16)

                def turn(h, b, first=False):
                    pe.wait_ge(normed, b + 1)
                    if not first:
                        pe.wait_ge(evac, b - 1)
                    for k in range(DH):
                        last = nc.tensor.transpose(p_turn[:, h, k * P:(k + 1) * P], xl[:, h, k * P:(k + 1) * P],
                                                   K["ident"][:, :])
                    last.then_inc(turned_sem, 1)

                def product(h, b, first=False):
                    pe.wait_ge(evac, b + 1)
                    if not first:
                        pe.wait_ge(proj_out, b - 1)
                    for k in range(DH):
                        last = nc.tensor.matmul(p_proj[:, h, 0:W], xT[:, h, k], w[:, k, :],
                                                start=(k == 0), stop=(k == DH - 1))
                    last.then_inc(projd, 1)

                turn(0, 0, True)
                turn(1, 1, True)
                if proj:
                    product(0, 0, True)
                    product(1, 1, True)

                def step(h, b, i):
                    turn(h, b)
                    if proj:
                        product(h, b)
                blocks(pe, step)
                step(0, NB - 1, PAIRS)


def network0_stage(nc, K, tag, X, acc, w1_in, b1_in, w2_in, b2_in, gamma_in, beta_in):
    MH = HID // P
    with Scope(nc, tag) as s:
        w1 = s.sb("w1", [P, DH, HID], F32)
        w2 = s.sb("w2", [P, MH, D], F32)
        b1 = s.sb("b1", [P, MH], F32)
        b2 = s.sb("b2", [P, DH], F32)
        gamma = s.sb("gamma", [P, DH], F32)
        beta = s.sb("beta", [P, DH], F32)
        hid = s.sb("hid", [P, MH, CH], F32)
        NC = len(CHUNKS)
        stats = s.sb("stats", [P, DH, NC, 6], F32)
        agg = s.sb("agg", [P, DH, 2], F32)
        root = s.sb("root", [P, DH], F32)
        scale = s.sb("scale", [P, DH], F32)
        shift = s.sb("shift", [P, DH], F32)
        tmp = s.sb("tmp", [P, DH], F32)
        bn = s.sb("bn", [P, 2, DH, P], F32)
        p_hid = s.ps("p_hid", [P, MH, 512])
        p_out = s.ps("p_out", [P, DH, 512])
        p_back = s.ps("p_back", [P, 2, 512])
        loaded, hid_mm, hid_ready = s.sem("loaded"), s.sem("hid_mm"), s.sem("hid_ready")
        out_mm, out_ready, stat, chain = s.sem("out_mm"), s.sem("out_ready"), s.sem("stat"), s.sem("chain")
        rooted, bn_ready, backed, addx = s.sem("rooted"), s.sem("bn_ready"), s.sem("backed"), s.sem("addx")
        CW = CHUNKS[-1][1]
        with nc.Block() as block:
            @block.sync
            def _(sp):
                sp.dma_start(w1[:, :, :], w1_in.rearrange("(k p) n -> p k n", p=P)).then_inc(loaded, 16)
                sp.dma_start(w2[:, :, :], w2_in.rearrange("(k p) n -> p k n", p=P)).then_inc(loaded, 16)
                with nc.allow_non_contiguous_dma(reason="a few hundred floats"):
                    sp.dma_start(b1[:, :], b1_in.rearrange("(m p) -> p m", p=P)).then_inc(loaded, 16)
                    sp.dma_start(b2[:, :], b2_in.rearrange("(m p) -> p m", p=P)).then_inc(loaded, 16)
                    sp.dma_start(gamma[:, :], gamma_in.rearrange("(m p) -> p m", p=P)).then_inc(loaded, 16)
                    sp.dma_start(beta[:, :], beta_in.rearrange("(m p) -> p m", p=P)).then_inc(loaded, 16)

            @block.tensor
            def _(pe):
                pe.wait_ge(loaded, 96)

                def chunk(c, n, w, first=False):
                    for m in range(MH):
                        if not first:
                            pe.wait_ge(hid_ready, n * MH - MH + m + 1)
                        for k in range(DH):
                            last = nc.tensor.matmul(p_hid[:, m, 0:w], w1[:, k, m * P:(m + 1) * P],
                                                    acc[:, k, bass.ds(c, w)], start=(k == 0), stop=(k == DH - 1))
                        last.then_inc(hid_mm, 1)
                    for o in range(DH):
                        if not first:
                            pe.wait_ge(out_ready, n * DH - DH + o + 1)
                        for m in range(MH):
                            if o == 0:
                                pe.wait_ge(hid_ready, n * MH + m + 1)
                            last = nc.tensor.matmul(p_out[:, o, 0:w], w2[:, m, o * P:(o + 1) * P], hid[:, m, 0:w],
                                                    start=(m == 0), stop=(m == MH - 1))
                        last.then_inc(out_mm, 1)

                chunk(0, 0, CH, True)
                with pe.Fori(1, NC - 1) as n:
                    chunk(n * CH, n, CH)
                chunk((NC - 1) * CH, NC - 1, CW)

                def back(h, b, first=False):
                    pe.wait_ge(bn_ready, b + 1)
                    if not first:
                        pe.wait_ge(addx, b - 1)
                    for k in range(DH):
                        last = nc.tensor.transpose(p_back[:, h, k * P:(k + 1) * P], bn[:, h, k], K["ident"][:, :])
                    last.then_inc(backed, 1)
                back(0, 0, True)
                back(1, 1, True)
                with pe.Fori(1, NB // 2) as i:
                    for h in range(2):
                        back(h, 2 * i + h)
                back(0, NB - 1)

            @block.scalar
            def _(act):
                act.wait_ge(loaded, 96)

                def chunk(c, n, w, first=False):
                    for m in range(MH):
                        act.wait_ge(hid_mm, n * MH + m + 1)
                        if not first:
                            act.wait_ge(out_mm, n * DH)
                        nc.scalar.activation(hid[:, m, 0:w], p_hid[:, m, 0:w], ACT.Relu,
                                             bias=b1[:, m:m + 1]).then_inc(hid_ready, 1)
                chunk(0, 0, CH, True)
                with act.Fori(1, NC - 1) as n:
                    chunk(n * CH, n, CH)
                chunk((NC - 1) * CH, NC - 1, CW)
                act.wait_ge(chain, 3)
                nc.scalar.activation(root[:, :], tmp[:, :], ACT.Sqrt).then_inc(rooted, 1)
                act.wait_ge(chain, 10)

                def norm(h, b, first=False):
                    if not first:
                        act.wait_ge(backed, b - 1)
                    for k in range(DH):
                        last = nc.scalar.activation(bn[:, h, k], acc[:, k, bass.ds(b * P, P)], ACT.Identity,
                                                    bias=shift[:, k:k + 1], scale=scale[:, k:k + 1])
                    last.then_inc(bn_ready, 1)
                norm(0, 0, True)
                norm(1, 1, True)
                with act.Fori(1, NB // 2) as i:
                    for h in range(2):
                        norm(h, 2 * i + h)
                norm(0, NB - 1)

            @block.vector
            def _(dve):
                dve.wait_ge(loaded, 96)

                def chunk(c, n, w):
                    for o in range(DH):
                        dve.wait_ge(out_mm, n * DH + o + 1)
                        nc.vector.tensor_scalar(acc[:, o, bass.ds(c, w)], p_out[:, o, 0:w], b2[:, o:o + 1], None,
                                                ALU.add).then_inc(out_ready, 1)
                    for o in range(DH):
                        dve.wait_ge(out_ready, n * DH + o + 1)
                        v = min(w, N - (NC - 1) * CH) if w != CH else w
                        nc.vector.bn_stats(stats[:, o, bass.ds(n, 1), :].rearrange("p a s -> p (a s)"),
                                           acc[:, o, bass.ds(c, v)]).then_inc(stat, 1)
                with dve.Fori(0, NC - 1) as n:
                    chunk(n * CH, n, CH)
                chunk((NC - 1) * CH, NC - 1, CW)
                dve.wait_ge(stat, DH * NC)
                for o in range(DH):
                    nc.vector.bn_aggr(agg[:, o, :], stats[:, o, :, :].rearrange("p n s -> p (n s)")).then_inc(chain, 1)
                dve.wait_ge(chain, 2)
                nc.vector.tensor_scalar(tmp[:, :], agg[:, :, 1], 1e-5, None, ALU.add).then_inc(chain, 1)
                dve.wait_ge(rooted, 1)
                nc.vector.reciprocal(scale[:, :], root[:, :]).then_inc(chain, 1)
                dve.wait_ge(chain, 4)
                nc.vector.tensor_tensor(shift[:, :], scale[:, :], scale[:, :], ALU.mult).then_inc(chain, 1)
                dve.wait_ge(chain, 5)
                nc.vector.tensor_tensor(shift[:, :], shift[:, :], tmp[:, :], ALU.mult).then_inc(chain, 1)
                dve.wait_ge(chain, 6)
                nc.vector.tensor_scalar(shift[:, :], shift[:, :], -0.5, 1.5, ALU.mult, ALU.add).then_inc(chain, 1)
                dve.wait_ge(chain, 7)
                nc.vector.tensor_tensor(scale[:, :], scale[:, :], shift[:, :], ALU.mult).then_inc(chain, 1)
                dve.wait_ge(chain, 8)
                nc.vector.tensor_tensor(scale[:, :], scale[:, :], gamma[:, :], ALU.mult).then_inc(chain, 1)
                dve.wait_ge(chain, 9)
                for o in range(DH):
                    nc.vector.scalar_tensor_tensor(tmp[:, o:o + 1], agg[:, o, 0:1], -1.0, scale[:, o:o + 1],
                                                   ALU.mult, ALU.mult).then_inc(stat, 1)
                dve.wait_ge(stat, DH * NC + DH)
                nc.vector.tensor_tensor(shift[:, :], tmp[:, :], beta[:, :], ALU.add).then_inc(chain, 1)

                def add(h, b):
                    dve.wait_ge(backed, b + 1)
                    xb = X[:, bass.ds(b, 1), :].rearrange("p a d -> p (a d)")
                    nc.vector.tensor_tensor(xb, xb, p_back[:, h, 0:D], ALU.add).then_inc(addx, 1)
                with dve.Fori(0, NB // 2) as i:
                    for h in range(2):
                        add(h, 2 * i + h)
                add(0, NB - 1)
                dve.wait_ge(addx, NB)


def in_pairs(eng, count, body):
    body(0, 0, 0, True)
    body(1, 1, 0, True)
    with eng.Fori(1, count // 2) as i:
        for h in range(2):
            body(h, 2 * i + h, i, False)
    if count % 2:
        body(0, count - 1, count // 2, False)


def waits_of_half(count, h):
    return (count + 1 - h) // 2


def laplace_stage(nc, K, tag, X, acc, out, order, w_in, prev, prev2, mine, table, bias_in):
    last_term = order == 3
    with Scope(nc, tag) as s:
        w = s.sb("w", [P, DH, D], F32)
        bias = s.sb("bias", [P, D], F32)
        fm = s.sb("fm", [P, 2, DH, P], F32)
        t1 = s.sb("t1", [P, 2, D], F32)
        t2 = s.sb("t2", [P, 2, D], F32)
        part = s.sb("part", [P, 2, D], F32)
        term = s.sb("term", [P, 2, D], F32)
        xs = s.sb("xs", [P, 2, D], F32)
        tT = s.sb("tT", [P, 2, DH, P], F32)
        p_sum = s.ps("p_sum", [P, 2, 512])
        p_turn = s.ps("p_turn", [P, 2, 512])
        p_out = s.ps("p_out", [P, 2, 512])
        loaded = s.sem("loaded")
        t_in = [s.sem(f"t_in{h}") for h in range(2)]
        cut, cleared, summed, parted = s.sem("cut"), s.sem("cleared"), s.sem("summed"), s.sem("parted")
        lapl, termed, turned, evac = s.sem("lapl"), s.sem("termed"), s.sem("turned"), s.sem("evac")
        scaled, outd, added, biased = s.sem("scaled"), s.sem("outd"), s.sem("added"), s.sem("biased")
        mine_stored = [s.sem(f"mine_stored{h}") for h in range(2)]
        xs_stored = [s.sem(f"xs_stored{h}") for h in range(2)]
        LOADS = 1 if order == 1 else 2
        with nc.Block() as block:
            @block.sync
            def _(sp):
                sp.dma_start(w[:, :, :], w_in.rearrange("(k p) n -> p k n", p=P)).then_inc(loaded, 16)
                sp.dma_start(bias[:, :], bias_in.partition_broadcast(P)).then_inc(loaded, 16)

                def load(h, b, i, first):
                    if not first:
                        sp.wait_ge(termed, b - 1)
                    sp.dma_start(t1[:, h, :], prev[bass.ds(b * P, P), :]).then_inc(t_in[h], 16)
                    if order > 1:
                        sp.dma_start(t2[:, h, :], prev2[bass.ds(b * P, P), :]).then_inc(t_in[h], 16)
                in_pairs(sp, NB, load)

            @block.scalar
            def _(act):
                def cut_block(h, b, first):
                    if not first:
                        act.wait_ge(summed, b - 1)
                    nc.scalar.copy(fm[:, h], acc[:, :, bass.ds(b * P, P)]).then_inc(cut, 1)

                def step(h, b, i, first):
                    cut_block(h, b, first)
                    act.wait_ge(turned, b + 1)
                    if not first:
                        act.wait_ge(outd, b - 1)
                    nc.scalar.copy(tT[:, h], p_turn[:, h, 0:D].rearrange("p (k v) -> p k v", k=DH)).then_inc(evac, 1)
                    if not last_term:
                        if not first:
                            act.wait_ge(xs_stored[h], 16 * i)
                        nc.scalar.activation(xs[:, h, :], term[:, h, :], ACT.Copy,
                                             scale=K["dis"][:, bass.ds(b, 1)]).then_inc(scaled, 1)
                        act.wait_ge(scaled, b + 1)
                        act.dma_start(table[bass.ds(b * P, P), :], xs[:, h, :]).then_inc(xs_stored[h], 16)
                        act.dma_start(mine[bass.ds(b * P, P), :], term[:, h, :]).then_inc(mine_stored[h], 16)
                in_pairs(act, NB, step)
                if not last_term:
                    for h in range(2):
                        act.wait_ge(xs_stored[h], 16 * waits_of_half(NB, h))
                        act.wait_ge(mine_stored[h], 16 * waits_of_half(NB, h))

            @block.tensor
            def _(pe):
                pe.wait_ge(loaded, 32)

                def step(h, b, i, first):
                    pe.wait_ge(cut, b + 1)
                    if not first:
                        pe.wait_ge(parted, b - 1)
                    for k in range(DH):
                        last = nc.tensor.transpose(p_sum[:, h, k * P:(k + 1) * P], fm[:, h, k], K["ident"][:, :])
                    last.then_inc(summed, 1)
                    pe.wait_ge(termed, b + 1)
                    if not first:
                        pe.wait_ge(evac, b - 1)
                    for k in range(DH):
                        last = nc.tensor.transpose(p_turn[:, h, k * P:(k + 1) * P], term[:, h, k * P:(k + 1) * P],
                                                   K["ident"][:, :])
                    last.then_inc(turned, 1)
                    pe.wait_ge(evac, b + 1)
                    if not first:
                        pe.wait_ge(added, b - 1)
                    for k in range(DH):
                        last = nc.tensor.matmul(p_out[:, h, 0:D], tT[:, h, k], w[:, k, :],
                                                start=(k == 0), stop=(k == DH - 1))
                    last.then_inc(outd, 1)
                in_pairs(pe, NB, step)

            @block.vector
            def _(dve):
                if last_term:
                    dve.wait_ge(loaded, 32)

                def step(h, b, i, first):
                    dve.wait_ge(cut, b + 1)
                    nc.vector.tensor_copy(acc[:, :, bass.ds(b * P, P)], K["zero"][:, :, :]).then_inc(cleared, 1)
                    dve.wait_ge(summed, b + 1)
                    nc.vector.tensor_scalar(part[:, h, :], p_sum[:, h, 0:D], K["ndis"][:, bass.ds(b, 1)], None,
                                            ALU.mult).then_inc(parted, 1)
                    dve.wait_ge(parted, b + 1)
                    dve.wait_ge(t_in[h], 16 * LOADS * i + 16 * LOADS)
                    if not first:
                        dve.wait_ge(turned, b - 1)
                        if not last_term:
                            dve.wait_ge(scaled, b - 1)
                            dve.wait_ge(mine_stored[h], 16 * i)
                    if order == 1:
                        nc.vector.scalar_tensor_tensor(term[:, h, :], t1[:, h, :], K["nloop"][:, bass.ds(b, 1)],
                                                       part[:, h, :], ALU.mult, ALU.add).then_inc(termed, 1)
                    else:
                        nc.vector.scalar_tensor_tensor(part[:, h, :], t1[:, h, :], K["nloop"][:, bass.ds(b, 1)],
                                                       part[:, h, :], ALU.mult, ALU.add).then_inc(lapl, 1)
                        dve.wait_ge(lapl, b + 1)
                        nc.vector.scalar_tensor_tensor(term[:, h, :], part[:, h, :], 2.0, t2[:, h, :],
                                                       ALU.mult, ALU.subtract).then_inc(termed, 1)
                    dve.wait_ge(outd, b + 1)
                    ob = out[:, bass.ds(b, 1), :].rearrange("p a d -> p (a d)")
                    nc.vector.tensor_tensor(ob, ob, p_out[:, h, 0:D], ALU.add).then_inc(added, 1)
                    if last_term:
                        xb = X[:, bass.ds(b, 1), :].rearrange("p a d -> p (a d)")
                        dve.wait_ge(added, b + 1)
                        nc.vector.tensor_tensor(xb, xb, bias[:, :], ALU.add).then_inc(biased, 1)
                        dve.wait_ge(biased, 2 * b + 1)
                        nc.vector.tensor_tensor(xb, xb, ob, ALU.add).then_inc(biased, 1)
                in_pairs(dve, NB, step)


T0 = -(-(2 * N + NE * (P - 1)) // (2 * P)) * 2
T1E = -(-CAP // CH) * CH


def route_stage(nc, K, tag, logits, R, top, bias_in=None):
    first_mix = top == 2
    with Scope(nc, tag) as s:
        shape = [P, NB, NE]
        best = s.sb("best", [P, NB], F32)
        ssum = s.sb("ssum", [P, NB], F32)
        ex = s.sb("ex", shape, F32)
        prob = s.sb("prob", shape, F32)
        eq = s.sb("eq", shape, F32)
        cand = s.sb("cand", shape, F32)
        hot = s.sb("hot", [P, 2, NB, NE], F32)
        both = s.sb("both", shape, F32)
        valid = s.sb("valid", [P, NB], F32)
        top_p = s.sb("top_p", [P, 2, NB], F32)
        low = s.sb("low", [P, NB], F32)
        before = s.sb("before", [P, NB + 1, NE], F32)
        cnt_i = s.sb("cnt_i", [P, NE], I32)
        tiles_i = s.sb("tiles_i", [P, NE], I32)
        tiles = s.sb("tiles", [P, NE], F32)
        ends = s.sb("ends", [P, NE + 1], F32)
        place = s.sb("place", shape, F32)
        slot = s.sb("slot", [P, 2, NB], F32)
        over = s.sb("over", [P, NB], F32)
        tnum = s.sb("tnum", [P, P], F32)
        past = s.sb("past", [P, P], F32)
        gb = s.sb("gb", [P, NE], F32)
        p_pre = s.ps("p_pre", [P, 512])
        p_tot = s.ps("p_tot", [P, 512])
        chain, biased, exped, hotted, counted = (s.sem(n) for n in ("chain", "biased", "exped", "hotted", "counted"))
        iota8 = bc_mid(K["iota"][:, 0:NE], NB)
        with nc.Block() as block:
            @block.sync
            def _(sp):
                if bias_in is not None:
                    sp.dma_start(gb[:, :], bias_in.partition_broadcast(P)).then_inc(biased, 16)

            @block.vector
            def _(dve):
                n = [0]

                def link(ins):
                    n[0] += 1
                    ins.then_inc(chain, 1)
                    dve.wait_ge(chain, n[0])

                if bias_in is not None:
                    dve.wait_ge(biased, 16)
                    link(nc.vector.tensor_tensor(logits[:, :, :], logits[:, :, :], bc_mid(gb[:, :], NB), ALU.add))
                link(nc.vector.tensor_reduce(best[:, :], logits[:, :, :], AX.X, ALU.max))
                link(nc.vector.tensor_tensor(ex[:, :, :], logits[:, :, :], bc_last(best[:, :], NE), ALU.subtract))
                nc.vector.memset(valid[:, :], 1.0).then_inc(hotted, 1)
                dve.wait_ge(hotted, 1)
                link(nc.vector.tensor_scalar(valid[:, NB - 1:NB], K["part"][:, 0:1], float(LAST), None, ALU.is_lt))
                dve.wait_ge(exped, 1)
                link(nc.vector.tensor_reduce(ssum[:, :], prob[:, :, :], AX.X, ALU.add))
                link(nc.vector.reciprocal(best[:, :], ssum[:, :]))
                link(nc.vector.tensor_tensor(prob[:, :, :], prob[:, :, :], bc_last(best[:, :], NE), ALU.mult))
                for c in range(top):
                    link(nc.vector.tensor_reduce(top_p[:, c, :], prob[:, :, :], AX.X, ALU.max))
                    link(nc.vector.tensor_tensor(eq[:, :, :], prob[:, :, :], bc_last(top_p[:, c, :], NE), ALU.is_equal))
                    link(nc.vector.scalar_tensor_tensor(cand[:, :, :], eq[:, :, :], -float(NE), iota8,
                                                        ALU.mult, ALU.add))
                    link(nc.vector.tensor_reduce(low[:, :], cand[:, :, :], AX.X, ALU.min))
                    link(nc.vector.tensor_tensor(eq[:, :, :], cand[:, :, :], bc_last(low[:, :], NE), ALU.is_equal))
                    link(nc.vector.tensor_tensor(hot[:, c], eq[:, :, :], bc_last(valid[:, :], NE), ALU.mult))
                    if c + 1 < top:
                        link(nc.vector.scalar_tensor_tensor(prob[:, :, :], eq[:, :, :], -2.0, prob[:, :, :],
                                                            ALU.mult, ALU.add))
                if first_mix:
                    nc.vector.tensor_tensor(both[:, :, :], hot[:, 0], hot[:, 1], ALU.add).then_inc(hotted, 1)
                    link(nc.vector.tensor_tensor(low[:, :], top_p[:, 0, :], top_p[:, 1, :], ALU.add))
                    link(nc.vector.tensor_scalar(low[:, :], low[:, :], 1e-9, None, ALU.add))
                    link(nc.vector.reciprocal(best[:, :], low[:, :]))
                    link(nc.vector.tensor_tensor(R["gate"][:, :, :], top_p[:, :, :], bc_mid(best[:, :], 2), ALU.mult))
                else:
                    nc.vector.tensor_copy(both[:, :, :], hot[:, 0]).then_inc(hotted, 1)
                dve.wait_ge(counted, 1)
                tot = p_tot[:, 0:NB * NE].rearrange("p (b e) -> p b e", e=NE)
                pre = p_pre[:, 0:NB * NE].rearrange("p (b e) -> p b e", e=NE)
                link(nc.vector.memset(before[:, 0, :], 0.0))
                for b in range(NB):
                    link(nc.vector.tensor_tensor(before[:, b + 1, :], before[:, b, :], tot[:, b, :], ALU.add))
                link(nc.vector.tensor_tensor(place[:, :, :], before[:, 0:NB, :], pre, ALU.add))
                if first_mix:
                    link(nc.vector.tensor_scalar(cnt_i[:, :], before[:, NB, :], float(P - 1), None, ALU.add))
                    link(nc.vector.tensor_scalar(tiles_i[:, :], cnt_i[:, :], 7, None, ALU.arith_shift_right))
                    link(nc.vector.tensor_copy(tiles[:, :], tiles_i[:, :]))
                    link(nc.vector.memset(ends[:, 0:1], 0.0))
                    for e in range(NE):
                        link(nc.vector.tensor_tensor(ends[:, e + 1:e + 2], ends[:, e:e + 1], tiles[:, e:e + 1], ALU.add))
                    link(nc.vector.tensor_scalar(tiles[:, :], ends[:, 0:NE], float(P), None, ALU.mult))
                    link(nc.vector.tensor_tensor(place[:, :, :], place[:, :, :], bc_mid(tiles[:, :], NB), ALU.add))
                    link(nc.vector.memset(tnum[:, :], 0.0))
                    for e in range(NE - 1):
                        link(nc.vector.tensor_scalar(past[:, :], K["iota"][:, :], ends[:, e + 1:e + 2], None, ALU.is_ge))
                        link(nc.vector.tensor_tensor(tnum[:, :], tnum[:, :], past[:, :], ALU.add))
                    link(nc.vector.tensor_copy(R["tile_expert"][:, :], tnum[:, :]))
                for c in range(top):
                    link(nc.vector.tensor_tensor(eq[:, :, :], hot[:, c], place[:, :, :], ALU.mult))
                    link(nc.vector.tensor_reduce(slot[:, c, :], eq[:, :, :], AX.X, ALU.add))
                if first_mix:
                    link(nc.vector.tensor_copy(R["to"][:, :, :], slot[:, :, :]))
                    link(nc.vector.tensor_copy(R["of"][:, :, :], slot[:, :, :]))
                else:
                    link(nc.vector.tensor_scalar(over[:, :], slot[:, 0, :], float(CAP), None, ALU.is_ge))
                    link(nc.vector.tensor_scalar(best[:, :], over[:, :], -1.0, 1.0, ALU.mult, ALU.add))
                    link(nc.vector.tensor_tensor(R["gate"][:, 0, :], top_p[:, 0, :], best[:, :], ALU.mult))
                    link(nc.vector.tensor_scalar(slot[:, 0, :], slot[:, 0, :], float(CAP - 1), None, ALU.min))
                    link(nc.vector.tensor_scalar(low[:, :], low[:, :], float(NE), float(T1E), ALU.add, ALU.mult))
                    link(nc.vector.tensor_tensor(slot[:, 0, :], slot[:, 0, :], low[:, :], ALU.add))
                    link(nc.vector.tensor_copy(R["of"][:, 0, :], slot[:, 0, :]))
                    link(nc.vector.scalar_tensor_tensor(slot[:, 1, :], over[:, :], float(NE * T1E), slot[:, 0, :],
                                                        ALU.mult, ALU.add))
                    link(nc.vector.tensor_copy(R["to"][:, 0, :], slot[:, 1, :]))

            @block.scalar
            def _(act):
                act.wait_ge(chain, 2 + (bias_in is not None))
                nc.scalar.activation(prob[:, :, :], ex[:, :, :], ACT.Exp).then_inc(exped, 1)

            @block.tensor
            def _(pe):
                pe.wait_ge(hotted, 2)
                rhs = both[:, :, :].rearrange("p b e -> p (b e)")
                nc.tensor.matmul(p_pre[:, 0:NB * NE], K["after"][:, :], rhs, start=True, stop=True)
                nc.tensor.matmul(p_tot[:, 0:NB * NE], K["ones"][:, :], rhs, start=True, stop=True).then_inc(counted, 1)


def dispatch_stage(nc, K, tag, R, top, xl, rows, limit):
    with Scope(nc, tag) as s:
        x = s.sb("x", [P, 2, D], F32)
        idx = s.sb("idx", [P, 2, top], U32)
        x_in = [s.sem(f"x_in{h}") for h in range(2)]
        sent = [s.sem(f"sent{h}") for h in range(2)]
        idx_ready, pool_go = s.sem("idx_ready"), s.sem("pool_go")
        with nc.Block() as block:
            @block.sync
            def _(sp):
                def load(h, b, i, first):
                    if not first:
                        sp.wait_ge(sent[h], 16 * top * i)
                    sp.dma_start(x[:, h, :], xl[bass.ds(b * P, P), :]).then_inc(x_in[h], 16)
                in_pairs(sp, NB, load)

            @block.scalar
            def _(act):
                def copy(h, b, i, first):
                    if not first:
                        act.wait_ge(sent[h], 16 * top * i)
                    nc.scalar.copy(idx[:, h, :], R["to"][:, 0:top, bass.ds(b, 1)]
                                   .rearrange("p c a -> p (c a)")).then_inc(idx_ready, 1)
                in_pairs(act, NB, copy)

            @block.gpsimd
            def _(pool):
                def send(h, b, i, first, n=P):
                    pool.wait_ge(x_in[h], 16 * i + 16)
                    pool.sem_inc(pool_go, 1)
                    pool.wait_ge(idx_ready, b + 1)
                    pool.sem_inc(pool_go, 1)
                    for c in range(top):
                        nc.gpsimd.indirect_dma_start(
                            out=rows, out_offset=bass.IndirectOffsetOnAxis(ap=idx[0:n, h, c:c + 1], axis=0),
                            in_=x[0:n, h, :], in_offset=None, bounds_check=limit - 1,
                            oob_is_err=False).then_inc(sent[h], 16)
                in_pairs(pool, NB - 1, send)
                send(0, NB - 1, NB // 2, False, LAST)
                for h in range(2):
                    pool.wait_ge(sent[h], 16 * top * waits_of_half(NB, h))


def combine_stage(nc, K, tag, X, R, top, rows, out=None):
    with Scope(nc, tag) as s:
        y = s.sb("y", [P, 2, top, D], F32)
        idx = s.sb("idx", [P, 2, top], U32)
        yw = s.sb("yw", [P, D], F32)
        flag = s.sb("flag", [P, 3, D], I32)
        fixed = s.sb("fixed", [P, 3, D], F32)
        got = [s.sem(f"got{h}") for h in range(2)]
        idx_ready, pool_go, used, chain = s.sem("idx_ready"), s.sem("pool_go"), s.sem("used"), s.sem("chain")
        stored, fixes = s.sem("stored"), s.sem("fixes")
        with nc.Block() as block:
            @block.scalar
            def _(act):
                def copy(h, b, i, first):
                    if not first:
                        act.wait_ge(got[h], 16 * top * i)
                    nc.scalar.copy(idx[:, h, :], R["of"][:, 0:top, bass.ds(b, 1)]
                                   .rearrange("p c a -> p (c a)")).then_inc(idx_ready, 1)
                in_pairs(act, NB, copy)

            @block.gpsimd
            def _(pool):
                def fetch(h, b, i, first):
                    pool.wait_ge(idx_ready, b + 1)
                    pool.sem_inc(pool_go, 1)
                    if not first:
                        pool.wait_ge(used, b - 1)
                        pool.sem_inc(pool_go, 1)
                    for c in range(top):
                        nc.gpsimd.indirect_dma_start(
                            out=y[:, h, c, :], out_offset=None, in_=rows,
                            in_offset=bass.IndirectOffsetOnAxis(ap=idx[:, h, c:c + 1], axis=0)).then_inc(got[h], 16)
                in_pairs(pool, NB, fetch)

            @block.vector
            def _(dve):
                if out is not None:
                    for c, v in enumerate((0.0, 1e4, -1e4)):
                        nc.vector.memset(fixed[:, c, :], v).then_inc(fixes, 1)
                    dve.wait_ge(fixes, 3)
                STEPS = 8 if out is not None else 2

                def add(h, b, i, first):
                    xb = X[:, bass.ds(b, 1), :].rearrange("p a d -> p (a d)")
                    dve.wait_ge(got[h], 16 * top * i + 16 * top)
                    c = b * STEPS
                    if out is None:
                        nc.vector.scalar_tensor_tensor(xb, y[:, h, 0, :], R["gate"][:, 0, bass.ds(b, 1)], xb,
                                                       ALU.mult, ALU.add).then_inc(chain, 1)
                        dve.wait_ge(chain, c + 1)
                        nc.vector.scalar_tensor_tensor(xb, y[:, h, 1, :], R["gate"][:, 1, bass.ds(b, 1)], xb,
                                                       ALU.mult, ALU.add).then_inc(chain, 1)
                        dve.wait_ge(chain, c + 2)
                        dve.sem_inc(used, 1)
                        return
                    nc.vector.tensor_scalar(yw[:, :], y[:, h, 0, :], R["gate"][:, 0, bass.ds(b, 1)], None,
                                            ALU.mult).then_inc(chain, 1)
                    dve.wait_ge(chain, c + 1)
                    nc.vector.tensor_tensor(flag[:, 0, :], yw[:, :], yw[:, :], ALU.not_equal).then_inc(chain, 1)
                    nc.vector.tensor_scalar(flag[:, 1, :], yw[:, :], float("inf"), None, ALU.is_equal).then_inc(chain, 1)
                    nc.vector.tensor_scalar(flag[:, 2, :], yw[:, :], float("-inf"), None, ALU.is_equal).then_inc(chain, 1)
                    dve.wait_ge(chain, c + 4)
                    dve.sem_inc(fixes, 1)
                    for m in range(3):
                        nc.vector.copy_predicated(yw[:, :], flag[:, m, :], fixed[:, m, :]).then_inc(chain, 1)
                        dve.wait_ge(chain, c + 5 + m)
                        dve.sem_inc(fixes, 1)
                    nc.vector.tensor_tensor(xb, xb, yw[:, :], ALU.add).then_inc(chain, 1)
                    dve.wait_ge(chain, c + 8)
                    dve.sem_inc(used, 1)
                in_pairs(dve, NB, add)

            @block.sync
            def _(sp):
                if out is not None:
                    with sp.Fori(0, NB - 1) as b:
                        sp.wait_ge(used, b + 1)
                        sp.dma_start(out[bass.ds(b * P, P), :],
                                     X[:, bass.ds(b, 1), :].rearrange("p a d -> p (a d)")).then_inc(stored, 16)
                    sp.wait_ge(used, NB)
                    sp.dma_start(out[(NB - 1) * P:N, :], X[0:LAST, NB - 1, :]).then_inc(stored, 16)
                    sp.wait_ge(stored, 16 * NB)


def experts0_stage(nc, K, tag, R, w13_in, w2_in, rows, out_rows):
    HW = H0 // 2
    KH = -(-H0 // P)
    KL = H0 - (KH - 1) * P
    with Scope(nc, tag) as s:
        w13 = s.sb("w13", [P, DH, NE * 2 * H0], F32)
        w2 = s.sb("w2", [P, KH, NE * D], F32)
        x = s.sb("x", [P, 2, D], F32)
        xT = s.sb("xT", [P, 2, DH, P], F32)
        sg = s.sb("sg", [P, H0], F32)
        hid = s.sb("hid", [P, KH * P], F32)
        hT = s.sb("hT", [P, KH, P], F32)
        y = s.sb("y", [P, 2, D], F32)
        p_h = s.ps("p_h", [P, 2, 2, 512])
        p_x = s.ps("p_x", [P, 512])
        p_hT = s.ps("p_hT", [P, 2, 512])
        p_y = s.ps("p_y", [P, 512])
        loaded, xturned, xT_ready = s.sem("loaded"), s.sem("xturned"), s.sem("xT_ready")
        x_in = [s.sem(f"x_in{h}") for h in range(2)]
        y_stored = [s.sem(f"y_stored{h}") for h in range(2)]
        h_mm, silud, h_ready = s.sem("h_mm"), s.sem("silud"), s.sem("h_ready")
        hturned, hT_a, hT_b = s.sem("hturned"), s.sem("hT_a"), s.sem("hT_b")
        y_mm, y_ready = s.sem("y_mm"), s.sem("y_ready")
        cleared = s.sem("cleared")
        with nc.Block() as block:
            @block.sync
            def _(sp):
                for e in range(0, NE, 2):
                    sp.dma_start(w13[:, :, e * 2 * H0:(e + 2) * 2 * H0],
                                 w13_in[:, e * 2 * H0:(e + 2) * 2 * H0].rearrange("(k p) n -> p k n", p=P)).then_inc(loaded, 16)
                sp.dma_start(w2[:, 0:KH - 1, :], w2_in[0:(KH - 1) * P, :].rearrange("(k p) n -> p k n", p=P)).then_inc(loaded, 16)
                sp.dma_start(w2[0:KL, KH - 1, :], w2_in[(KH - 1) * P:H0, :]).then_inc(loaded, 16)

                def load(h, t, i, first):
                    if not first:
                        sp.wait_ge(xturned, t - 1)
                    sp.dma_start(x[:, h, :], rows[bass.ds(t * P, P), :]).then_inc(x_in[h], 16)
                in_pairs(sp, T0, load)

            @block.tensor
            def _(pe):
                def x_turn(h, t, i, first):
                    pe.wait_ge(x_in[h], 16 * i + 16)
                    if not (first and h == 0):
                        pe.wait_ge(xT_ready, t)
                    for k in range(DH):
                        last = nc.tensor.transpose(p_x[:, k * P:(k + 1) * P], x[:, h, k * P:(k + 1) * P],
                                                   K["ident"][:, :])
                    last.then_inc(xturned, 1)

                def up(h, t, e, first):
                    pe.wait_ge(xT_ready, t + 1)
                    for c in range(2):
                        if not first:
                            pe.wait_ge(h_ready, 2 * t - 2 + c + 1)
                        for m in range(2):
                            for k in range(DH):
                                last = nc.tensor.matmul(p_h[:, c, m, 0:HW], xT[:, h, k],
                                                        w13[:, k, bass.ds(e * (2 * H0) + (m * H0 + c * HW), HW)],
                                                        start=(k == 0), stop=(k == DH - 1))
                        last.then_inc(h_mm, 1)

                def down(t, e, first):
                    pe.wait_ge(h_ready, 2 * t + 2)
                    if not first:
                        pe.wait_ge(hT_a, t)
                        pe.wait_ge(hT_b, t)
                    for k in range(KH):
                        r = P if k < KH - 1 else KL
                        last = nc.tensor.transpose(p_hT[0:r, k // 4, (k % 4) * P:(k % 4 + 1) * P],
                                                   hid[:, k * P:k * P + r], K["ident"][:, :])
                        if k in (3, KH - 1):
                            last.then_inc(hturned, 1)
                    if not first:
                        pe.wait_ge(y_ready, t)
                    for k in range(KH):
                        if k == 0:
                            pe.wait_ge(hT_a, t + 1)
                        if k == 4:
                            pe.wait_ge(hT_b, t + 1)
                        r = P if k < KH - 1 else KL
                        last = nc.tensor.matmul(p_y[:, 0:D], hT[0:r, k], w2[0:r, k, bass.ds(e * D, D)],
                                                start=(k == 0), stop=(k == KH - 1))
                    last.then_inc(y_mm, 1)

                def experts(t, n):
                    return nc.values_load_multi_w_load_instructions(
                        R["tile_expert"][0:1, bass.ds(t, n)], engines=[PE_ENGINE], min_val=0, max_val=NE - 1,
                        skip_runtime_bounds_check_because="a count of at most NE - 1 experts")[1]

                pe.wait_ge(loaded, 16 * (NE // 2 + 2))
                e = experts(0, 2)
                x_turn(0, 0, 0, True)
                x_turn(1, 1, 0, True)
                up(0, 0, e[0], True)
                down(0, e[0], True)
                with pe.Fori(1, T0 // 2) as i:
                    e = experts(2 * i - 1, 2)
                    x_turn(0, 2 * i, i, False)
                    up(1, 2 * i - 1, e[0], False)
                    down(2 * i - 1, e[0], False)
                    x_turn(1, 2 * i + 1, i, False)
                    up(0, 2 * i, e[1], False)
                    down(2 * i, e[1], False)
                e = experts(T0 - 1, 1)
                up(1, T0 - 1, e[0], False)
                down(T0 - 1, e[0], False)

            @block.scalar
            def _(act):
                def take_x(h, t, first):
                    act.wait_ge(xturned, t + 1)
                    if not first:
                        act.wait_ge(h_mm, 2 * (t - 1))
                    nc.scalar.copy(xT[:, h], p_x[:, 0:D].rearrange("p (k v) -> p k v", k=DH)).then_inc(xT_ready, 1)

                def silu(t, first):
                    for c in range(2):
                        act.wait_ge(h_mm, 2 * t + c + 1)
                        if not first:
                            act.wait_ge(h_ready, 2 * t - 2 + c + 1)
                        nc.scalar.activation(sg[:, c * HW:(c + 1) * HW], p_h[:, c, 0, 0:HW], ACT.Silu).then_inc(silud, 1)
                    act.wait_ge(hturned, 2 * t + 1)
                    if not first:
                        act.wait_ge(y_mm, t)
                    nc.scalar.copy(hT[:, 0:4], p_hT[:, 0, :].rearrange("p (k v) -> p k v", k=4)).then_inc(hT_a, 1)

                take_x(0, 0, True)
                take_x(1, 1, True)
                silu(0, True)
                with act.Fori(1, T0 // 2) as i:
                    take_x(0, 2 * i, False)
                    silu(2 * i - 1, False)
                    take_x(1, 2 * i + 1, False)
                    silu(2 * i, False)
                silu(T0 - 1, False)

            @block.vector
            def _(dve):
                def step(h, t, i, first):
                    first_of_all = first and h == 0
                    for c in range(2):
                        dve.wait_ge(silud, 2 * t + c + 1)
                        if not first_of_all:
                            dve.wait_ge(hturned, 2 * t)
                        nc.vector.tensor_tensor(hid[:, c * HW:(c + 1) * HW], sg[:, c * HW:(c + 1) * HW],
                                                p_h[:, c, 1, 0:HW], ALU.mult).then_inc(h_ready, 1)
                    dve.wait_ge(hturned, 2 * t + 2)
                    if not first_of_all:
                        dve.wait_ge(y_mm, t)
                    nc.vector.tensor_copy(hT[:, 4], p_hT[:, 1, 0:P]).then_inc(cleared, 1)
                    nc.vector.tensor_copy(hT[0:KL, 5], p_hT[0:KL, 1, P:2 * P]).then_inc(hT_b, 1)
                    dve.wait_ge(y_mm, t + 1)
                    if not first:
                        dve.wait_ge(y_stored[h], 16 * i)
                    nc.vector.tensor_copy(y[:, h, :], p_y[:, 0:D]).then_inc(y_ready, 1)
                in_pairs(dve, T0, step)

            @block.gpsimd
            def _(pool):
                def store(h, t, i, first):
                    pool.wait_ge(y_ready, t + 1)
                    pool.sem_inc(cleared, 1)
                    nc.gpsimd.dma_start(out_rows[bass.ds(t * P, P), :], y[:, h, :]).then_inc(y_stored[h], 16)
                in_pairs(pool, T0, store)
                for h in range(2):
                    pool.wait_ge(y_stored[h], 16 * waits_of_half(T0, h))


def experts1_stage(nc, K, tag, w1_in, b1_in, w2_in, b2_in, rows, out_rows):
    MF = F1 // P
    TT = T1E // P
    TC = CH // P
    NCH = T1E // CH
    with Scope(nc, tag) as s:
        w1 = s.sb("w1", [P, 2, DH, F1], F32)
        w2 = s.sb("w2", [P, 2, MF, D], F32)
        b1 = s.sb("b1", [P, 2, MF], F32)
        b2 = s.sb("b2", [P, 2, D], F32)
        x = s.sb("x", [P, 2, TT, D], F32)
        xT = s.sb("xT", [P, DH, T1E], F32)
        hid = s.sb("hid", [P, MF, CH], F32)
        y = s.sb("y", [P, 2, D], F32)
        p_x = s.ps("p_x", [P, 2, 512])
        p_h = s.ps("p_h", [P, 4, 512])
        p_y = s.ps("p_y", [P, 2, 512])
        e_in = [s.sem(f"e_in{h}") for h in range(2)]
        y_stored = [s.sem(f"y_stored{h}") for h in range(2)]
        xturned, xT_ready, h_mm, h_ready = s.sem("xturned"), s.sem("xT_ready"), s.sem("h_mm"), s.sem("h_ready")
        y_mm, y_ready, pool_go = s.sem("y_mm"), s.sem("y_ready"), s.sem("pool_go")
        XP = NCH * DH
        HP = NCH * MF
        LOADS = 5

        def per_expert(eng, body):
            body(0, 0, 0, True)
            body(1, 1, 0, False)
            with eng.Fori(1, NE // 2) as i:
                for h in range(2):
                    body(h, 2 * i + h, i, False)

        with nc.Block() as block:
            @block.sync
            def _(sp):
                def load(h, e, i, first):
                    sp.wait_ge(y_mm, TT * (e - 1))
                    sp.wait_ge(y_ready, TT * (e - 1))
                    fetch(h, e)

                def fetch(h, e):
                    sp.dma_start(x[:, h], rows[bass.ds(e * T1E, T1E), :].rearrange("(t p) d -> p t d", p=P)).then_inc(e_in[h], 16)
                    sp.dma_start(w1[:, h], w1_in[bass.ds(e * D, D), :].rearrange("(k p) f -> p k f", p=P)).then_inc(e_in[h], 16)
                    sp.dma_start(b1[:, h], b1_in[bass.ds(e * P, P), :]).then_inc(e_in[h], 16)
                    sp.dma_start(w2[:, h], w2_in[bass.ds(e * F1, F1), :].rearrange("(m p) d -> p m d", p=P)).then_inc(e_in[h], 16)
                    sp.dma_start(b2[:, h], b2_in[bass.ds(e * D, D)].partition_broadcast(P)).then_inc(e_in[h], 16)
                fetch(0, 0)
                fetch(1, 1)
                with sp.Fori(1, NE // 2) as i:
                    for h in range(2):
                        load(h, 2 * i + h, i, False)

            @block.tensor
            def _(pe):
                def expert(h, e, i, first):
                    pe.wait_ge(e_in[h], 16 * LOADS * i + 16 * LOADS)
                    for c in range(NCH):
                        for k in range(DH):
                            j = c * DH + k
                            if not (first and j < 2):
                                pe.wait_ge(xT_ready, e * XP + j - 1)
                            for t in range(TC):
                                last = nc.tensor.transpose(p_x[:, j % 2, t * P:(t + 1) * P],
                                                           x[:, h, c * TC + t, k * P:(k + 1) * P], K["ident"][:, :])
                            last.then_inc(xturned, 1)
                    for c in range(NCH):
                        pe.wait_ge(xT_ready, e * XP + (c + 1) * DH)
                        for m in range(MF):
                            j = c * MF + m
                            if not (first and j < 4):
                                pe.wait_ge(h_ready, e * HP + j - 3)
                            for k in range(DH):
                                last = nc.tensor.matmul(p_h[:, m % 4, :], w1[:, h, k, m * P:(m + 1) * P],
                                                        xT[:, k, c * CH:(c + 1) * CH],
                                                        start=(k == 0), stop=(k == DH - 1))
                            last.then_inc(h_mm, 1)
                        for t in range(TC):
                            j = c * TC + t
                            if not (first and j < 2):
                                pe.wait_ge(y_ready, e * TT + j - 1)
                            for m in range(MF):
                                if t == 0:
                                    pe.wait_ge(h_ready, e * HP + c * MF + m + 1)
                                last = nc.tensor.matmul(p_y[:, j % 2, 0:D], hid[:, m, t * P:(t + 1) * P],
                                                        w2[:, h, m, :], start=(m == 0), stop=(m == MF - 1))
                            last.then_inc(y_mm, 1)
                per_expert(pe, expert)

            @block.scalar
            def _(act):
                def expert(h, e, i, first):
                    act.wait_ge(e_in[h], 16 * LOADS * i + 16 * LOADS)
                    for c in range(NCH):
                        for m in range(MF):
                            act.wait_ge(h_mm, e * HP + c * MF + m + 1)
                            if not (first and c == 0):
                                act.wait_ge(y_mm, e * TT + c * TC)
                            nc.scalar.activation(hid[:, m, :], p_h[:, m % 4, :], ACT.Relu,
                                                 bias=b1[:, h, m:m + 1]).then_inc(h_ready, 1)
                per_expert(act, expert)

            @block.vector
            def _(dve):
                def expert(h, e, i, first):
                    dve.wait_ge(e_in[h], 16 * LOADS * i + 16 * LOADS)
                    for c in range(NCH):
                        for k in range(DH):
                            dve.wait_ge(xturned, e * XP + c * DH + k + 1)
                            if not first:
                                dve.wait_ge(h_mm, e * HP)
                            nc.vector.tensor_copy(xT[:, k, c * CH:(c + 1) * CH],
                                                  p_x[:, (c * DH + k) % 2, :]).then_inc(xT_ready, 1)
                    for j in range(TT):
                        dve.wait_ge(y_mm, e * TT + j + 1)
                        if not (first and j < 2):
                            dve.wait_ge(y_stored[j % 2], 16 * (e * (TT // 2) + j // 2))
                        nc.vector.tensor_tensor(y[:, j % 2, :], p_y[:, j % 2, 0:D], b2[:, h, :],
                                                ALU.add).then_inc(y_ready, 1)
                per_expert(dve, expert)

            @block.gpsimd
            def _(pool):
                with pool.Fori(0, NE * TT // 2) as i:
                    for h in range(2):
                        pool.wait_ge(y_ready, 2 * i + h + 1)
                        pool.sem_inc(pool_go, 1)
                        nc.gpsimd.dma_start(out_rows[bass.ds((2 * i + h) * P, P), :], y[:, h, :]).then_inc(y_stored[h], 16)
                for h in range(2):
                    pool.wait_ge(y_stored[h], 16 * NE * TT // 2)


def make_constants(nc, ctx):
    K = {}
    for name, shape, dt in (("ones", [P, P], F32), ("iota", [P, P], F32), ("iota_b", [P, P], BF16),
                            ("part", [P, 1], F32), ("ident", [P, P], F32), ("before", [P, P], F32),
                            ("after", [P, P], F32), ("first", [P, 2, NB], F32), ("nloop", [P, NB], F32),
                            ("dis", [P, NB], F32), ("zero", [P, DH, P], F32), ("ndis", [P, NB], F32)):
        K[name] = ctx.enter_context(nc.sbuf_tensor(f"k_{name}", shape, dt))
    return K


def bass_gnn_ffn_kernel(nc, x, dst_p, src_p, dst_r, src_r, eps, m_w1, m_b1, m_w2, m_b2, gamma, beta,
                        router, w13, w2e, cheb_w, cheb_b, gate_w, gate_b, f_w1, f_b1, f_w2, f_b2, out):
    def dram(name, shape, dt=F32):
        return nc.dram_tensor(name, shape, dt, kind="Internal").ap()

    rows = dram("edge_rows", [2, 2, EP])
    by_dst = dram("by_dst", [P * ET, 2], I32)
    by_src = dram("by_src", [P * ET, 2], I32)
    table = dram("table", [NP, D])
    terms = [dram(f"term{k}", [NP, D]) for k in range(3)]
    xl = dram("xl", [NP, D])
    in0, out0 = dram("in0", [T0 * P, D]), dram("out0", [T0 * P, D])
    in1, out1 = dram("in1", [NE * T1E, D]), dram("out1", [NE * T1E, D])
    with ExitStack() as ctx:
        def sb(name, shape, dt=F32):
            return ctx.enter_context(nc.sbuf_tensor(name, shape, dt))

        K = make_constants(nc, ctx)
        X = sb("X", [P, NB, D])
        R = {"gate": sb("r_gate", [P, 2, NB]), "to": sb("r_to", [P, 2, NB], I32),
             "of": sb("r_of", [P, 2, NB], I32), "tile_expert": sb("r_tile_expert", [P, P], I32)}
        logits = sb("logits", [P, NB, NE])
        constants_stage(nc, K)

        with nc.sbuf_tensor("acc_a", [P, DH, ACC_W], F32) as acc:
            clear_stage(nc, "clr", [in0, in1], acc)
            counts_stage(nc, K, dst_p, src_p, dst_r, src_r, rows)
            sort_stage(nc, K, "sd", 0, dst_p, src_p, rows, by_dst)
            sort_stage(nc, K, "ss", 1, src_p, dst_p, rows, by_src)
            norm_stage(nc, K, "n0", X, x_in=x, xl_out=table, turned=(acc, eps))
            spread_stage(nc, K, "s0", by_dst, table, acc)
            network0_stage(nc, K, "m0", X, acc, m_w1, m_b1, m_w2, m_b2, gamma, beta)

        norm_stage(nc, K, "n1", X, xl_out=xl, proj=(router, logits))
        route_stage(nc, K, "r0", logits, R, 2)
        dispatch_stage(nc, K, "d0", R, 2, xl, in0, T0 * P)
        experts0_stage(nc, K, "e0", R, w13, w2e, in0, out0)
        combine_stage(nc, K, "c0", X, R, 2, out0)

        with nc.sbuf_tensor("acc_b", [P, DH, ACC_W], F32) as acc, nc.sbuf_tensor("cheb", [P, NB, D], F32) as cheb:
            clear_stage(nc, "clr2", [], acc)
            norm_stage(nc, K, "n2", X, xl_out=terms[0], scaled_out=table, proj=(cheb_w[0:D, :], cheb))
            for k in range(1, 4):
                spread_stage(nc, K, f"s{k}", by_src, table, acc)
                laplace_stage(nc, K, f"l{k}", X, acc, cheb, k, cheb_w[k * D:(k + 1) * D, :], terms[k - 1],
                              terms[k - 2] if k > 1 else None, terms[k] if k < 3 else None, table, cheb_b)

        norm_stage(nc, K, "n3", X, xl_out=xl, proj=(gate_w, logits))
        route_stage(nc, K, "r1", logits, R, 1, gate_b)
        dispatch_stage(nc, K, "d1", R, 1, xl, in1, NE * T1E)
        experts1_stage(nc, K, "e1", f_w1, f_b1, f_w2, f_b2, in1, out1)
        combine_stage(nc, K, "c1", X, R, 1, out1, out=out)


def kernel(**inputs):
    import concourse.bacc as bacc
    from concourse.bass_utils import run_bass_kernel_spmd

    a = {k: np.asarray(v) for k, v in inputs.items()}
    loop = np.arange(N, dtype=np.int32)
    pad = np.full(EP - E_ALL, PAD_KEY, np.int32)
    src = np.concatenate([a["src"], loop, pad])
    dst = np.concatenate([a["dst"], loop, pad])
    tiles = lambda v: np.ascontiguousarray(v.reshape(ET, P).T)
    arrays = {
        "x": a["x"], "dst_p": tiles(dst), "src_p": tiles(src),
        "dst_r": dst.reshape(P, ET), "src_r": src.reshape(P, ET),
        "eps": a["L0_gnn_eps"], "m_w1": a["L0_gnn_W1"], "m_b1": a["L0_gnn_b1"], "m_w2": a["L0_gnn_W2"],
        "m_b2": a["L0_gnn_b2"], "gamma": a["L0_gnn_gamma"], "beta": a["L0_gnn_beta"],
        "router": a["L0_ffn_router_w"].T,
        "w13": np.concatenate([a["L0_ffn_w1"], a["L0_ffn_w3"]], 1).transpose(2, 0, 1).reshape(D, NE * 2 * H0),
        "w2e": a["L0_ffn_w2"].transpose(2, 0, 1).reshape(H0, NE * D),
        "cheb_w": a["L1_gnn_weight"].reshape(4 * D, D), "cheb_b": a["L1_gnn_bias"],
        "gate_w": a["L1_ffn_gate_w"], "gate_b": a["L1_ffn_gate_b"],
        "f_w1": a["L1_ffn_w1"].reshape(NE * D, F1),
        "f_b1": a["L1_ffn_b1"].reshape(NE, F1 // P, P).transpose(0, 2, 1).reshape(NE * P, F1 // P),
        "f_w2": a["L1_ffn_w2"].reshape(NE * F1, D), "f_b2": a["L1_ffn_b2"].reshape(NE * D),
    }
    arrays = {k: np.ascontiguousarray(v) for k, v in arrays.items()}
    nc = bacc.Bacc("TRN2", target_bir_lowering=False, num_devices=1)
    args = [nc.dram_tensor(f"in_{k}", v.shape, mybir.dt.from_np(v.dtype), kind="ExternalInput").ap()
            for k, v in arrays.items()]
    args.append(nc.dram_tensor("out_x", (N, D), F32, kind="ExternalOutput").ap())
    bass_gnn_ffn_kernel(nc, *args)
    r = run_bass_kernel_spmd(nc, [{f"in_{k}": v for k, v in arrays.items()}], core_ids=[0])
    return r.results[0]["out_x"]
```

```python
import numpy as np
from contextlib import ExitStack

import concourse.bass as bass
from concourse import mybir
from concourse.alu_op_type import AluOpType as ALU

F32 = mybir.dt.float32
BF16 = mybir.dt.bfloat16
I32 = mybir.dt.int32
U32 = mybir.dt.uint32
ACT = mybir.ActivationFunctionType
AX = mybir.AxisListType
DVE_ENGINE = mybir.EngineType.DVE
PE_ENGINE = mybir.EngineType.PE

P = 128
N = 6250
D = 256
DH = D // P
NB = -(-N // P)
NP = NB * P
LAST = N - (NB - 1) * P
E_IN = 106250
G = 8
ET_IN = -(-E_IN // P)
ET = -(-(ET_IN + NB) // (2 * G)) * 2 * G
EP = ET * P
NG = ET // G
PAD_KEY = NP - 1
ACC_W = NP + P
HID = 512
NE = 8
H0 = 682
F1 = 1024
CAP = -(-125 * N // (100 * NE))
LN_EPS = 1e-5
RB = 4
CH = 512
CHUNKS = [(c, min(CH, NP - c)) for c in range(0, NP, CH)]


class Scope:

    def __init__(self, nc, tag):
        self.nc, self.tag, self.ctx, self.sems = nc, tag, ExitStack(), []

    def __enter__(self):
        self.ctx.__enter__()
        return self

    def __exit__(self, *a):
        self.nc.clear_and_free_semaphores(self.sems)
        self.nc.all_engine_barrier()
        return self.ctx.__exit__(*a)

    def sb(self, name, shape, dt):
        return self.ctx.enter_context(self.nc.sbuf_tensor(f"{self.tag}_{name}", shape, dt))

    def ps(self, name, shape, dt=F32):
        return self.ctx.enter_context(self.nc.psum_tensor(f"{self.tag}_{name}", shape, dt))

    def sem(self, name):
        self.sems.append(self.nc.alloc_semaphore(name=f"{self.tag}_{name}"))
        return self.sems[-1]


def bc_mid(ap, n):
    return ap.unsqueeze(1).to_broadcast([ap.shape[0], n, ap.shape[1]])


def bc_last(ap, n):
    return ap.unsqueeze(2).to_broadcast([ap.shape[0], ap.shape[1], n])


def constants_stage(nc, K):
    with Scope(nc, "cst") as s:
        made = s.sem("made")
        floats = s.sem("floats")
        iota_i = s.sb("iota_i", [P, P], I32)
        part_i = s.sb("part_i", [P, 1], I32)
        zeroed = s.sem("zeroed")
        with nc.Block() as block:
            @block.gpsimd
            def _(pool):
                nc.gpsimd.iota(iota_i[:, :], pattern=[[1, P]], base=0, channel_multiplier=0).then_inc(made, 1)
                nc.gpsimd.iota(part_i[:, :], pattern=[[0, 1]], base=0, channel_multiplier=1).then_inc(made, 1)

            @block.vector
            def _(dve):
                nc.vector.memset(K["ones"][:, :], 1.0).then_inc(zeroed, 1)
                nc.vector.memset(K["zero"][:, :, :], 0.0).then_inc(zeroed, 1)
                dve.wait_ge(made, 2)
                nc.vector.tensor_copy(K["iota"][:, :], iota_i[:, :]).then_inc(floats, 1)
                nc.vector.tensor_copy(K["iota_b"][:, :], iota_i[:, :]).then_inc(floats, 1)
                nc.vector.tensor_copy(K["part"][:, :], part_i[:, :]).then_inc(floats, 1)
                dve.wait_ge(floats, 3)
                nc.vector.tensor_scalar(K["ident"][:, :], K["iota"][:, :], K["part"][:, 0:1], None,
                                        ALU.is_equal).then_inc(floats, 1)
                nc.vector.tensor_scalar(K["before"][:, :], K["iota"][:, :], K["part"][:, 0:1], None,
                                        ALU.is_lt).then_inc(floats, 1)
                nc.vector.tensor_scalar(K["after"][:, :], K["iota"][:, :], K["part"][:, 0:1], None,
                                        ALU.is_gt).then_inc(floats, 1)


def ends_stage(nc, K, dst_p, src_p, dst_r, src_r, rows, by_dst, R):
    with Scope(nc, "end") as s:
        ends = s.sb("ends", [P, 2, ET], I32)
        pairs = s.sb("pairs", [P, ET, 2], I32)
        row_i = s.sb("row_i", [P, 2, ET], I32)
        row_f = s.sb("row_f", [P, 2, ET], F32)
        rlo_i = s.sb("rlo_i", [P, 2, ET], I32)
        rlo_f = s.sb("rlo_f", [P, 2, ET], F32)
        key_f = s.sb("key_f", [P, ET], F32)
        col = s.sb("col", [P, ET], F32)
        real = s.sb("real", [P, ET], F32)
        high = s.sb("high", [P, ET], F32)
        low = s.sb("low", [P, ET], F32)
        bad = s.sb("bad", [P, 1], F32)
        p_start = s.ps("p_start", [P, 2, 512])
        p_bad = s.ps("p_bad", [P, 1])
        loaded, rows_out, rows_ready, paired = (s.sem(n) for n in ("loaded", "rows_out", "rows_ready", "paired"))
        prep, started, col_ready, chain, summed = (s.sem(n) for n in ("prep", "started", "col_ready", "chain", "summed"))
        pieces = [(c, min(512, ET - c)) for c in range(0, ET, 512)]
        with nc.Block() as block:
            @block.sync
            def _(sp):
                sp.dma_start(ends[:, 0, :], dst_p).then_inc(loaded, 16)
                sp.dma_start(ends[:, 1, :], src_p).then_inc(loaded, 16)
                sp.dma_start(row_i[:, 0, :], dst_r).then_inc(loaded, 16)
                sp.dma_start(row_i[:, 1, :], src_r).then_inc(loaded, 16)
                sp.wait_ge(paired, 2)
                sp.dma_start(by_dst.rearrange("(p t) k -> p t k", p=P), pairs[:, :, :]).then_inc(rows_out, 16)
                sp.wait_ge(rows_ready, 2)
                for k in range(2):
                    sp.dma_start(rows[k, 0].rearrange("(p t) -> p t", p=P), row_f[:, k, :]).then_inc(rows_out, 16)
                    sp.dma_start(rows[k, 1].rearrange("(p t) -> p t", p=P), rlo_f[:, k, :]).then_inc(rows_out, 16)
                sp.wait_ge(rows_out, 80)

            @block.scalar
            def _(act):
                act.wait_ge(loaded, 64)
                for k in range(2):
                    nc.scalar.copy(pairs[:, :, k], ends[:, k, :]).then_inc(paired, 1)
                nc.scalar.copy(row_f[:, :, :], row_i[:, :, :]).then_inc(rows_ready, 1)

            @block.tensor
            def _(pe):
                pe.wait_ge(prep, 1)
                for n, (c, w) in enumerate(pieces):
                    nc.tensor.matmul(p_start[:, n, 0:w], K["ones"][0:1, :], key_f[0:1, c:c + w],
                                     start=True, stop=True).then_inc(started, 1)
                pe.wait_ge(chain, 6)
                nc.tensor.matmul(p_bad[:, :], K["ones"][:, :], bad[:, :], start=True, stop=True).then_inc(summed, 1)

            @block.vector
            def _(dve):
                dve.wait_ge(loaded, 64)
                nc.vector.tensor_copy(key_f[:, :], ends[:, 0, :]).then_inc(prep, 1)
                nc.vector.tensor_scalar(rlo_i[:, :, :], row_i[:, :, :], P - 1, None,
                                        ALU.bitwise_and).then_inc(prep, 1)
                dve.wait_ge(prep, 2)
                nc.vector.tensor_copy(rlo_f[:, :, :], rlo_i[:, :, :]).then_inc(rows_ready, 1)
                for n, (c, w) in enumerate(pieces):
                    dve.wait_ge(started, n + 1)
                    nc.vector.tensor_tensor(col[:, c:c + w], key_f[:, c:c + w], p_start[:, n, 0:w],
                                            ALU.subtract).then_inc(col_ready, 1)
                dve.wait_ge(col_ready, len(pieces))
                nc.vector.tensor_scalar(real[:, :], key_f[:, :], float(PAD_KEY), None, ALU.is_lt).then_inc(chain, 1)
                nc.vector.tensor_scalar(high[:, :], col[:, :], float(P), None, ALU.is_ge).then_inc(chain, 1)
                dve.wait_ge(chain, 2)
                nc.vector.tensor_tensor(high[:, :], high[:, :], real[:, :], ALU.mult).then_inc(chain, 1)
                nc.vector.tensor_scalar(low[:, :], col[:, :], 0.0, None, ALU.is_lt).then_inc(chain, 1)
                dve.wait_ge(chain, 4)
                nc.vector.tensor_tensor(high[:, :], high[:, :], low[:, :], ALU.add).then_inc(chain, 1)
                dve.wait_ge(chain, 5)
                nc.vector.tensor_reduce(bad[:, :], high[:, :], AX.X, ALU.max).then_inc(chain, 1)
                dve.wait_ge(summed, 1)
                nc.vector.tensor_scalar(R["unsorted"][:, :], p_bad[:, :], 1.0, None, ALU.min).then_inc(chain, 1)
                dve.wait_ge(chain, 7)


def unsorted_only(eng, R, body):
    flag = eng.value_load(R["unsorted"][0:1, 0:1], min_val=0, max_val=1)
    with eng.If(flag > 0):
        body()


def always(eng, R, body):
    body()


def counts_stage(nc, K, tag, which, key_p, other_p, R, when):
    deg = which == 1
    NH = 2 if deg else 1
    with Scope(nc, tag) as s:
        loaded = s.sem("loaded")
        ends = s.sb("ends", [P, 2, ET], I32)
        lo_i = s.sb("lo_i", [P, ET], I32)
        hi_i = s.sb("hi_i", [P, ET], I32)
        lo_b = s.sb("lo_b", [P, ET], BF16)
        hi_b = s.sb("hi_b", [P, 2, ET], BF16)
        same = s.sb("same", [P, ET], F32)
        oh_lo = s.sb("oh_lo", [P, 2, G, P], BF16)
        oh_hi = s.sb("oh_hi", [P, 2, 2, G, NB], BF16)
        total = s.sb("total", [P, 2, NB], F32)
        excl = s.sb("excl", [P, NB + 1], F32)
        rdeg = s.sb("rdeg", [P, NB], F32)
        degc = s.sb("degc", [P, NB], F32)
        p_cnt = s.ps("p_cnt", [P, 2, NB])
        p_pre = s.ps("p_pre", [P, NB])
        p_tot = s.ps("p_tot", [P, NB])
        bits, hots, hots_hi, counted = s.sem("bits"), s.sem("hots"), s.sem("hots_hi"), s.sem("counted")
        chain, cnt_done, pre_done, rooted = s.sem("chain"), s.sem("cnt_done"), s.sem("pre_done"), s.sem("rooted")
        with nc.Block() as block:
            @block.sync
            def _(sp):
                def body():
                    sp.dma_start(ends[:, 0, :], key_p).then_inc(loaded, 16)
                    sp.dma_start(ends[:, 1, :], other_p).then_inc(loaded, 16)
                when(sp, R, body)

            @block.vector
            def _(dve):
                def body():
                    dve.wait_ge(loaded, 32)
                    nc.vector.tensor_scalar(lo_i[:, :], ends[:, 0, :], P - 1, None, ALU.bitwise_and).then_inc(bits, 1)
                    nc.vector.tensor_scalar(hi_i[:, :], ends[:, 0, :], 7, None, ALU.arith_shift_right).then_inc(bits, 1)
                    nc.vector.tensor_tensor(same[:, :], ends[:, 0, :], ends[:, 1, :], ALU.not_equal).then_inc(bits, 1)
                    dve.wait_ge(bits, 3)
                    nc.vector.tensor_copy(lo_b[:, :], lo_i[:, :]).then_inc(bits, 1)
                    nc.vector.tensor_copy(hi_b[:, 0, :], hi_i[:, :]).then_inc(bits, 1)
                    nc.vector.scalar_tensor_tensor(hi_b[:, 1, :], same[:, :], 64.0, hi_i[:, :],
                                                   ALU.mult, ALU.add).then_inc(bits, 1)
                    dve.wait_ge(bits, 6)

                    def one_hots(h, q):
                        nc.vector.tensor_tensor(oh_lo[:, h], bc_mid(K["iota_b"][:, :], G),
                                                bc_last(lo_b[:, bass.ds(q * G, G)], P),
                                                ALU.is_equal).then_inc(hots, 1)
                        for k in range(NH):
                            nc.vector.tensor_tensor(oh_hi[:, h, k], bc_mid(K["iota_b"][:, 0:NB], G),
                                                    bc_last(hi_b[:, k, bass.ds(q * G, G)], NB),
                                                    ALU.is_equal).then_inc(hots_hi, 1)
                    for h in range(2):
                        one_hots(h, h)
                    with dve.Fori(1, NG // 2) as i:
                        for h in range(2):
                            dve.wait_ge(counted, 2 * i + h - 1)
                            one_hots(h, 2 * i + h)
                    dve.wait_ge(counted, NG)
                    nc.vector.tensor_copy(total[:, 0:NH, :], p_cnt[:, 0:NH, :]).then_inc(cnt_done, 1)
                    dve.wait_ge(cnt_done, 1)
                    nc.vector.memset(excl[:, 0:1], 0.0).then_inc(chain, 1)
                    nc.vector.tensor_scalar(degc[:, :], total[:, 0, :], 1.0, None, ALU.max).then_inc(cnt_done, 1)
                    dve.wait_ge(pre_done, 1)
                    for b in range(NB):
                        dve.wait_ge(chain, b + 1)
                        nc.vector.tensor_tensor(excl[:, b + 1:b + 2], excl[:, b:b + 1], p_tot[:, b:b + 1],
                                                ALU.add).then_inc(chain, 1)
                    dve.wait_ge(chain, NB + 1)
                    nc.vector.tensor_tensor(K["first"][:, which, :], excl[:, 0:NB], p_pre[:, :],
                                            ALU.add).then_inc(chain, 1)
                    if deg:
                        nc.vector.tensor_copy(K["nloop"][:, :], total[:, 1, :]).then_inc(cnt_done, 1)
                        dve.wait_ge(rooted, 1)
                        nc.vector.reciprocal(K["dis"][:, :], rdeg[:, :]).then_inc(chain, 1)
                        dve.wait_ge(chain, NB + 3)
                        nc.vector.tensor_tensor(rdeg[:, :], K["dis"][:, :], K["dis"][:, :], ALU.mult).then_inc(chain, 1)
                        dve.wait_ge(chain, NB + 4)
                        nc.vector.tensor_tensor(degc[:, :], rdeg[:, :], degc[:, :], ALU.mult).then_inc(chain, 1)
                        dve.wait_ge(chain, NB + 5)
                        nc.vector.tensor_scalar(rdeg[:, :], degc[:, :], -0.5, 1.5, ALU.mult, ALU.add).then_inc(chain, 1)
                        dve.wait_ge(chain, NB + 6)
                        nc.vector.tensor_tensor(K["dis"][:, :], rdeg[:, :], K["dis"][:, :], ALU.mult).then_inc(chain, 1)
                        dve.wait_ge(chain, NB + 7)
                        nc.vector.tensor_scalar(K["ndis"][:, :], K["dis"][:, :], -1.0, None, ALU.mult).then_inc(chain, 1)
                        dve.wait_ge(chain, NB + 8)
                    else:
                        dve.wait_ge(chain, NB + 2)
                when(dve, R, body)

            if deg:
                @block.scalar
                def _(act):
                    act.wait_ge(cnt_done, 2)
                    nc.scalar.activation(rdeg[:, :], degc[:, :], ACT.Sqrt).then_inc(rooted, 1)

            @block.tensor
            def _(pe):
                def count(h, start, stop):
                    for g in range(G):
                        last = nc.tensor.matmul(p_cnt[:, 0:NH, :], oh_lo[:, h, g], oh_hi[:, h, 0:NH, g],
                                                start=start and g == 0, stop=stop and g == G - 1)
                    last.then_inc(counted, 1)

                def body():
                    for h in range(2):
                        pe.wait_ge(hots, h + 1)
                        pe.wait_ge(hots_hi, NH * (h + 1))
                        count(h, h == 0, False)
                    with pe.Fori(1, NG // 2 - 1) as i:
                        for h in range(2):
                            pe.wait_ge(hots, 2 * i + h + 1)
                            pe.wait_ge(hots_hi, 2 * NH * i + NH * (h + 1))
                            count(h, False, False)
                    for h in range(2):
                        pe.wait_ge(hots, NG - 1 + h)
                        pe.wait_ge(hots_hi, NH * (NG - 1 + h))
                        count(h, False, h == 1)
                    pe.wait_ge(cnt_done, 1)
                    nc.tensor.matmul(p_pre[:, :], K["after"][:, :], total[:, 0, :], start=True, stop=True)
                    nc.tensor.matmul(p_tot[:, :], K["ones"][:, :], total[:, 0, :],
                                     start=True, stop=True).then_inc(pre_done, 1)
                when(pe, R, body)


def early(q, k):
    return isinstance(q, int) and q < k


def in_ring(eng, count, R, *steps):
    deep = max(lag for lag, _ in steps)
    head = -(-(R + deep) // R) * R
    turns = (count - head) // R

    def turn(n, k, i):
        for lag, body in steps:
            if isinstance(n, int) and not 0 <= n - lag < count:
                continue
            body((k - lag) % R, n - lag, i + (k - lag) // R)
    for n in range(head):
        turn(n, n % R, n // R)
    with eng.Fori(head // R, head // R + turns) as i:
        for k in range(R):
            turn(R * i + k, k, i)
    for n in range(head + turns * R, count + deep):
        turn(n, n % R, n // R)


def uses(count, R, k):
    return (count - k + R - 1) // R


def over_groups(eng, body):
    body(0, 0, 0)
    body(1, 1, 0)
    with eng.Fori(1, NG // 2 - 1) as i:
        for h in range(2):
            body(h, 2 * i + h, i)
    body(0, NG - 2, NG // 2 - 1)
    body(1, NG - 1, NG // 2 - 1)


def edge_stage(nc, K, tag, R, spread=None, sort=None, when=always):
    with Scope(nc, tag) as s:
        pieces = [(c, min(512, ET - c)) for c in range(0, ET, 512)]
        pool_go = s.sem("pool_go")
        if spread:
            placed_in, table, acc = spread
            pairs = s.sb("pairs", [P, ET, 2], I32)
            col = s.sb("col", [P, ET], F32)
            gidx = s.sb("gidx", [P, 2, G], U32)
            gath = s.sb("gath", [P, 2, G, D], F32)
            hot = s.sb("hot", [P, 2, G, P], F32)
            p_sum = s.ps("p_sum", [P, G // 2, 2, 2 * P])
            p_first = p_sum[:, :, :, :].rearrange("p b t x -> p b (t x)")
            pairs_in, prep, starts, col_ready = (s.sem(n) for n in ("pairs_in", "prep", "starts", "col_ready"))
            gidx_ready, hot_ready = s.sem("gidx_ready"), s.sem("hot_ready")
            gathered = [s.sem(f"gathered{h}") for h in range(2)]
            summed, added = s.sem("summed"), s.sem("added")
        if sort:
            which, key_p, other_p, rows, placed_out = sort
            ends = s.sb("ends", [P, 2, ET], I32)
            part_i = s.sb("part_i", [P, ET], I32)
            lo_b = s.sb("lo_b", [P, ET], BF16)
            hi_b = s.sb("hi_b", [P, ET], BF16)
            key_f = s.sb("key_f", [P, ET], F32)
            row = s.sb("row", [P, 2, 2, G * P], F32)
            oh_lo = s.sb("oh_lo", [P, 2, G, P], BF16)
            oh_hi = s.sb("oh_hi", [P, 2, G, NB], BF16)
            oh_loT = s.sb("oh_loT", [P, G, P], F32)
            base = s.sb("base", [P, 2, G + 1, NB], F32)
            same = s.sb("same", [P, 2, P], F32)
            rank = s.sb("rank", [P, G], F32)
            picked = s.sb("picked", [P, G, NB], F32)
            place_f = s.sb("place_f", [P, G], F32)
            place_i = s.sb("place_i", [P, G], I32)
            pl_hi = s.sb("pl_hi", [P, G], I32)
            pl_lo = s.sb("pl_lo", [P, G], I32)
            addr_f = s.sb("addr_f", [P, G], F32)
            addr = s.sb("addr", [P, 2, G], U32)
            pair = s.sb("pair", [P, 2, G, 2], I32)
            p_cnt = s.ps("p_cnt", [P, 2, 512])
            p_pick = s.ps("p_pick", [P, 2, 512])
            loaded, keyed = s.sem("loaded"), s.sem("keyed")
            row_in = [s.sem(f"row_in{h}") for h in range(2)]
            hots, hotsT, counted = s.sem("hots"), s.sem("hotsT"), s.sem("counted")
            based, base_moved, pick_done = s.sem("based"), s.sem("base_moved"), s.sem("pick_done")
            ranked, chain, addr_ready, pair_ready = s.sem("ranked"), s.sem("chain"), s.sem("addr_ready"), s.sem("pair_ready")
            scattered = [s.sem(f"scattered{h}") for h in range(2)]
            PS = 7
        with nc.Block() as block:
            @block.sync
            def _(sp):
                def body():
                    if spread:
                        sp.dma_start(pairs[:, :, :], placed_in.rearrange("(p t) k -> p t k", p=P)).then_inc(pairs_in, 16)
                    if sort:
                        sp.dma_start(ends[:, 0, :], key_p).then_inc(loaded, 16)
                        sp.dma_start(ends[:, 1, :], other_p).then_inc(loaded, 16)

                        def load(h, q, i):
                            if not early(q, 2):
                                sp.wait_ge(ranked, G * (q - 1))
                                sp.wait_ge(hotsT, q - 1)
                            for r in range(2):
                                sp.dma_start(row[:, h, r, :], rows[which, r, bass.ds(q * (G * P), G * P)]
                                             .partition_broadcast(P)).then_inc(row_in[h], 16)
                        over_groups(sp, load)
                when(sp, R, body)

            @block.tensor
            def _(pe):
                def tile_starts():
                    pe.wait_ge(prep, 1)
                    for n, (c, w) in enumerate(pieces):
                        nc.tensor.matmul(p_first[:, n, 0:w], K["ones"][0:1, :], col[0:1, c:c + w],
                                         start=True, stop=True).then_inc(starts, 1)
                    pe.wait_ge(col_ready, len(pieces))

                def counts(h, q, i):
                    pe.wait_ge(hots, 2 * q + 2)
                    if not early(q, 2):
                        pe.wait_ge(based, q - 1)
                    for g in range(G):
                        last = nc.tensor.matmul(
                            p_cnt[:, h, g * NB:G * NB].rearrange("p (g b) -> p g b", b=NB),
                            oh_lo[:, h, g], bc_mid(oh_hi[:, h, g], G - g), start=(g == 0), stop=(g == G - 1))
                    last.then_inc(counted, 1)

                def sums(h, q, i):
                    pe.wait_ge(gathered[h], 16 * G * i + 16 * G)
                    pe.wait_ge(hot_ready, q + 1)
                    for g in range(G):
                        if g % 2 == 0 and not early(q, 1):
                            pe.wait_ge(added, q * G + g - G + 2)
                        for d in range(2):
                            last = nc.tensor.matmul(p_sum[:, g // 2, g % 2, d * P:(d + 1) * P],
                                                    gath[:, h, g, d * P:(d + 1) * P], hot[:, h, g],
                                                    start=True, stop=True)
                        last.then_inc(summed, 1)

                def picks(h, q, i):
                    pe.wait_ge(hotsT, q + 1)
                    pe.wait_ge(based, q + 1)
                    if not early(q, 2):
                        pe.wait_ge(chain, PS * (q - 1))
                    for g in range(G):
                        last = nc.tensor.matmul(p_pick[:, h, g * NB:(g + 1) * NB], oh_loT[:, g],
                                                base[:, h, g], start=True, stop=True)
                    last.then_inc(pick_done, 1)

                def group(h, q, i):
                    if sort:
                        counts(h, q, i)
                    if spread:
                        sums(h, q, i)
                    if sort:
                        picks(h, q, i)

                def body():
                    if spread:
                        tile_starts()
                    over_groups(pe, group)
                when(pe, R, body)

            @block.vector
            def _(dve):
                def spread_start():
                    dve.wait_ge(pairs_in, 16)
                    nc.vector.tensor_copy(col[:, :], pairs[:, :, 0]).then_inc(prep, 1)
                    dve.wait_ge(prep, 1)
                    for n, (c, w) in enumerate(pieces):
                        dve.wait_ge(starts, n + 1)
                        nc.vector.tensor_tensor(col[:, c:c + w], col[:, c:c + w], p_first[:, n, 0:w],
                                                ALU.subtract).then_inc(col_ready, 1)
                    dve.wait_ge(col_ready, len(pieces))
                    windows_hot(0, 0)

                def windows_hot(h, q):
                    nc.vector.tensor_tensor(hot[:, h], bc_mid(K["iota"][:, :], G),
                                            bc_last(col[:, bass.ds(q * G, G)], P), ALU.is_equal).then_inc(hot_ready, 1)

                def adds(h, q, i):
                    if not (isinstance(q, int) and q == NG - 1):
                        if not early(q, 1):
                            dve.wait_ge(summed, q * G)
                        windows_hot(1 - h, q + 1)
                    offs = nc.values_load_multi_w_load_instructions(
                        pairs[0:1, bass.ds(q * G, G), 0], engines=[DVE_ENGINE], min_val=0, max_val=PAD_KEY,
                        skip_runtime_bounds_check_because="an edge's end is a node or PAD_KEY")[1]
                    for g in range(G):
                        if g % 2 == 0:
                            dve.wait_ge(summed, q * G + g + 2)
                        if not (early(q, 1) and g == 0):
                            dve.wait_ge(added, q * G + g)
                        win = acc[:, :, bass.ds(offs[g], P)]
                        nc.vector.tensor_tensor(win, win, p_sum[:, g // 2, g % 2, :].rearrange("p (d v) -> p d v", d=2),
                                                ALU.add).then_inc(added, 1)

                def sort_start():
                    dve.wait_ge(loaded, 32)
                    nc.vector.tensor_scalar(part_i[:, :], ends[:, 0, :], P - 1, None, ALU.bitwise_and).then_inc(keyed, 1)
                    nc.vector.tensor_copy(key_f[:, :], ends[:, 0, :]).then_inc(keyed, 1)
                    nc.vector.tensor_copy(base[:, 0, 0, :], K["first"][:, which, :]).then_inc(keyed, 1)
                    dve.wait_ge(keyed, 3)
                    nc.vector.tensor_copy(lo_b[:, :], part_i[:, :]).then_inc(keyed, 1)
                    dve.wait_ge(keyed, 4)
                    nc.vector.tensor_scalar(part_i[:, :], ends[:, 0, :], 7, None, ALU.arith_shift_right).then_inc(keyed, 1)
                    dve.wait_ge(keyed, 5)
                    nc.vector.tensor_copy(hi_b[:, :], part_i[:, :]).then_inc(keyed, 1)
                    dve.wait_ge(keyed, 6)
                    key_hots(0, 0)

                def key_hots(h, q):
                    nc.vector.tensor_tensor(oh_lo[:, h], bc_mid(K["iota_b"][:, :], G),
                                            bc_last(lo_b[:, bass.ds(q * G, G)], P), ALU.is_equal).then_inc(hots, 1)
                    nc.vector.tensor_tensor(oh_hi[:, h], bc_mid(K["iota_b"][:, 0:NB], G),
                                            bc_last(hi_b[:, bass.ds(q * G, G)], NB), ALU.is_equal).then_inc(hots, 1)

                def ranks(h, q, i):
                    if not early(q, 1):
                        dve.wait_ge(pick_done, q)
                        dve.wait_ge(chain, PS * q)
                    dve.wait_ge(row_in[h], 32 * i + 32)
                    nc.vector.tensor_scalar(oh_loT[:, :].rearrange("p g e -> p (g e)"), row[:, h, 1, :],
                                            K["part"][:, 0:1], None, ALU.is_equal).then_inc(hotsT, 1)
                    dve.wait_ge(counted, q + 1)
                    if not early(q, 1):
                        dve.wait_ge(base_moved, q)
                    nc.vector.tensor_tensor(base[:, h, 1:G + 1, :], bc_mid(base[:, h, 0, :], G),
                                            p_cnt[:, h, 0:G * NB].rearrange("p (g b) -> p g b", g=G),
                                            ALU.add).then_inc(based, 1)
                    for g in range(G):
                        if not (early(q, 1) and g < 2):
                            dve.wait_ge(ranked, q * G + g - 1)
                        nc.vector.scalar_tensor_tensor(same[:, g % 2, :], row[:, h, 0, g * P:(g + 1) * P],
                                                       key_f[:, bass.ds(q * G + g, 1)],
                                                       K["before"][:, :], ALU.is_equal, ALU.mult,
                                                       accum_out=rank[:, g:g + 1]).then_inc(ranked, 1)
                    dve.wait_ge(based, q + 1)
                    nc.vector.tensor_copy(base[:, 1 - h, 0, :], base[:, h, G, :]).then_inc(base_moved, 1)
                    if not (isinstance(q, int) and q == NG - 1):
                        key_hots(1 - h, q + 1)

                def places(h, q, i):
                    dve.wait_ge(pick_done, q + 1)
                    c = q * PS
                    nc.vector.tensor_tensor(picked[:, :, :], p_pick[:, h, 0:G * NB].rearrange("p (g b) -> p g b", g=G),
                                            oh_hi[:, h], ALU.mult).then_inc(chain, 1)
                    dve.wait_ge(chain, c + 1)
                    nc.vector.tensor_reduce(place_f[:, :], picked[:, :, :], AX.X, ALU.add).then_inc(chain, 1)
                    dve.wait_ge(ranked, q * G + G)
                    dve.wait_ge(chain, c + 2)
                    nc.vector.tensor_tensor(place_i[:, :], place_f[:, :], rank[:, :], ALU.add).then_inc(chain, 1)
                    dve.wait_ge(chain, c + 3)
                    nc.vector.tensor_scalar(pl_hi[:, :], place_i[:, :], 7, None, ALU.arith_shift_right).then_inc(chain, 1)
                    nc.vector.tensor_scalar(pl_lo[:, :], place_i[:, :], P - 1, None, ALU.bitwise_and).then_inc(chain, 1)
                    dve.wait_ge(chain, c + 5)
                    nc.vector.tensor_scalar(addr_f[:, :], pl_lo[:, :], float(ET), None, ALU.mult).then_inc(chain, 1)
                    dve.wait_ge(chain, c + 6)
                    if not early(q, 2):
                        dve.wait_ge(scattered[h], 16 * G * i)
                    nc.vector.tensor_tensor(addr[:, h, :], addr_f[:, :], pl_hi[:, :], ALU.add).then_inc(chain, 1)
                    dve.wait_ge(chain, c + 7)
                    dve.sem_inc(addr_ready, 1)

                def group(h, q, i):
                    if sort:
                        ranks(h, q, i)
                    if spread:
                        adds(h, q, i)
                    if sort:
                        places(h, q, i)

                def body():
                    if spread:
                        spread_start()
                    if sort:
                        sort_start()
                    over_groups(dve, group)
                when(dve, R, body)

            @block.scalar
            def _(act):
                def group(h, q, i):
                    if spread:
                        if not early(q, 2):
                            act.wait_ge(gathered[h], 16 * G * i)
                        nc.scalar.copy(gidx[:, h, :], pairs[:, bass.ds(q * G, G), 1]).then_inc(gidx_ready, 1)
                    if sort:
                        if not early(q, 2):
                            act.wait_ge(scattered[h], 16 * G * i)
                        for k in range(2):
                            nc.scalar.copy(pair[:, h, :, k], ends[:, k, bass.ds(q * G, G)]).then_inc(pair_ready, 1)

                def body():
                    if spread:
                        act.wait_ge(pairs_in, 16)
                    if sort:
                        act.wait_ge(loaded, 32)
                    over_groups(act, group)
                when(act, R, body)

            @block.gpsimd
            def _(pool):
                def gathers(h, q, i):
                    pool.wait_ge(gidx_ready, q + 1)
                    pool.sem_inc(pool_go, 1)
                    if not early(q, 2):
                        pool.wait_ge(summed, (q - 1) * G)
                        pool.sem_inc(pool_go, 1)
                    for g in range(G):
                        nc.gpsimd.indirect_dma_start(
                            out=gath[:, h, g, :], out_offset=None, in_=table,
                            in_offset=bass.IndirectOffsetOnAxis(ap=gidx[:, h, g:g + 1], axis=0)).then_inc(gathered[h], 16)

                def scatters(h, q):
                    pool.wait_ge(pair_ready, 2 * q + 2)
                    pool.sem_inc(pool_go, 1)
                    pool.wait_ge(addr_ready, q + 1)
                    pool.sem_inc(pool_go, 1)
                    for g in range(G):
                        nc.gpsimd.indirect_dma_start(
                            out=placed_out, out_offset=bass.IndirectOffsetOnAxis(ap=addr[:, h, g:g + 1], axis=0),
                            in_=pair[:, h, g, :], in_offset=None).then_inc(scattered[h], 16)

                def group(h, q, i):
                    if spread:
                        gathers(h, q, i)
                    if sort and not early(q, 1):
                        scatters(1 - h, q - 1)

                def body():
                    over_groups(pool, group)
                    if sort:
                        scatters(1, NG - 1)
                        for h in range(2):
                            pool.wait_ge(scattered[h], 16 * G * (NG // 2))
                when(pool, R, body)


def clear_stage(nc, tag, arrays, acc):
    with Scope(nc, tag) as s:
        ROWS = 8
        zero = s.sb("zero", [P, ROWS * D], F32)
        made, stored = s.sem("made"), s.sem("stored")
        n = 0
        with nc.Block() as block:
            @block.vector
            def _(dve):
                nc.vector.memset(zero[:, :], 0.0).then_inc(made, 1)
                nc.vector.memset(acc[:, :, :], 0.0).then_inc(made, 1)
                dve.wait_ge(made, 2)

            @block.sync
            def _(sp):
                sp.wait_ge(made, 1)
                n = 0
                for a in arrays:
                    for r in range(0, a.shape[0], P * ROWS):
                        m = min(ROWS, (a.shape[0] - r) // P)
                        sp.dma_start(a[r:r + m * P, :].rearrange("(p r) d -> p (r d)", p=P),
                                     zero[:, 0:m * D]).then_inc(stored, 16)
                        n += 1
                sp.wait_ge(stored, 16 * n)


def norm_stage(nc, K, tag, X, x_in=None, xl_out=None, scaled_out=None, turned=None, proj=None):
    W = proj[0].shape[1] if proj else 0
    with Scope(nc, tag) as s:
        stats = s.sb("stats", [P, NB, 6], F32)
        mean = s.sb("mean", [P, NB], F32)
        var = s.sb("var", [P, NB], F32)
        half = s.sb("half", [P, NB], F32)
        root = s.sb("root", [P, NB], F32)
        rstd = s.sb("rstd", [P, NB], F32)
        xl = s.sb("xl", [P, RB, D], F32)
        xs = s.sb("xs", [P, RB, D], F32)
        xT = s.sb("xT", [P, RB, DH, P], F32)
        factor = s.sb("factor", [P, 1], F32)
        w = s.sb("w", [P, DH, max(W, 1)], F32)
        p_turn = s.ps("p_turn", [P, RB, 512])
        p_proj = s.ps("p_proj", [P, RB, 512])
        x_loaded, w_loaded, padded = s.sem("x_loaded"), s.sem("w_loaded"), s.sem("padded")
        stat, chain, rooted = s.sem("stat"), s.sem("chain"), s.sem("rooted")
        normed, scaled, turned_sem, evac = s.sem("normed"), s.sem("scaled"), s.sem("turned"), s.sem("evac")
        projd, proj_out = s.sem("projd"), s.sem("proj_out")
        xl_stored = [s.sem(f"xl_stored{h}") for h in range(RB)]
        xs_stored = [s.sem(f"xs_stored{h}") for h in range(RB)]
        with nc.Block() as block:
            @block.sync
            def _(sp):
                if x_in is not None:
                    whole = (NB - 1) * P
                    sp.wait_ge(padded, 1)
                    sp.dma_start(X[0:LAST, NB - 1, :], x_in[whole:N, :]).then_inc(x_loaded, 16)
                    for c in range(0, NB - 1, 12):
                        sp.dma_start(X[:, c:c + 12, :], x_in[c * P:(c + 12) * P, :]
                                     .rearrange("(b p) d -> p b d", p=P)).then_inc(x_loaded, 16)
                if turned:
                    sp.dma_start(factor[:, :], turned[1].partition_broadcast(P)).then_inc(w_loaded, 16)
                if proj:
                    sp.dma_start(w[:, :, :], proj[0].rearrange("(k p) w -> p k w", p=P)).then_inc(w_loaded, 16)

                if xl_out is not None:
                    def store(h, b, i):
                        sp.wait_ge(normed, b + 1)
                        sp.dma_start(xl_out[bass.ds(b * P, P), :], xl[:, h, :]).then_inc(xl_stored[h], 16)
                    in_ring(sp, NB, RB, (0, store))
                    for h in range(RB):
                        sp.wait_ge(xl_stored[h], 16 * uses(NB, RB, h))

            @block.vector
            def _(dve):
                if x_in is not None:
                    nc.vector.memset(X[:, NB - 1, :], 0.0).then_inc(padded, 1)
                    dve.wait_ge(x_loaded, 16 * (1 + len(range(0, NB - 1, 12))))
                with dve.Fori(0, NB) as b:
                    nc.vector.bn_stats(stats[:, bass.ds(b, 1), :].rearrange("p a s -> p (a s)"),
                                       X[:, bass.ds(b, 1), :].rearrange("p a d -> p (a d)")).then_inc(stat, 1)
                dve.wait_ge(stat, NB)
                nc.vector.tensor_tensor(mean[:, :], stats[:, :, 1], stats[:, :, 4], ALU.add).then_inc(chain, 1)
                nc.vector.tensor_tensor(half[:, :], stats[:, :, 1], stats[:, :, 4], ALU.subtract).then_inc(chain, 1)
                nc.vector.tensor_tensor(var[:, :], stats[:, :, 2], stats[:, :, 5], ALU.add).then_inc(chain, 1)
                dve.wait_ge(chain, 3)
                nc.vector.tensor_scalar(mean[:, :], mean[:, :], 0.5, None, ALU.mult).then_inc(chain, 1)
                nc.vector.tensor_tensor(half[:, :], half[:, :], half[:, :], ALU.mult).then_inc(chain, 1)
                nc.vector.tensor_scalar(var[:, :], var[:, :], 1.0 / D, LN_EPS, ALU.mult, ALU.add).then_inc(chain, 1)
                dve.wait_ge(chain, 6)
                nc.vector.scalar_tensor_tensor(var[:, :], half[:, :], 0.25, var[:, :], ALU.mult,
                                               ALU.add).then_inc(chain, 1)
                dve.wait_ge(rooted, 1)
                nc.vector.reciprocal(rstd[:, :], root[:, :]).then_inc(chain, 1)
                dve.wait_ge(chain, 8)
                nc.vector.tensor_tensor(half[:, :], rstd[:, :], rstd[:, :], ALU.mult).then_inc(chain, 1)
                dve.wait_ge(chain, 9)
                nc.vector.tensor_tensor(half[:, :], half[:, :], var[:, :], ALU.mult).then_inc(chain, 1)
                dve.wait_ge(chain, 10)
                nc.vector.tensor_scalar(half[:, :], half[:, :], -0.5, 1.5, ALU.mult, ALU.add).then_inc(chain, 1)
                dve.wait_ge(chain, 11)
                nc.vector.tensor_tensor(rstd[:, :], rstd[:, :], half[:, :], ALU.mult).then_inc(chain, 1)
                dve.wait_ge(chain, 12)

                def norm(h, b, i):
                    if not early(b, RB):
                        if xl_out is not None:
                            dve.wait_ge(xl_stored[h], 16 * i)
                        if scaled_out is not None:
                            dve.wait_ge(scaled, b - RB + 1)
                        dve.wait_ge(turned_sem, b - RB + 1)
                    nc.vector.tensor_scalar(xl[:, h, :], X[:, bass.ds(b, 1), :].rearrange("p a d -> p (a d)"),
                                            mean[:, bass.ds(b, 1)], rstd[:, bass.ds(b, 1)],
                                            ALU.subtract, ALU.mult).then_inc(normed, 1)

                def take(h, b, i):
                    dve.wait_ge(projd, b + 1)
                    nc.vector.tensor_copy(proj[1][:, bass.ds(b, 1), :].rearrange("p a w -> p (a w)"),
                                          p_proj[:, h, 0:W]).then_inc(proj_out, 1)

                if proj:
                    in_ring(dve, NB, RB, (0, norm), (3, take))
                    dve.wait_ge(proj_out, NB)
                else:
                    in_ring(dve, NB, RB, (0, norm))

            @block.scalar
            def _(act):
                act.wait_ge(chain, 7)
                nc.scalar.activation(root[:, :], var[:, :], ACT.Sqrt).then_inc(rooted, 1)
                if turned:
                    act.wait_ge(w_loaded, 16)

                def scale(h, b, i):
                    act.wait_ge(normed, b + 1)
                    if not early(b, RB):
                        act.wait_ge(xs_stored[h], 16 * i)
                    nc.scalar.activation(xs[:, h, :], xl[:, h, :], ACT.Copy,
                                         scale=K["dis"][:, bass.ds(b, 1)]).then_inc(scaled, 1)

                def store(h, b, i):
                    act.wait_ge(scaled, b + 1)
                    act.dma_start(scaled_out[bass.ds(b * P, P), :], xs[:, h, :]).then_inc(xs_stored[h], 16)

                def take(h, b, i):
                    act.wait_ge(turned_sem, b + 1)
                    src = p_turn[:, h, 0:D].rearrange("p (k v) -> p k v", k=DH)
                    if turned:
                        nc.scalar.activation(turned[0][:, :, bass.ds(b * P, P)], src, ACT.Copy,
                                             scale=factor[:, 0:1]).then_inc(evac, 1)
                    else:
                        if not early(b, RB):
                            act.wait_ge(projd, b - RB + 1)
                        nc.scalar.copy(xT[:, h], src).then_inc(evac, 1)

                if scaled_out is not None:
                    in_ring(act, NB, RB, (0, scale), (1, take), (1, store))
                    for h in range(RB):
                        act.wait_ge(xs_stored[h], 16 * uses(NB, RB, h))
                else:
                    in_ring(act, NB, RB, (0, take))
                act.wait_ge(evac, NB)

            @block.tensor
            def _(pe):
                if proj:
                    pe.wait_ge(w_loaded, 16)

                def turn(h, b, i):
                    pe.wait_ge(normed, b + 1)
                    if not early(b, RB):
                        pe.wait_ge(evac, b - RB + 1)
                    for k in range(DH):
                        last = nc.tensor.transpose(p_turn[:, h, k * P:(k + 1) * P], xl[:, h, k * P:(k + 1) * P],
                                                   K["ident"][:, :])
                    last.then_inc(turned_sem, 1)

                def product(h, b, i):
                    pe.wait_ge(evac, b + 1)
                    if not early(b, RB):
                        pe.wait_ge(proj_out, b - RB + 1)
                    for k in range(DH):
                        last = nc.tensor.matmul(p_proj[:, h, 0:W], xT[:, h, k], w[:, k, :],
                                                start=(k == 0), stop=(k == DH - 1))
                    last.then_inc(projd, 1)

                if proj:
                    in_ring(pe, NB, RB, (0, turn), (2, product))
                else:
                    in_ring(pe, NB, RB, (0, turn))


def network0_stage(nc, K, tag, X, acc, w1_in, b1_in, w2_in, b2_in, gamma_in, beta_in):
    MH = HID // P
    with Scope(nc, tag) as s:
        w1 = s.sb("w1", [P, DH, HID], F32)
        w2 = s.sb("w2", [P, MH, D], F32)
        b1 = s.sb("b1", [P, MH], F32)
        b2 = s.sb("b2", [P, DH], F32)
        gamma = s.sb("gamma", [P, DH], F32)
        beta = s.sb("beta", [P, DH], F32)
        hid = s.sb("hid", [P, MH, CH], F32)
        NC = len(CHUNKS)
        stats = s.sb("stats", [P, DH, NC, 6], F32)
        agg = s.sb("agg", [P, DH, 2], F32)
        root = s.sb("root", [P, DH], F32)
        scale = s.sb("scale", [P, DH], F32)
        shift = s.sb("shift", [P, DH], F32)
        tmp = s.sb("tmp", [P, DH], F32)
        bn = s.sb("bn", [P, 2, DH, P], F32)
        p_hid = s.ps("p_hid", [P, MH, 512])
        p_out = s.ps("p_out", [P, DH, 512])
        p_back = s.ps("p_back", [P, 2, 512])
        loaded, hid_mm, hid_ready = s.sem("loaded"), s.sem("hid_mm"), s.sem("hid_ready")
        out_mm, out_ready, stat, chain = s.sem("out_mm"), s.sem("out_ready"), s.sem("stat"), s.sem("chain")
        rooted, bn_ready, backed, addx = s.sem("rooted"), s.sem("bn_ready"), s.sem("backed"), s.sem("addx")
        CW = CHUNKS[-1][1]
        with nc.Block() as block:
            @block.sync
            def _(sp):
                sp.dma_start(w1[:, :, :], w1_in.rearrange("(k p) n -> p k n", p=P)).then_inc(loaded, 16)
                sp.dma_start(w2[:, :, :], w2_in.rearrange("(k p) n -> p k n", p=P)).then_inc(loaded, 16)
                with nc.allow_non_contiguous_dma(reason="a few hundred floats"):
                    sp.dma_start(b1[:, :], b1_in.rearrange("(m p) -> p m", p=P)).then_inc(loaded, 16)
                    sp.dma_start(b2[:, :], b2_in.rearrange("(m p) -> p m", p=P)).then_inc(loaded, 16)
                    sp.dma_start(gamma[:, :], gamma_in.rearrange("(m p) -> p m", p=P)).then_inc(loaded, 16)
                    sp.dma_start(beta[:, :], beta_in.rearrange("(m p) -> p m", p=P)).then_inc(loaded, 16)

            @block.tensor
            def _(pe):
                pe.wait_ge(loaded, 96)

                def chunk(c, n, w, first=False):
                    for m in range(MH):
                        if not first:
                            pe.wait_ge(hid_ready, n * MH - MH + m + 1)
                        for k in range(DH):
                            last = nc.tensor.matmul(p_hid[:, m, 0:w], w1[:, k, m * P:(m + 1) * P],
                                                    acc[:, k, bass.ds(c, w)], start=(k == 0), stop=(k == DH - 1))
                        last.then_inc(hid_mm, 1)
                    for o in range(DH):
                        if not first:
                            pe.wait_ge(out_ready, n * DH - DH + o + 1)
                        for m in range(MH):
                            if o == 0:
                                pe.wait_ge(hid_ready, n * MH + m + 1)
                            last = nc.tensor.matmul(p_out[:, o, 0:w], w2[:, m, o * P:(o + 1) * P], hid[:, m, 0:w],
                                                    start=(m == 0), stop=(m == MH - 1))
                        last.then_inc(out_mm, 1)

                chunk(0, 0, CH, True)
                with pe.Fori(1, NC - 1) as n:
                    chunk(n * CH, n, CH)
                chunk((NC - 1) * CH, NC - 1, CW)

                def back(h, b, first=False):
                    pe.wait_ge(bn_ready, b + 1)
                    if not first:
                        pe.wait_ge(addx, b - 1)
                    for k in range(DH):
                        last = nc.tensor.transpose(p_back[:, h, k * P:(k + 1) * P], bn[:, h, k], K["ident"][:, :])
                    last.then_inc(backed, 1)
                back(0, 0, True)
                back(1, 1, True)
                with pe.Fori(1, NB // 2) as i:
                    for h in range(2):
                        back(h, 2 * i + h)
                back(0, NB - 1)

            @block.scalar
            def _(act):
                act.wait_ge(loaded, 96)

                def chunk(c, n, w, first=False):
                    for m in range(MH):
                        act.wait_ge(hid_mm, n * MH + m + 1)
                        if not first:
                            act.wait_ge(out_mm, n * DH)
                        nc.scalar.activation(hid[:, m, 0:w], p_hid[:, m, 0:w], ACT.Relu,
                                             bias=b1[:, m:m + 1]).then_inc(hid_ready, 1)
                chunk(0, 0, CH, True)
                with act.Fori(1, NC - 1) as n:
                    chunk(n * CH, n, CH)
                chunk((NC - 1) * CH, NC - 1, CW)
                act.wait_ge(chain, 3)
                nc.scalar.activation(root[:, :], tmp[:, :], ACT.Sqrt).then_inc(rooted, 1)
                act.wait_ge(chain, 10)

                def norm(h, b, first=False):
                    if not first:
                        act.wait_ge(backed, b - 1)
                    for k in range(DH):
                        last = nc.scalar.activation(bn[:, h, k], acc[:, k, bass.ds(b * P, P)], ACT.Identity,
                                                    bias=shift[:, k:k + 1], scale=scale[:, k:k + 1])
                    last.then_inc(bn_ready, 1)
                norm(0, 0, True)
                norm(1, 1, True)
                with act.Fori(1, NB // 2) as i:
                    for h in range(2):
                        norm(h, 2 * i + h)
                norm(0, NB - 1)

            @block.vector
            def _(dve):
                dve.wait_ge(loaded, 96)

                def chunk(c, n, w):
                    for o in range(DH):
                        dve.wait_ge(out_mm, n * DH + o + 1)
                        nc.vector.tensor_scalar(acc[:, o, bass.ds(c, w)], p_out[:, o, 0:w], b2[:, o:o + 1], None,
                                                ALU.add).then_inc(out_ready, 1)
                    for o in range(DH):
                        dve.wait_ge(out_ready, n * DH + o + 1)
                        v = min(w, N - (NC - 1) * CH) if w != CH else w
                        nc.vector.bn_stats(stats[:, o, bass.ds(n, 1), :].rearrange("p a s -> p (a s)"),
                                           acc[:, o, bass.ds(c, v)]).then_inc(stat, 1)
                with dve.Fori(0, NC - 1) as n:
                    chunk(n * CH, n, CH)
                chunk((NC - 1) * CH, NC - 1, CW)
                dve.wait_ge(stat, DH * NC)
                for o in range(DH):
                    nc.vector.bn_aggr(agg[:, o, :], stats[:, o, :, :].rearrange("p n s -> p (n s)")).then_inc(chain, 1)
                dve.wait_ge(chain, 2)
                nc.vector.tensor_scalar(tmp[:, :], agg[:, :, 1], 1e-5, None, ALU.add).then_inc(chain, 1)
                dve.wait_ge(rooted, 1)
                nc.vector.reciprocal(scale[:, :], root[:, :]).then_inc(chain, 1)
                dve.wait_ge(chain, 4)
                nc.vector.tensor_tensor(shift[:, :], scale[:, :], scale[:, :], ALU.mult).then_inc(chain, 1)
                dve.wait_ge(chain, 5)
                nc.vector.tensor_tensor(shift[:, :], shift[:, :], tmp[:, :], ALU.mult).then_inc(chain, 1)
                dve.wait_ge(chain, 6)
                nc.vector.tensor_scalar(shift[:, :], shift[:, :], -0.5, 1.5, ALU.mult, ALU.add).then_inc(chain, 1)
                dve.wait_ge(chain, 7)
                nc.vector.tensor_tensor(scale[:, :], scale[:, :], shift[:, :], ALU.mult).then_inc(chain, 1)
                dve.wait_ge(chain, 8)
                nc.vector.tensor_tensor(scale[:, :], scale[:, :], gamma[:, :], ALU.mult).then_inc(chain, 1)
                dve.wait_ge(chain, 9)
                for o in range(DH):
                    nc.vector.scalar_tensor_tensor(tmp[:, o:o + 1], agg[:, o, 0:1], -1.0, scale[:, o:o + 1],
                                                   ALU.mult, ALU.mult).then_inc(stat, 1)
                dve.wait_ge(stat, DH * NC + DH)
                nc.vector.tensor_tensor(shift[:, :], tmp[:, :], beta[:, :], ALU.add).then_inc(chain, 1)

                def add(h, b):
                    dve.wait_ge(backed, b + 1)
                    xb = X[:, bass.ds(b, 1), :].rearrange("p a d -> p (a d)")
                    nc.vector.tensor_tensor(xb, xb, p_back[:, h, 0:D], ALU.add).then_inc(addx, 1)
                with dve.Fori(0, NB // 2) as i:
                    for h in range(2):
                        add(h, 2 * i + h)
                add(0, NB - 1)
                dve.wait_ge(addx, NB)


def in_pairs(eng, count, body):
    body(0, 0, 0, True)
    body(1, 1, 0, True)
    with eng.Fori(1, count // 2) as i:
        for h in range(2):
            body(h, 2 * i + h, i, False)
    if count % 2:
        body(0, count - 1, count // 2, False)


def waits_of_half(count, h):
    return (count + 1 - h) // 2


def laplace_stage(nc, K, tag, X, acc, out, order, w_in, prev, prev2, mine, table, bias_in):
    last_term = order == 3
    with Scope(nc, tag) as s:
        w = s.sb("w", [P, DH, D], F32)
        bias = s.sb("bias", [P, D], F32)
        fm = s.sb("fm", [P, RB, DH, P], F32)
        t1 = s.sb("t1", [P, RB, D], F32)
        t2 = s.sb("t2", [P, RB, D], F32)
        part = s.sb("part", [P, RB, D], F32)
        term = s.sb("term", [P, RB, D], F32)
        xs = s.sb("xs", [P, RB, D], F32)
        tT = s.sb("tT", [P, RB, DH, P], F32)
        p_sum = s.ps("p_sum", [P, 2, 512])
        p_turn = s.ps("p_turn", [P, 2, 512])
        p_out = s.ps("p_out", [P, RB, 512])
        loaded, pool_go = s.sem("loaded"), s.sem("pool_go")
        t_in = [s.sem(f"t_in{h}") for h in range(RB)]
        cut, cleared, summed, parted = s.sem("cut"), s.sem("cleared"), s.sem("summed"), s.sem("parted")
        lapl, termed, turned, evac = s.sem("lapl"), s.sem("termed"), s.sem("turned"), s.sem("evac")
        scaled, outd, added, biased = s.sem("scaled"), s.sem("outd"), s.sem("added"), s.sem("biased")
        mine_stored = [s.sem(f"mine_stored{h}") for h in range(RB)]
        xs_stored = [s.sem(f"xs_stored{h}") for h in range(RB)]
        LOADS = 1 if order == 1 else 2
        with nc.Block() as block:
            @block.sync
            def _(sp):
                sp.dma_start(w[:, :, :], w_in.rearrange("(k p) n -> p k n", p=P)).then_inc(loaded, 16)
                sp.dma_start(bias[:, :], bias_in.partition_broadcast(P)).then_inc(loaded, 16)

                def load(h, b, i):
                    if not early(b, RB):
                        sp.wait_ge(termed, b - RB + 1)
                    sp.dma_start(t1[:, h, :], prev[bass.ds(b * P, P), :]).then_inc(t_in[h], 16)
                    if order > 1:
                        sp.dma_start(t2[:, h, :], prev2[bass.ds(b * P, P), :]).then_inc(t_in[h], 16)
                in_ring(sp, NB, RB, (0, load))

            @block.scalar
            def _(act):
                def cut_block(h, b, i):
                    if not early(b, RB):
                        act.wait_ge(summed, b - RB + 1)
                    nc.scalar.copy(fm[:, h], acc[:, :, bass.ds(b * P, P)]).then_inc(cut, 1)

                def take(h, b, i):
                    act.wait_ge(turned, b + 1)
                    if not early(b, RB):
                        act.wait_ge(outd, b - RB + 1)
                    nc.scalar.copy(tT[:, h], p_turn[:, h % 2, 0:D].rearrange("p (k v) -> p k v", k=DH)).then_inc(evac, 1)

                def scale(h, b, i):
                    act.wait_ge(termed, b + 1)
                    if not early(b, RB):
                        act.wait_ge(xs_stored[h], 16 * i)
                    nc.scalar.activation(xs[:, h, :], term[:, h, :], ACT.Copy,
                                         scale=K["dis"][:, bass.ds(b, 1)]).then_inc(scaled, 1)

                if last_term:
                    in_ring(act, NB, RB, (0, cut_block), (3, take))
                else:
                    in_ring(act, NB, RB, (0, cut_block), (2, scale), (3, take))

            if not last_term:
                @block.gpsimd
                def _(pool):
                    def store(h, b, i):
                        pool.wait_ge(scaled, b + 1)
                        pool.sem_inc(pool_go, 1)
                        nc.gpsimd.dma_start(table[bass.ds(b * P, P), :], xs[:, h, :]).then_inc(xs_stored[h], 16)
                        pool.wait_ge(termed, b + 1)
                        pool.sem_inc(pool_go, 1)
                        nc.gpsimd.dma_start(mine[bass.ds(b * P, P), :], term[:, h, :]).then_inc(mine_stored[h], 16)
                    in_ring(pool, NB, RB, (0, store))
                    for h in range(RB):
                        pool.wait_ge(xs_stored[h], 16 * uses(NB, RB, h))
                        pool.wait_ge(mine_stored[h], 16 * uses(NB, RB, h))

            @block.tensor
            def _(pe):
                pe.wait_ge(loaded, 32)

                def turn_sums(h, b, i):
                    pe.wait_ge(cut, b + 1)
                    if not early(b, 2):
                        pe.wait_ge(parted, b - 1)
                    for k in range(DH):
                        last = nc.tensor.transpose(p_sum[:, h % 2, k * P:(k + 1) * P], fm[:, h, k], K["ident"][:, :])
                    last.then_inc(summed, 1)

                def turn_term(h, b, i):
                    pe.wait_ge(termed, b + 1)
                    if not early(b, 2):
                        pe.wait_ge(evac, b - 1)
                    for k in range(DH):
                        last = nc.tensor.transpose(p_turn[:, h % 2, k * P:(k + 1) * P], term[:, h, k * P:(k + 1) * P],
                                                   K["ident"][:, :])
                    last.then_inc(turned, 1)

                def product(h, b, i):
                    pe.wait_ge(evac, b + 1)
                    if not early(b, RB):
                        pe.wait_ge(added, b - RB + 1)
                    for k in range(DH):
                        last = nc.tensor.matmul(p_out[:, h, 0:D], tT[:, h, k], w[:, k, :],
                                                start=(k == 0), stop=(k == DH - 1))
                    last.then_inc(outd, 1)
                in_ring(pe, NB, RB, (0, turn_sums), (2, turn_term), (4, product))

            @block.vector
            def _(dve):
                if last_term:
                    dve.wait_ge(loaded, 32)

                def make(h, b, i):
                    dve.wait_ge(cut, b + 1)
                    nc.vector.tensor_copy(acc[:, :, bass.ds(b * P, P)], K["zero"][:, :, :]).then_inc(cleared, 1)
                    dve.wait_ge(summed, b + 1)
                    nc.vector.tensor_scalar(part[:, h, :], p_sum[:, h % 2, 0:D], K["ndis"][:, bass.ds(b, 1)], None,
                                            ALU.mult).then_inc(parted, 1)
                    dve.wait_ge(parted, b + 1)
                    dve.wait_ge(t_in[h], 16 * LOADS * i + 16 * LOADS)
                    if not early(b, RB):
                        dve.wait_ge(turned, b - RB + 1)
                        if not last_term:
                            dve.wait_ge(scaled, b - RB + 1)
                            dve.wait_ge(mine_stored[h], 16 * i)
                    if order == 1:
                        nc.vector.scalar_tensor_tensor(term[:, h, :], t1[:, h, :], K["nloop"][:, bass.ds(b, 1)],
                                                       part[:, h, :], ALU.mult, ALU.add).then_inc(termed, 1)
                    else:
                        nc.vector.scalar_tensor_tensor(part[:, h, :], t1[:, h, :], K["nloop"][:, bass.ds(b, 1)],
                                                       part[:, h, :], ALU.mult, ALU.add).then_inc(lapl, 1)
                        dve.wait_ge(lapl, b + 1)
                        nc.vector.scalar_tensor_tensor(term[:, h, :], part[:, h, :], 2.0, t2[:, h, :],
                                                       ALU.mult, ALU.subtract).then_inc(termed, 1)

                def add(h, b, i):
                    dve.wait_ge(outd, b + 1)
                    ob = out[:, bass.ds(b, 1), :].rearrange("p a d -> p (a d)")
                    nc.vector.tensor_tensor(ob, ob, p_out[:, h, 0:D], ALU.add).then_inc(added, 1)
                    if last_term:
                        xb = X[:, bass.ds(b, 1), :].rearrange("p a d -> p (a d)")
                        nc.vector.tensor_tensor(xb, xb, bias[:, :], ALU.add).then_inc(biased, 1)
                        dve.wait_ge(added, b + 1)
                        dve.wait_ge(biased, 2 * b + 1)
                        nc.vector.tensor_tensor(xb, xb, ob, ALU.add).then_inc(biased, 1)
                in_ring(dve, NB, RB, (0, make), (5, add))


T0 = -(-(2 * N + NE * (P - 1)) // (2 * P)) * 2
T1E = -(-CAP // CH) * CH


def route_stage(nc, K, tag, logits, R, top, bias_in=None):
    first_mix = top == 2
    with Scope(nc, tag) as s:
        shape = [P, NB, NE]
        best = s.sb("best", [P, NB], F32)
        ssum = s.sb("ssum", [P, NB], F32)
        ex = s.sb("ex", shape, F32)
        prob = s.sb("prob", shape, F32)
        eq = s.sb("eq", shape, F32)
        cand = s.sb("cand", shape, F32)
        hot = s.sb("hot", [P, 2, NB, NE], F32)
        both = s.sb("both", shape, F32)
        valid = s.sb("valid", [P, NB], F32)
        top_p = s.sb("top_p", [P, 2, NB], F32)
        low = s.sb("low", [P, NB], F32)
        before = s.sb("before", [P, NB + 1, NE], F32)
        cnt_i = s.sb("cnt_i", [P, NE], I32)
        tiles_i = s.sb("tiles_i", [P, NE], I32)
        tiles = s.sb("tiles", [P, NE], F32)
        ends = s.sb("ends", [P, NE + 1], F32)
        place = s.sb("place", shape, F32)
        slot = s.sb("slot", [P, 2, NB], F32)
        over = s.sb("over", [P, NB], F32)
        tnum = s.sb("tnum", [P, P], F32)
        past = s.sb("past", [P, P], F32)
        gb = s.sb("gb", [P, NE], F32)
        p_pre = s.ps("p_pre", [P, 512])
        p_tot = s.ps("p_tot", [P, 512])
        chain, biased, exped, hotted, counted = (s.sem(n) for n in ("chain", "biased", "exped", "hotted", "counted"))
        iota8 = bc_mid(K["iota"][:, 0:NE], NB)
        with nc.Block() as block:
            @block.sync
            def _(sp):
                if bias_in is not None:
                    sp.dma_start(gb[:, :], bias_in.partition_broadcast(P)).then_inc(biased, 16)

            @block.vector
            def _(dve):
                n = [0]

                def link(ins):
                    n[0] += 1
                    ins.then_inc(chain, 1)
                    dve.wait_ge(chain, n[0])

                if bias_in is not None:
                    dve.wait_ge(biased, 16)
                    link(nc.vector.tensor_tensor(logits[:, :, :], logits[:, :, :], bc_mid(gb[:, :], NB), ALU.add))
                link(nc.vector.tensor_reduce(best[:, :], logits[:, :, :], AX.X, ALU.max))
                link(nc.vector.tensor_tensor(ex[:, :, :], logits[:, :, :], bc_last(best[:, :], NE), ALU.subtract))
                nc.vector.memset(valid[:, :], 1.0).then_inc(hotted, 1)
                dve.wait_ge(hotted, 1)
                link(nc.vector.tensor_scalar(valid[:, NB - 1:NB], K["part"][:, 0:1], float(LAST), None, ALU.is_lt))
                dve.wait_ge(exped, 1)
                link(nc.vector.tensor_reduce(ssum[:, :], prob[:, :, :], AX.X, ALU.add))
                link(nc.vector.reciprocal(best[:, :], ssum[:, :]))
                link(nc.vector.tensor_tensor(prob[:, :, :], prob[:, :, :], bc_last(best[:, :], NE), ALU.mult))
                for c in range(top):
                    link(nc.vector.tensor_reduce(top_p[:, c, :], prob[:, :, :], AX.X, ALU.max))
                    link(nc.vector.tensor_tensor(eq[:, :, :], prob[:, :, :], bc_last(top_p[:, c, :], NE), ALU.is_equal))
                    link(nc.vector.scalar_tensor_tensor(cand[:, :, :], eq[:, :, :], -float(NE), iota8,
                                                        ALU.mult, ALU.add))
                    link(nc.vector.tensor_reduce(low[:, :], cand[:, :, :], AX.X, ALU.min))
                    link(nc.vector.tensor_tensor(eq[:, :, :], cand[:, :, :], bc_last(low[:, :], NE), ALU.is_equal))
                    link(nc.vector.tensor_tensor(hot[:, c], eq[:, :, :], bc_last(valid[:, :], NE), ALU.mult))
                    if c + 1 < top:
                        link(nc.vector.scalar_tensor_tensor(prob[:, :, :], eq[:, :, :], -2.0, prob[:, :, :],
                                                            ALU.mult, ALU.add))
                if first_mix:
                    nc.vector.tensor_tensor(both[:, :, :], hot[:, 0], hot[:, 1], ALU.add).then_inc(hotted, 1)
                    link(nc.vector.tensor_tensor(low[:, :], top_p[:, 0, :], top_p[:, 1, :], ALU.add))
                    link(nc.vector.tensor_scalar(low[:, :], low[:, :], 1e-9, None, ALU.add))
                    link(nc.vector.reciprocal(best[:, :], low[:, :]))
                    link(nc.vector.tensor_tensor(R["gate"][:, :, :], top_p[:, :, :], bc_mid(best[:, :], 2), ALU.mult))
                else:
                    nc.vector.tensor_copy(both[:, :, :], hot[:, 0]).then_inc(hotted, 1)
                dve.wait_ge(counted, 1)
                tot = p_tot[:, 0:NB * NE].rearrange("p (b e) -> p b e", e=NE)
                pre = p_pre[:, 0:NB * NE].rearrange("p (b e) -> p b e", e=NE)
                link(nc.vector.memset(before[:, 0, :], 0.0))
                for b in range(NB):
                    link(nc.vector.tensor_tensor(before[:, b + 1, :], before[:, b, :], tot[:, b, :], ALU.add))
                link(nc.vector.tensor_tensor(place[:, :, :], before[:, 0:NB, :], pre, ALU.add))
                if first_mix:
                    link(nc.vector.tensor_scalar(cnt_i[:, :], before[:, NB, :], float(P - 1), None, ALU.add))
                    link(nc.vector.tensor_scalar(tiles_i[:, :], cnt_i[:, :], 7, None, ALU.arith_shift_right))
                    link(nc.vector.tensor_copy(tiles[:, :], tiles_i[:, :]))
                    link(nc.vector.memset(ends[:, 0:1], 0.0))
                    for e in range(NE):
                        link(nc.vector.tensor_tensor(ends[:, e + 1:e + 2], ends[:, e:e + 1], tiles[:, e:e + 1], ALU.add))
                    link(nc.vector.tensor_scalar(tiles[:, :], ends[:, 0:NE], float(P), None, ALU.mult))
                    link(nc.vector.tensor_tensor(place[:, :, :], place[:, :, :], bc_mid(tiles[:, :], NB), ALU.add))
                    link(nc.vector.memset(tnum[:, :], 0.0))
                    for e in range(NE - 1):
                        link(nc.vector.tensor_scalar(past[:, :], K["iota"][:, :], ends[:, e + 1:e + 2], None, ALU.is_ge))
                        link(nc.vector.tensor_tensor(tnum[:, :], tnum[:, :], past[:, :], ALU.add))
                    link(nc.vector.tensor_copy(R["tile_expert"][:, :], tnum[:, :]))
                for c in range(top):
                    link(nc.vector.tensor_tensor(eq[:, :, :], hot[:, c], place[:, :, :], ALU.mult))
                    link(nc.vector.tensor_reduce(slot[:, c, :], eq[:, :, :], AX.X, ALU.add))
                if first_mix:
                    link(nc.vector.tensor_copy(R["to"][:, :, :], slot[:, :, :]))
                    link(nc.vector.tensor_copy(R["of"][:, :, :], slot[:, :, :]))
                else:
                    link(nc.vector.tensor_scalar(over[:, :], slot[:, 0, :], float(CAP), None, ALU.is_ge))
                    link(nc.vector.tensor_scalar(best[:, :], over[:, :], -1.0, 1.0, ALU.mult, ALU.add))
                    link(nc.vector.tensor_tensor(R["gate"][:, 0, :], top_p[:, 0, :], best[:, :], ALU.mult))
                    link(nc.vector.tensor_scalar(slot[:, 0, :], slot[:, 0, :], float(CAP - 1), None, ALU.min))
                    link(nc.vector.tensor_scalar(low[:, :], low[:, :], float(NE), float(T1E), ALU.add, ALU.mult))
                    link(nc.vector.tensor_tensor(slot[:, 0, :], slot[:, 0, :], low[:, :], ALU.add))
                    link(nc.vector.tensor_copy(R["of"][:, 0, :], slot[:, 0, :]))
                    link(nc.vector.scalar_tensor_tensor(slot[:, 1, :], over[:, :], float(NE * T1E), slot[:, 0, :],
                                                        ALU.mult, ALU.add))
                    link(nc.vector.tensor_copy(R["to"][:, 0, :], slot[:, 1, :]))

            @block.scalar
            def _(act):
                act.wait_ge(chain, 2 + (bias_in is not None))
                nc.scalar.activation(prob[:, :, :], ex[:, :, :], ACT.Exp).then_inc(exped, 1)

            @block.tensor
            def _(pe):
                pe.wait_ge(hotted, 2)
                rhs = both[:, :, :].rearrange("p b e -> p (b e)")
                nc.tensor.matmul(p_pre[:, 0:NB * NE], K["after"][:, :], rhs, start=True, stop=True)
                nc.tensor.matmul(p_tot[:, 0:NB * NE], K["ones"][:, :], rhs, start=True, stop=True).then_inc(counted, 1)


def dispatch_stage(nc, K, tag, R, top, xl, rows, limit):
    with Scope(nc, tag) as s:
        x = s.sb("x", [P, 2, D], F32)
        idx = s.sb("idx", [P, 2, top], U32)
        x_in = [s.sem(f"x_in{h}") for h in range(2)]
        sent = [s.sem(f"sent{h}") for h in range(2)]
        idx_ready, pool_go = s.sem("idx_ready"), s.sem("pool_go")
        with nc.Block() as block:
            @block.sync
            def _(sp):
                def load(h, b, i, first):
                    if not first:
                        sp.wait_ge(sent[h], 16 * top * i)
                    sp.dma_start(x[:, h, :], xl[bass.ds(b * P, P), :]).then_inc(x_in[h], 16)
                in_pairs(sp, NB, load)

            @block.scalar
            def _(act):
                def copy(h, b, i, first):
                    if not first:
                        act.wait_ge(sent[h], 16 * top * i)
                    nc.scalar.copy(idx[:, h, :], R["to"][:, 0:top, bass.ds(b, 1)]
                                   .rearrange("p c a -> p (c a)")).then_inc(idx_ready, 1)
                in_pairs(act, NB, copy)

            @block.gpsimd
            def _(pool):
                def send(h, b, i, first, n=P):
                    pool.wait_ge(x_in[h], 16 * i + 16)
                    pool.sem_inc(pool_go, 1)
                    pool.wait_ge(idx_ready, b + 1)
                    pool.sem_inc(pool_go, 1)
                    for c in range(top):
                        nc.gpsimd.indirect_dma_start(
                            out=rows, out_offset=bass.IndirectOffsetOnAxis(ap=idx[0:n, h, c:c + 1], axis=0),
                            in_=x[0:n, h, :], in_offset=None, bounds_check=limit - 1,
                            oob_is_err=False).then_inc(sent[h], 16)
                in_pairs(pool, NB - 1, send)
                send(0, NB - 1, NB // 2, False, LAST)
                for h in range(2):
                    pool.wait_ge(sent[h], 16 * top * waits_of_half(NB, h))


def combine_stage(nc, K, tag, X, R, top, rows, out=None):
    with Scope(nc, tag) as s:
        y = s.sb("y", [P, 2, top, D], F32)
        idx = s.sb("idx", [P, 2, top], U32)
        yw = s.sb("yw", [P, D], F32)
        flag = s.sb("flag", [P, 3, D], I32)
        fixed = s.sb("fixed", [P, 3, D], F32)
        got = [s.sem(f"got{h}") for h in range(2)]
        idx_ready, pool_go, used, chain = s.sem("idx_ready"), s.sem("pool_go"), s.sem("used"), s.sem("chain")
        stored, fixes = s.sem("stored"), s.sem("fixes")
        with nc.Block() as block:
            @block.scalar
            def _(act):
                def copy(h, b, i, first):
                    if not first:
                        act.wait_ge(got[h], 16 * top * i)
                    nc.scalar.copy(idx[:, h, :], R["of"][:, 0:top, bass.ds(b, 1)]
                                   .rearrange("p c a -> p (c a)")).then_inc(idx_ready, 1)
                in_pairs(act, NB, copy)

            @block.gpsimd
            def _(pool):
                def fetch(h, b, i, first):
                    pool.wait_ge(idx_ready, b + 1)
                    pool.sem_inc(pool_go, 1)
                    if not first:
                        pool.wait_ge(used, b - 1)
                        pool.sem_inc(pool_go, 1)
                    for c in range(top):
                        nc.gpsimd.indirect_dma_start(
                            out=y[:, h, c, :], out_offset=None, in_=rows,
                            in_offset=bass.IndirectOffsetOnAxis(ap=idx[:, h, c:c + 1], axis=0)).then_inc(got[h], 16)
                in_pairs(pool, NB, fetch)

            @block.vector
            def _(dve):
                if out is not None:
                    for c, v in enumerate((0.0, 1e4, -1e4)):
                        nc.vector.memset(fixed[:, c, :], v).then_inc(fixes, 1)
                    dve.wait_ge(fixes, 3)
                STEPS = 8 if out is not None else 2

                def add(h, b, i, first):
                    xb = X[:, bass.ds(b, 1), :].rearrange("p a d -> p (a d)")
                    dve.wait_ge(got[h], 16 * top * i + 16 * top)
                    c = b * STEPS
                    if out is None:
                        nc.vector.scalar_tensor_tensor(xb, y[:, h, 0, :], R["gate"][:, 0, bass.ds(b, 1)], xb,
                                                       ALU.mult, ALU.add).then_inc(chain, 1)
                        dve.wait_ge(chain, c + 1)
                        nc.vector.scalar_tensor_tensor(xb, y[:, h, 1, :], R["gate"][:, 1, bass.ds(b, 1)], xb,
                                                       ALU.mult, ALU.add).then_inc(chain, 1)
                        dve.wait_ge(chain, c + 2)
                        dve.sem_inc(used, 1)
                        return
                    nc.vector.tensor_scalar(yw[:, :], y[:, h, 0, :], R["gate"][:, 0, bass.ds(b, 1)], None,
                                            ALU.mult).then_inc(chain, 1)
                    dve.wait_ge(chain, c + 1)
                    nc.vector.tensor_tensor(flag[:, 0, :], yw[:, :], yw[:, :], ALU.not_equal).then_inc(chain, 1)
                    nc.vector.tensor_scalar(flag[:, 1, :], yw[:, :], float("inf"), None, ALU.is_equal).then_inc(chain, 1)
                    nc.vector.tensor_scalar(flag[:, 2, :], yw[:, :], float("-inf"), None, ALU.is_equal).then_inc(chain, 1)
                    dve.wait_ge(chain, c + 4)
                    dve.sem_inc(fixes, 1)
                    for m in range(3):
                        nc.vector.copy_predicated(yw[:, :], flag[:, m, :], fixed[:, m, :]).then_inc(chain, 1)
                        dve.wait_ge(chain, c + 5 + m)
                        dve.sem_inc(fixes, 1)
                    nc.vector.tensor_tensor(xb, xb, yw[:, :], ALU.add).then_inc(chain, 1)
                    dve.wait_ge(chain, c + 8)
                    dve.sem_inc(used, 1)
                in_pairs(dve, NB, add)

            @block.sync
            def _(sp):
                if out is not None:
                    with sp.Fori(0, NB - 1) as b:
                        sp.wait_ge(used, b + 1)
                        sp.dma_start(out[bass.ds(b * P, P), :],
                                     X[:, bass.ds(b, 1), :].rearrange("p a d -> p (a d)")).then_inc(stored, 16)
                    sp.wait_ge(used, NB)
                    sp.dma_start(out[(NB - 1) * P:N, :], X[0:LAST, NB - 1, :]).then_inc(stored, 16)
                    sp.wait_ge(stored, 16 * NB)


def experts0_stage(nc, K, tag, R, w13_in, w2_in, rows, out_rows):
    HW = H0 // 2
    KH = -(-H0 // P)
    KL = H0 - (KH - 1) * P
    with Scope(nc, tag) as s:
        w13 = s.sb("w13", [P, DH, NE * 2 * H0], F32)
        w2 = s.sb("w2", [P, KH, NE * D], F32)
        x = s.sb("x", [P, 2, D], F32)
        xT = s.sb("xT", [P, 2, DH, P], F32)
        sg = s.sb("sg", [P, H0], F32)
        hid = s.sb("hid", [P, KH * P], F32)
        hT = s.sb("hT", [P, KH, P], F32)
        y = s.sb("y", [P, 2, D], F32)
        p_h = s.ps("p_h", [P, 2, 2, 512])
        p_x = s.ps("p_x", [P, 512])
        p_hT = s.ps("p_hT", [P, 2, 512])
        p_y = s.ps("p_y", [P, 512])
        loaded, xturned, xT_ready = s.sem("loaded"), s.sem("xturned"), s.sem("xT_ready")
        x_in = [s.sem(f"x_in{h}") for h in range(2)]
        y_stored = [s.sem(f"y_stored{h}") for h in range(2)]
        h_mm, silud, h_ready = s.sem("h_mm"), s.sem("silud"), s.sem("h_ready")
        hturned, hT_a, hT_b = s.sem("hturned"), s.sem("hT_a"), s.sem("hT_b")
        y_mm, y_ready = s.sem("y_mm"), s.sem("y_ready")
        cleared = s.sem("cleared")
        with nc.Block() as block:
            @block.sync
            def _(sp):
                for e in range(0, NE, 2):
                    sp.dma_start(w13[:, :, e * 2 * H0:(e + 2) * 2 * H0],
                                 w13_in[:, e * 2 * H0:(e + 2) * 2 * H0].rearrange("(k p) n -> p k n", p=P)).then_inc(loaded, 16)
                sp.dma_start(w2[:, 0:KH - 1, :], w2_in[0:(KH - 1) * P, :].rearrange("(k p) n -> p k n", p=P)).then_inc(loaded, 16)
                sp.dma_start(w2[0:KL, KH - 1, :], w2_in[(KH - 1) * P:H0, :]).then_inc(loaded, 16)

                def load(h, t, i, first):
                    if not first:
                        sp.wait_ge(xturned, t - 1)
                    sp.dma_start(x[:, h, :], rows[bass.ds(t * P, P), :]).then_inc(x_in[h], 16)
                in_pairs(sp, T0, load)

            @block.tensor
            def _(pe):
                def x_turn(h, t, i, first):
                    pe.wait_ge(x_in[h], 16 * i + 16)
                    if not (first and h == 0):
                        pe.wait_ge(xT_ready, t)
                    for k in range(DH):
                        last = nc.tensor.transpose(p_x[:, k * P:(k + 1) * P], x[:, h, k * P:(k + 1) * P],
                                                   K["ident"][:, :])
                    last.then_inc(xturned, 1)

                def up(h, t, e, first):
                    pe.wait_ge(xT_ready, t + 1)
                    for c in range(2):
                        if not first:
                            pe.wait_ge(h_ready, 2 * t - 2 + c + 1)
                        for m in range(2):
                            for k in range(DH):
                                last = nc.tensor.matmul(p_h[:, c, m, 0:HW], xT[:, h, k],
                                                        w13[:, k, bass.ds(e * (2 * H0) + (m * H0 + c * HW), HW)],
                                                        start=(k == 0), stop=(k == DH - 1))
                        last.then_inc(h_mm, 1)

                def down(t, e, first):
                    pe.wait_ge(h_ready, 2 * t + 2)
                    if not first:
                        pe.wait_ge(hT_a, t)
                        pe.wait_ge(hT_b, t)
                    for k in range(KH):
                        r = P if k < KH - 1 else KL
                        last = nc.tensor.transpose(p_hT[0:r, k // 4, (k % 4) * P:(k % 4 + 1) * P],
                                                   hid[:, k * P:k * P + r], K["ident"][:, :])
                        if k in (3, KH - 1):
                            last.then_inc(hturned, 1)
                    if not first:
                        pe.wait_ge(y_ready, t)
                    for k in range(KH):
                        if k == 0:
                            pe.wait_ge(hT_a, t + 1)
                        if k == 4:
                            pe.wait_ge(hT_b, t + 1)
                        r = P if k < KH - 1 else KL
                        last = nc.tensor.matmul(p_y[:, 0:D], hT[0:r, k], w2[0:r, k, bass.ds(e * D, D)],
                                                start=(k == 0), stop=(k == KH - 1))
                    last.then_inc(y_mm, 1)

                def experts(t, n):
                    return nc.values_load_multi_w_load_instructions(
                        R["tile_expert"][0:1, bass.ds(t, n)], engines=[PE_ENGINE], min_val=0, max_val=NE - 1,
                        skip_runtime_bounds_check_because="a count of at most NE - 1 experts")[1]

                pe.wait_ge(loaded, 16 * (NE // 2 + 2))
                e = experts(0, 2)
                x_turn(0, 0, 0, True)
                x_turn(1, 1, 0, True)
                up(0, 0, e[0], True)
                down(0, e[0], True)
                with pe.Fori(1, T0 // 2) as i:
                    e = experts(2 * i - 1, 2)
                    x_turn(0, 2 * i, i, False)
                    up(1, 2 * i - 1, e[0], False)
                    down(2 * i - 1, e[0], False)
                    x_turn(1, 2 * i + 1, i, False)
                    up(0, 2 * i, e[1], False)
                    down(2 * i, e[1], False)
                e = experts(T0 - 1, 1)
                up(1, T0 - 1, e[0], False)
                down(T0 - 1, e[0], False)

            @block.scalar
            def _(act):
                def take_x(h, t, first):
                    act.wait_ge(xturned, t + 1)
                    if not first:
                        act.wait_ge(h_mm, 2 * (t - 1))
                    nc.scalar.copy(xT[:, h], p_x[:, 0:D].rearrange("p (k v) -> p k v", k=DH)).then_inc(xT_ready, 1)

                def silu(t, first):
                    for c in range(2):
                        act.wait_ge(h_mm, 2 * t + c + 1)
                        if not first:
                            act.wait_ge(h_ready, 2 * t - 2 + c + 1)
                        nc.scalar.activation(sg[:, c * HW:(c + 1) * HW], p_h[:, c, 0, 0:HW], ACT.Silu).then_inc(silud, 1)
                    act.wait_ge(hturned, 2 * t + 1)
                    if not first:
                        act.wait_ge(y_mm, t)
                    nc.scalar.copy(hT[:, 0:4], p_hT[:, 0, :].rearrange("p (k v) -> p k v", k=4)).then_inc(hT_a, 1)

                take_x(0, 0, True)
                take_x(1, 1, True)
                silu(0, True)
                with act.Fori(1, T0 // 2) as i:
                    take_x(0, 2 * i, False)
                    silu(2 * i - 1, False)
                    take_x(1, 2 * i + 1, False)
                    silu(2 * i, False)
                silu(T0 - 1, False)

            @block.vector
            def _(dve):
                def step(h, t, i, first):
                    first_of_all = first and h == 0
                    for c in range(2):
                        dve.wait_ge(silud, 2 * t + c + 1)
                        if not first_of_all:
                            dve.wait_ge(hturned, 2 * t)
                        nc.vector.tensor_tensor(hid[:, c * HW:(c + 1) * HW], sg[:, c * HW:(c + 1) * HW],
                                                p_h[:, c, 1, 0:HW], ALU.mult).then_inc(h_ready, 1)
                    dve.wait_ge(hturned, 2 * t + 2)
                    if not first_of_all:
                        dve.wait_ge(y_mm, t)
                    nc.vector.tensor_copy(hT[:, 4], p_hT[:, 1, 0:P]).then_inc(cleared, 1)
                    nc.vector.tensor_copy(hT[0:KL, 5], p_hT[0:KL, 1, P:2 * P]).then_inc(hT_b, 1)
                    dve.wait_ge(y_mm, t + 1)
                    if not first:
                        dve.wait_ge(y_stored[h], 16 * i)
                    nc.vector.tensor_copy(y[:, h, :], p_y[:, 0:D]).then_inc(y_ready, 1)
                in_pairs(dve, T0, step)

            @block.gpsimd
            def _(pool):
                def store(h, t, i, first):
                    pool.wait_ge(y_ready, t + 1)
                    pool.sem_inc(cleared, 1)
                    nc.gpsimd.dma_start(out_rows[bass.ds(t * P, P), :], y[:, h, :]).then_inc(y_stored[h], 16)
                in_pairs(pool, T0, store)
                for h in range(2):
                    pool.wait_ge(y_stored[h], 16 * waits_of_half(T0, h))


def experts1_stage(nc, K, tag, w1_in, b1_in, w2_in, b2_in, rows, out_rows):
    MF = F1 // P
    TT = T1E // P
    TC = CH // P
    NCH = T1E // CH
    with Scope(nc, tag) as s:
        w1 = s.sb("w1", [P, 2, DH, F1], F32)
        w2 = s.sb("w2", [P, 2, MF, D], F32)
        b1 = s.sb("b1", [P, 2, MF], F32)
        b2 = s.sb("b2", [P, 2, D], F32)
        x = s.sb("x", [P, 2, TT, D], F32)
        xT = s.sb("xT", [P, DH, T1E], F32)
        hid = s.sb("hid", [P, MF, CH], F32)
        y = s.sb("y", [P, 2, D], F32)
        p_x = s.ps("p_x", [P, 2, 512])
        p_h = s.ps("p_h", [P, 4, 512])
        p_y = s.ps("p_y", [P, 2, 512])
        e_in = [s.sem(f"e_in{h}") for h in range(2)]
        y_stored = [s.sem(f"y_stored{h}") for h in range(2)]
        xturned, xT_ready, h_mm, h_ready = s.sem("xturned"), s.sem("xT_ready"), s.sem("h_mm"), s.sem("h_ready")
        y_mm, y_ready, pool_go = s.sem("y_mm"), s.sem("y_ready"), s.sem("pool_go")
        XP = NCH * DH
        HP = NCH * MF
        LOADS = 5

        def per_expert(eng, body):
            body(0, 0, 0, True)
            body(1, 1, 0, False)
            with eng.Fori(1, NE // 2) as i:
                for h in range(2):
                    body(h, 2 * i + h, i, False)

        with nc.Block() as block:
            @block.sync
            def _(sp):
                def load(h, e, i, first):
                    sp.wait_ge(y_mm, TT * (e - 1))
                    sp.wait_ge(y_ready, TT * (e - 1))
                    fetch(h, e)

                def fetch(h, e):
                    sp.dma_start(x[:, h], rows[bass.ds(e * T1E, T1E), :].rearrange("(t p) d -> p t d", p=P)).then_inc(e_in[h], 16)
                    sp.dma_start(w1[:, h], w1_in[bass.ds(e * D, D), :].rearrange("(k p) f -> p k f", p=P)).then_inc(e_in[h], 16)
                    sp.dma_start(b1[:, h], b1_in[bass.ds(e * P, P), :]).then_inc(e_in[h], 16)
                    sp.dma_start(w2[:, h], w2_in[bass.ds(e * F1, F1), :].rearrange("(m p) d -> p m d", p=P)).then_inc(e_in[h], 16)
                    sp.dma_start(b2[:, h], b2_in[bass.ds(e * D, D)].partition_broadcast(P)).then_inc(e_in[h], 16)
                fetch(0, 0)
                fetch(1, 1)
                with sp.Fori(1, NE // 2) as i:
                    for h in range(2):
                        load(h, 2 * i + h, i, False)

            @block.tensor
            def _(pe):
                def expert(h, e, i, first):
                    pe.wait_ge(e_in[h], 16 * LOADS * i + 16 * LOADS)
                    for c in range(NCH):
                        for k in range(DH):
                            j = c * DH + k
                            if not (first and j < 2):
                                pe.wait_ge(xT_ready, e * XP + j - 1)
                            for t in range(TC):
                                last = nc.tensor.transpose(p_x[:, j % 2, t * P:(t + 1) * P],
                                                           x[:, h, c * TC + t, k * P:(k + 1) * P], K["ident"][:, :])
                            last.then_inc(xturned, 1)
                    for c in range(NCH):
                        pe.wait_ge(xT_ready, e * XP + (c + 1) * DH)
                        for m in range(MF):
                            j = c * MF + m
                            if not (first and j < 4):
                                pe.wait_ge(h_ready, e * HP + j - 3)
                            for k in range(DH):
                                last = nc.tensor.matmul(p_h[:, m % 4, :], w1[:, h, k, m * P:(m + 1) * P],
                                                        xT[:, k, c * CH:(c + 1) * CH],
                                                        start=(k == 0), stop=(k == DH - 1))
                            last.then_inc(h_mm, 1)
                        for t in range(TC):
                            j = c * TC + t
                            if not (first and j < 2):
                                pe.wait_ge(y_ready, e * TT + j - 1)
                            for m in range(MF):
                                if t == 0:
                                    pe.wait_ge(h_ready, e * HP + c * MF + m + 1)
                                last = nc.tensor.matmul(p_y[:, j % 2, 0:D], hid[:, m, t * P:(t + 1) * P],
                                                        w2[:, h, m, :], start=(m == 0), stop=(m == MF - 1))
                            last.then_inc(y_mm, 1)
                per_expert(pe, expert)

            @block.scalar
            def _(act):
                def expert(h, e, i, first):
                    act.wait_ge(e_in[h], 16 * LOADS * i + 16 * LOADS)
                    for c in range(NCH):
                        for m in range(MF):
                            act.wait_ge(h_mm, e * HP + c * MF + m + 1)
                            if not (first and c == 0):
                                act.wait_ge(y_mm, e * TT + c * TC)
                            nc.scalar.activation(hid[:, m, :], p_h[:, m % 4, :], ACT.Relu,
                                                 bias=b1[:, h, m:m + 1]).then_inc(h_ready, 1)
                per_expert(act, expert)

            @block.vector
            def _(dve):
                def expert(h, e, i, first):
                    dve.wait_ge(e_in[h], 16 * LOADS * i + 16 * LOADS)
                    for c in range(NCH):
                        for k in range(DH):
                            dve.wait_ge(xturned, e * XP + c * DH + k + 1)
                            if not first:
                                dve.wait_ge(h_mm, e * HP)
                            nc.vector.tensor_copy(xT[:, k, c * CH:(c + 1) * CH],
                                                  p_x[:, (c * DH + k) % 2, :]).then_inc(xT_ready, 1)
                    for j in range(TT):
                        dve.wait_ge(y_mm, e * TT + j + 1)
                        if not (first and j < 2):
                            dve.wait_ge(y_stored[j % 2], 16 * (e * (TT // 2) + j // 2))
                        nc.vector.tensor_tensor(y[:, j % 2, :], p_y[:, j % 2, 0:D], b2[:, h, :],
                                                ALU.add).then_inc(y_ready, 1)
                per_expert(dve, expert)

            @block.gpsimd
            def _(pool):
                with pool.Fori(0, NE * TT // 2) as i:
                    for h in range(2):
                        pool.wait_ge(y_ready, 2 * i + h + 1)
                        pool.sem_inc(pool_go, 1)
                        nc.gpsimd.dma_start(out_rows[bass.ds((2 * i + h) * P, P), :], y[:, h, :]).then_inc(y_stored[h], 16)
                for h in range(2):
                    pool.wait_ge(y_stored[h], 16 * NE * TT // 2)


def make_constants(nc, ctx):
    K = {}
    for name, shape, dt in (("ones", [P, P], F32), ("iota", [P, P], F32), ("iota_b", [P, P], BF16),
                            ("part", [P, 1], F32), ("ident", [P, P], F32), ("before", [P, P], F32),
                            ("after", [P, P], F32), ("first", [P, 2, NB], F32), ("nloop", [P, NB], F32),
                            ("dis", [P, NB], F32), ("zero", [P, DH, P], F32), ("ndis", [P, NB], F32)):
        K[name] = ctx.enter_context(nc.sbuf_tensor(f"k_{name}", shape, dt))
    return K


def bass_gnn_ffn_kernel(nc, x, dst_p, src_p, dst_r, src_r, eps, m_w1, m_b1, m_w2, m_b2, gamma, beta,
                        router, w13, w2e, cheb_w, cheb_b, gate_w, gate_b, f_w1, f_b1, f_w2, f_b2, out):
    def dram(name, shape, dt=F32):
        return nc.dram_tensor(name, shape, dt, kind="Internal").ap()

    rows = dram("edge_rows", [2, 2, EP])
    by_dst = dram("by_dst", [P * ET, 2], I32)
    by_src = dram("by_src", [P * ET, 2], I32)
    table = dram("table", [NP, D])
    terms = [dram(f"term{k}", [NP, D]) for k in range(3)]
    xl = dram("xl", [NP, D])
    in0, out0 = dram("in0", [T0 * P, D]), dram("out0", [T0 * P, D])
    in1, out1 = dram("in1", [NE * T1E, D]), dram("out1", [NE * T1E, D])
    with ExitStack() as ctx:
        def sb(name, shape, dt=F32):
            return ctx.enter_context(nc.sbuf_tensor(name, shape, dt))

        K = make_constants(nc, ctx)
        X = sb("X", [P, NB, D])
        R = {"gate": sb("r_gate", [P, 2, NB]), "to": sb("r_to", [P, 2, NB], I32),
             "of": sb("r_of", [P, 2, NB], I32), "tile_expert": sb("r_tile_expert", [P, P], I32),
             "unsorted": sb("r_unsorted", [P, 1], I32)}
        logits = sb("logits", [P, NB, NE])
        constants_stage(nc, K)

        with nc.sbuf_tensor("acc_a", [P, DH, ACC_W], F32) as acc:
            clear_stage(nc, "clr", [in0, in1], acc)
            ends_stage(nc, K, dst_p, src_p, dst_r, src_r, rows, by_dst, R)
            counts_stage(nc, K, "cd", 0, dst_p, src_p, R, unsorted_only)
            edge_stage(nc, K, "sd", R, sort=(0, dst_p, src_p, rows, by_dst), when=unsorted_only)
            counts_stage(nc, K, "cs", 1, src_p, dst_p, R, always)
            norm_stage(nc, K, "n0", X, x_in=x, xl_out=table, turned=(acc, eps))
            edge_stage(nc, K, "s0", R, spread=(by_dst, table, acc), sort=(1, src_p, dst_p, rows, by_src))
            network0_stage(nc, K, "m0", X, acc, m_w1, m_b1, m_w2, m_b2, gamma, beta)

        norm_stage(nc, K, "n1", X, xl_out=xl, proj=(router, logits))
        route_stage(nc, K, "r0", logits, R, 2)
        dispatch_stage(nc, K, "d0", R, 2, xl, in0, T0 * P)
        experts0_stage(nc, K, "e0", R, w13, w2e, in0, out0)
        combine_stage(nc, K, "c0", X, R, 2, out0)

        with nc.sbuf_tensor("acc_b", [P, DH, ACC_W], F32) as acc, nc.sbuf_tensor("cheb", [P, NB, D], F32) as cheb:
            clear_stage(nc, "clr2", [], acc)
            norm_stage(nc, K, "n2", X, xl_out=terms[0], scaled_out=table, proj=(cheb_w[0:D, :], cheb))
            for k in range(1, 4):
                edge_stage(nc, K, f"s{k}", R, spread=(by_src, table, acc))
                laplace_stage(nc, K, f"l{k}", X, acc, cheb, k, cheb_w[k * D:(k + 1) * D, :], terms[k - 1],
                              terms[k - 2] if k > 1 else None, terms[k] if k < 3 else None, table, cheb_b)

        norm_stage(nc, K, "n3", X, xl_out=xl, proj=(gate_w, logits))
        route_stage(nc, K, "r1", logits, R, 1, gate_b)
        dispatch_stage(nc, K, "d1", R, 1, xl, in1, NE * T1E)
        experts1_stage(nc, K, "e1", f_w1, f_b1, f_w2, f_b2, in1, out1)
        combine_stage(nc, K, "c1", X, R, 1, out1, out=out)


def kernel(**inputs):
    import concourse.bacc as bacc
    from concourse.bass_utils import run_bass_kernel_spmd

    a = {k: np.asarray(v) for k, v in inputs.items()}
    loop = np.arange(N, dtype=np.int32)
    pad = lambda n: np.full(n, PAD_KEY, np.int32)
    edges = lambda v: np.concatenate([v, pad(ET_IN * P - E_IN), loop, pad(EP - ET_IN * P - N)])
    src, dst = edges(a["src"]), edges(a["dst"])
    tiles = lambda v: np.ascontiguousarray(v.reshape(ET, P).T)
    arrays = {
        "x": a["x"], "dst_p": tiles(dst), "src_p": tiles(src),
        "dst_r": dst.reshape(P, ET), "src_r": src.reshape(P, ET),
        "eps": a["L0_gnn_eps"], "m_w1": a["L0_gnn_W1"], "m_b1": a["L0_gnn_b1"], "m_w2": a["L0_gnn_W2"],
        "m_b2": a["L0_gnn_b2"], "gamma": a["L0_gnn_gamma"], "beta": a["L0_gnn_beta"],
        "router": a["L0_ffn_router_w"].T,
        "w13": np.concatenate([a["L0_ffn_w1"], a["L0_ffn_w3"]], 1).transpose(2, 0, 1).reshape(D, NE * 2 * H0),
        "w2e": a["L0_ffn_w2"].transpose(2, 0, 1).reshape(H0, NE * D),
        "cheb_w": a["L1_gnn_weight"].reshape(4 * D, D), "cheb_b": a["L1_gnn_bias"],
        "gate_w": a["L1_ffn_gate_w"], "gate_b": a["L1_ffn_gate_b"],
        "f_w1": a["L1_ffn_w1"].reshape(NE * D, F1),
        "f_b1": a["L1_ffn_b1"].reshape(NE, F1 // P, P).transpose(0, 2, 1).reshape(NE * P, F1 // P),
        "f_w2": a["L1_ffn_w2"].reshape(NE * F1, D), "f_b2": a["L1_ffn_b2"].reshape(NE * D),
    }
    arrays = {k: np.ascontiguousarray(v) for k, v in arrays.items()}
    nc = bacc.Bacc("TRN2", target_bir_lowering=False, num_devices=1)
    args = [nc.dram_tensor(f"in_{k}", v.shape, mybir.dt.from_np(v.dtype), kind="ExternalInput").ap()
            for k, v in arrays.items()]
    args.append(nc.dram_tensor("out_x", (N, D), F32, kind="ExternalOutput").ap())
    bass_gnn_ffn_kernel(nc, *args)
    r = run_bass_kernel_spmd(nc, [{f"in_{k}": v for k, v in arrays.items()}], core_ids=[0])
    return r.results[0]["out_x"]
```
